# Optimizing a Trainium2 kernel written in Bass

```python
import numpy as np
import jax
import jax.numpy as jnp

def _softmax(x, axis=-1):
    return jax.nn.softmax(x, axis=axis)

def _gelu(x):
    return jax.nn.gelu(x, approximate=True)

def _silu(x):
    return jax.nn.silu(x)

def _sigmoid(x):
    return jax.nn.sigmoid(x)

def _layernorm(x, axis=-1, eps=1e-05):
    m = jnp.mean(x, axis=axis, keepdims=True)
    v = jnp.var(x, axis=axis, keepdims=True)
    return (x - m) / jnp.sqrt(v + eps)

def _scatter_add(tgt, idx, src, axis=0):
    return tgt.at[idx].add(src)

def _segment_sum(src, seg, n):
    return jax.ops.segment_sum(src, seg, n)
kernel_name = 'mk_seq_preln_d2_jaxref_r8_324883'

def setup_inputs(seed: int=0):
    np.random.seed(seed)
    _w = jnp.asarray

    def _L0_attn_setup():
        import jax, jax.numpy as jnp
        import numpy as np
        import math
        N_HEAD = 16
        LAYER = 1
        LAMBDA_INIT = 0.8 - 0.6 * math.exp(-0.3 * (LAYER - 1))
        key = jax.random.key(seed)
        ks = jax.random.split(key, 7)
        B, T, E = (2, 256, 256)
        s = 0.02
        return {'x': jax.random.normal(ks[0], (B, T, E), dtype=jnp.float32), 'W_attn': jax.random.normal(ks[1], (E, 3 * E), dtype=jnp.float32) * s, 'W_proj': jax.random.normal(ks[2], (E, E), dtype=jnp.float32) * s, 'lambda_q1': jax.random.normal(ks[3], (E,), dtype=jnp.float32) * 0.1, 'lambda_k1': jax.random.normal(ks[4], (E,), dtype=jnp.float32) * 0.1, 'lambda_q2': jax.random.normal(ks[5], (E,), dtype=jnp.float32) * 0.1, 'lambda_k2': jax.random.normal(ks[6], (E,), dtype=jnp.float32) * 0.1}
    _L0_attn_in = _L0_attn_setup()

    def _L0_ffn_setup():
        import jax, jax.numpy as jnp
        import numpy as np
        TARGET_SPARSITY = 0.9
        LN_EPS = 1e-05

        def ternary_quant(W):
            scale = jnp.mean(jnp.abs(W))
            q = jnp.clip(jnp.round(W / (scale + 1e-08)), -1.0, 1.0) * scale
            return W + jax.lax.stop_gradient(q - W)

        def layernorm(x, gamma, beta):
            mu = jnp.mean(x, axis=-1, keepdims=True)
            var = jnp.var(x, axis=-1, keepdims=True)
            return (x - mu) * jax.lax.rsqrt(var + LN_EPS) * gamma + beta
        key = jax.random.key(seed)
        ks = jax.random.split(key, 3)
        B, S, D, N = (4, 256, 256, 1024)
        x = jax.random.normal(ks[0], (B, S, D), dtype=jnp.float32)
        W_syn = jax.random.normal(ks[1], (N, D), dtype=jnp.float32) * (1.0 / np.sqrt(D))
        b_syn = jnp.zeros((N,), dtype=jnp.float32)
        W_out = jax.random.normal(ks[2], (D, N), dtype=jnp.float32) * (1.0 / np.sqrt(N))
        b_out = jnp.zeros((D,), dtype=jnp.float32)
        gamma = jnp.ones((D,), dtype=jnp.float32)
        beta = jnp.zeros((D,), dtype=jnp.float32)
        return {'x': x, 'W_syn': W_syn, 'b_syn': b_syn, 'W_out': W_out, 'b_out': b_out, 'gamma': gamma, 'beta': beta}
    _L0_ffn_in = _L0_ffn_setup()

    def _L1_attn_setup():
        import jax, jax.numpy as jnp
        import numpy as np
        B, S, QD = (2, 512, 256)
        H, D = (32, 64)
        INNER = H * D
        key = jax.random.key(seed)
        ks = jax.random.split(key, 6)
        scale = 1.0 / np.sqrt(QD)
        return {'hidden_states': jax.random.normal(ks[0], (B, S, QD), dtype=jnp.float32), 'Wq': jax.random.normal(ks[1], (QD, INNER), dtype=jnp.float32) * scale, 'Wk': jax.random.normal(ks[2], (QD, INNER), dtype=jnp.float32) * scale, 'Wv': jax.random.normal(ks[3], (QD, INNER), dtype=jnp.float32) * scale, 'Wo': jax.random.normal(ks[4], (INNER, QD), dtype=jnp.float32) * (1.0 / np.sqrt(INNER)), 'bo': jax.random.normal(ks[5], (QD,), dtype=jnp.float32) * 0.01}
    _L1_attn_in = _L1_attn_setup()

    def _L1_ffn_setup():
        import jax, jax.numpy as jnp
        import numpy as np
        TOP_K = 2
        key = jax.random.key(seed)
        ks = jax.random.split(key, 5)
        B, S, D, INTER, E = (4, 256, 256, 256, 8)
        x = jax.random.normal(ks[0], (B, S, D), dtype=jnp.float32)
        w1 = jax.random.normal(ks[1], (INTER, D), dtype=jnp.float32) * (1.0 / np.sqrt(D))
        w3 = jax.random.normal(ks[2], (INTER, INTER), dtype=jnp.float32) * (1.0 / np.sqrt(INTER))
        w2 = jax.random.normal(ks[3], (D, INTER), dtype=jnp.float32) * (1.0 / np.sqrt(INTER))
        wr = jax.random.normal(ks[4], (E, D), dtype=jnp.float32) * (1.0 / np.sqrt(D))
        return {'x': x, 'w1': w1, 'w3': w3, 'w2': w2, 'wr': wr}
    _L1_ffn_in = _L1_ffn_setup()
    _d = {'L0_attn_x': _L0_attn_in['x'], 'L0_attn_W_attn': _L0_attn_in['W_attn'], 'L0_attn_W_proj': _L0_attn_in['W_proj'], 'L0_attn_lambda_q1': _L0_attn_in['lambda_q1'], 'L0_attn_lambda_k1': _L0_attn_in['lambda_k1'], 'L0_attn_lambda_q2': _L0_attn_in['lambda_q2'], 'L0_attn_lambda_k2': _L0_attn_in['lambda_k2'], 'L0_ffn_W_syn': _L0_ffn_in['W_syn'], 'L0_ffn_b_syn': _L0_ffn_in['b_syn'], 'L0_ffn_W_out': _L0_ffn_in['W_out'], 'L0_ffn_b_out': _L0_ffn_in['b_out'], 'L0_ffn_gamma': _L0_ffn_in['gamma'], 'L0_ffn_beta': _L0_ffn_in['beta'], 'L1_attn_Wq': _L1_attn_in['Wq'], 'L1_attn_Wk': _L1_attn_in['Wk'], 'L1_attn_Wv': _L1_attn_in['Wv'], 'L1_attn_Wo': _L1_attn_in['Wo'], 'L1_attn_bo': _L1_attn_in['bo'], 'L1_ffn_w1': _L1_ffn_in['w1'], 'L1_ffn_w3': _L1_ffn_in['w3'], 'L1_ffn_w2': _L1_ffn_in['w2'], 'L1_ffn_wr': _L1_ffn_in['wr']}
    _x0 = _d['L0_attn_x']
    _d['L0_attn_x'] = jax.random.normal(jax.random.fold_in(jax.random.key(seed), 1), (2, 1024, 256), dtype=_x0.dtype)
    del _x0
    return _d

def reference(L0_attn_x, L0_attn_W_attn, L0_attn_W_proj, L0_attn_lambda_q1, L0_attn_lambda_k1, L0_attn_lambda_q2, L0_attn_lambda_k2, L0_ffn_W_syn, L0_ffn_b_syn, L0_ffn_W_out, L0_ffn_b_out, L0_ffn_gamma, L0_ffn_beta, L1_attn_Wq, L1_attn_Wk, L1_attn_Wv, L1_attn_Wo, L1_attn_bo, L1_ffn_w1, L1_ffn_w3, L1_ffn_w2, L1_ffn_wr):

    def _L0_attn_ref(x, W_attn, W_proj, lambda_q1, lambda_k1, lambda_q2, lambda_k2):
        import jax, jax.numpy as jnp
        import numpy as np
        import math
        N_HEAD = 16
        LAYER = 1
        LAMBDA_INIT = 0.8 - 0.6 * math.exp(-0.3 * (LAYER - 1))
        B, T, E = x.shape
        C = E // 2
        H = N_HEAD
        hd = E // H // 2
        scale = hd ** (-0.5)
        qkv = x @ W_attn
        q1 = qkv[..., 0 * C:1 * C].reshape(B, T, H, hd)
        k1 = qkv[..., 1 * C:2 * C].reshape(B, T, H, hd)
        q2 = qkv[..., 2 * C:3 * C].reshape(B, T, H, hd)
        k2 = qkv[..., 3 * C:4 * C].reshape(B, T, H, hd)
        v = qkv[..., 4 * C:6 * C].reshape(B, T, H, 2 * hd)
        lam = jnp.exp(jnp.dot(lambda_q1, lambda_k1)) - jnp.exp(jnp.dot(lambda_q2, lambda_k2)) + LAMBDA_INIT
        attn1 = jnp.einsum('bthd,bshd->bhts', q1, k1) * scale
        attn2 = jnp.einsum('bthd,bshd->bhts', q2, k2) * scale
        score = jax.nn.softmax(attn1 - lam * attn2, axis=-1)
        out = jnp.einsum('bhts,bshd->bthd', score, v)
        out = (1.0 - LAMBDA_INIT) * out.reshape(B, T, E)
        return out @ W_proj

    def _L0_ffn_ref(x, W_syn, b_syn, W_out, b_out, gamma, beta):
        import jax, jax.numpy as jnp
        import numpy as np
        TARGET_SPARSITY = 0.9
        LN_EPS = 1e-05

        def ternary_quant(W):
            scale = jnp.mean(jnp.abs(W))
            q = jnp.clip(jnp.round(W / (scale + 1e-08)), -1.0, 1.0) * scale
            return W + jax.lax.stop_gradient(q - W)

        def layernorm(x, gamma, beta):
            mu = jnp.mean(x, axis=-1, keepdims=True)
            var = jnp.var(x, axis=-1, keepdims=True)
            return (x - mu) * jax.lax.rsqrt(var + LN_EPS) * gamma + beta
        B, S, D = x.shape
        N = W_syn.shape[0]
        x_flat = x.reshape(-1, D)
        z = x_flat @ ternary_quant(W_syn).T + b_syn
        k = max(1, int(N * (1.0 - TARGET_SPARSITY)))
        topv, _ = jax.lax.top_k(z, k)
        thresh = topv[:, -1:]
        hidden = jnp.where(z >= thresh, jax.nn.relu(z), 0.0)
        out = hidden @ ternary_quant(W_out).T + b_out
        out = out.reshape(B, S, D)
        return layernorm(x + out, gamma, beta)

    def _L1_attn_ref(hidden_states, Wq, Wk, Wv, Wo, bo):
        import jax, jax.numpy as jnp
        import numpy as np
        B, S, QD = (2, 512, 256)
        H, D = (32, 64)
        INNER = H * D
        b, s, _ = hidden_states.shape

        def proj(W):
            return (hidden_states @ W).reshape(b, s, H, D).transpose(0, 2, 1, 3)
        q = jax.nn.relu(proj(Wq))
        k = jax.nn.relu(proj(Wk))
        v = proj(Wv)
        kv = jnp.einsum('bhsd,bhse->bhde', k, v)
        qkv = jnp.einsum('bhsd,bhde->bhse', q, kv)
        key_sum = k.sum(axis=2)
        normalizer = jnp.einsum('bhsd,bhd->bhs', q, key_sum)
        normalizer = jnp.clip(normalizer, 1e-06, None)[..., None]
        out = qkv / normalizer
        out = out.transpose(0, 2, 1, 3).reshape(b, s, INNER)
        return out @ Wo + bo

    def _L1_ffn_ref(x, w1, w3, w2, wr):
        import jax, jax.numpy as jnp
        import numpy as np
        TOP_K = 2
        B, S, D = x.shape
        xr = x.reshape(-1, D)
        route_probs = jax.nn.softmax(xr @ wr.T, axis=-1)
        routes_k, indices_k = jax.lax.top_k(route_probs, TOP_K)
        gates = routes_k / jnp.sum(routes_k, axis=-1, keepdims=True)
        h = jax.nn.silu(xr @ w1.T)
        h = jax.nn.silu(h @ w3.T)
        h = h @ w2.T
        out = jnp.zeros_like(xr)
        for k in range(TOP_K):
            out = out.at[indices_k[:, k]].add(gates[:, k:k + 1] * h)
        return out.reshape(B, S, D)
    x = L0_attn_x
    x = x + _L0_attn_ref(_layernorm(x, axis=-1), L0_attn_W_attn, L0_attn_W_proj, L0_attn_lambda_q1, L0_attn_lambda_k1, L0_attn_lambda_q2, L0_attn_lambda_k2)
    x = x + _L0_ffn_ref(_layernorm(x, axis=-1), L0_ffn_W_syn, L0_ffn_b_syn, L0_ffn_W_out, L0_ffn_b_out, L0_ffn_gamma, L0_ffn_beta)
    x = x + _L1_attn_ref(_layernorm(x, axis=-1), L1_attn_Wq, L1_attn_Wk, L1_attn_Wv, L1_attn_Wo, L1_attn_bo)
    x = x + _L1_ffn_ref(_layernorm(x, axis=-1), L1_ffn_w1, L1_ffn_w3, L1_ffn_w2, L1_ffn_wr)
    return x

_drawn_inputs = setup_inputs


def setup_inputs(seed=0):
    import zlib

    import numpy as np

    out = dict(_drawn_inputs(seed))
    spreads = {'L0_ffn_b_syn': (0.0, 0.567),
     'L0_ffn_b_out': (0.0, 0.374),
     'L0_ffn_gamma': (1.0, 0.2),
     'L0_ffn_beta': (0.0, 0.426)}
    factors = {'L0_attn_W_attn': 8.0,
     'L0_attn_W_proj': 8.0,
     'L0_attn_lambda_q1': 8.0,
     'L0_attn_lambda_k1': 8.0,
     'L0_attn_lambda_q2': 64.0,
     'L0_attn_lambda_k2': 64.0,
     'L1_attn_Wq': 49.096,
     'L1_attn_Wk': 31.888,
     'L1_attn_bo': 27.511,
     'L1_attn_Wv': 2.713}
    for name, (base, spread) in spreads.items():
        noise = np.random.default_rng([zlib.crc32(name.encode()), seed]).standard_normal(out[name].shape)
        drawn = base * np.exp(spread * noise) if base else spread * noise
        out[name] = jnp.asarray(drawn.astype(out[name].dtype))
    for name, factor in factors.items():
        out[name] = (out[name] * factor).astype(out[name].dtype)
    return out
```

```python
import math
from contextlib import ExitStack

import concourse.bass as bass
from concourse import mybir

F32 = mybir.dt.float32
F32R = mybir.dt.float32r
U32 = mybir.dt.uint32
ALU = mybir.AluOpType
ACT = mybir.ActivationFunctionType
AX = mybir.AxisListType

P = 128
EPS = 1e-5
LAMBDA_INIT = 0.8 - 0.6 * math.exp(-0.3 * 0)


def as_f32(ap):
    return ap.bitcast(F32)


class Dims:

    def __init__(self, x, w_syn, wq):
        self.B, self.S, self.E = x.shape
        self.TOK = self.B * self.S
        self.NT = self.TOK // P
        self.CH = 512
        self.TPC = self.CH // P
        self.NC = self.TOK // self.CH
        self.KT = self.E // P
        self.H = 16
        self.HD = self.E // self.H
        self.G = 4
        self.NG = self.H // self.G * self.B
        self.N = w_syn.shape[0]
        self.INNER = wq.shape[1]
        self.NCH = self.INNER // P


class Store:

    def __init__(self, nc, ctx, stage):
        self.nc, self.ctx, self.stage = nc, ctx, stage
        self.sems = []

    def sb(self, name, shape, dt=F32):
        return self.ctx.enter_context(self.nc.sbuf_tensor(f"{self.stage}_{name}", shape, dt))

    def ps(self, name, shape):
        return self.ctx.enter_context(self.nc.psum_tensor(f"{self.stage}_{name}", shape, F32))

    def sem(self, name):
        s = self.ctx.enter_context(self.nc.semaphore(f"{self.stage}_{name}"))
        self.sems.append(s.num)
        return s

    def clear(self):
        nc, first, last = self.nc, min(self.sems), max(self.sems)
        assert last - first + 1 == len(self.sems)
        with nc.Block() as block:
            @block.sync
            def _(sp):
                sp.sem_clear(range(first, last + 1))


def chain(eng, sem):
    done = [0]

    def link(ins):
        done[0] += 1
        ins.then_inc(sem, 1)
        eng.wait_ge(sem, done[0])
    return link


class NormWork:

    def __init__(self, st, tiles, tag=""):
        self.stats = st.sb("stats" + tag, [P, tiles, 6])
        self.mv = st.sb("mv" + tag, [P, tiles, 2])
        self.ve = st.sb("ve" + tag, [P, tiles])
        self.sd = st.sb("sd" + tag, [P, tiles])
        self.r0 = st.sb("r0" + tag, [P, tiles])
        self.t0 = st.sb("t0" + tag, [P, tiles])
        self.rstd = st.sb("rstd" + tag, [P, tiles])
        self.var_ready = st.sem("var_ready" + tag)
        self.sd_ready = st.sem("sd_ready" + tag)


def norm_stats(nc, dve, link, w, tiles, nth):
    for j, x in enumerate(tiles):
        ins = nc.vector.bn_stats(w.stats[:, j, :], x)
    link(ins)
    for j in range(len(tiles)):
        ins = nc.vector.bn_aggr(w.mv[:, j, :], w.stats[:, j, :])
    link(ins)
    nc.vector.tensor_scalar(w.ve[:], w.mv[:, :, 1], EPS, None, ALU.add).then_inc(w.var_ready, 1)
    dve.wait_ge(w.sd_ready, nth)
    link(nc.vector.reciprocal(w.r0[:], w.sd[:]))
    link(nc.vector.tensor_tensor(w.t0[:], w.r0[:], w.r0[:], ALU.mult))
    link(nc.vector.tensor_tensor(w.t0[:], w.t0[:], w.ve[:], ALU.mult))
    link(nc.vector.tensor_scalar(w.t0[:], w.t0[:], -0.5, 1.5, ALU.mult, ALU.add))
    link(nc.vector.tensor_tensor(w.rstd[:], w.t0[:], w.r0[:], ALU.mult))


def norm_root(nc, act, w, nth):
    act.wait_ge(w.var_ready, nth)
    nc.scalar.activation(w.sd[:], w.ve[:], ACT.Sqrt).then_inc(w.sd_ready, 1)


def norm_apply(nc, w, j, out, x):
    return nc.vector.tensor_scalar(out, x, w.mv[:, j, 0:1], w.rstd[:, j:j + 1], ALU.subtract, ALU.mult)


def mm_split(nc, out, lhs_hi, lhs_lo, rhs_hi, rhs_lo, first, last):
    terms = [(lhs_hi, rhs_hi)]
    if rhs_lo is not None:
        terms.append((lhs_hi, rhs_lo))
    if lhs_lo is not None:
        terms.append((lhs_lo, rhs_hi))
    for n, (a, b) in enumerate(terms):
        ins = nc.tensor.matmul(out, a, b, start=first and n == 0, stop=last and n == len(terms) - 1)
    return ins


def stage_qkv(nc, d, io, keep, scratch):
    with ExitStack() as ctx:
        st = Store(nc, ctx, "qkv")
        X, ident = keep["X"], keep["ident"]
        q_dram, v_dram, zero_dram = scratch["qk"], scratch["v"], scratch["zero"]
        w_raw = st.sb("w_raw", [P, d.KT, 3 * d.E])
        w_hi = st.sb("w_hi", [P, d.KT, 3 * d.E], F32R)
        w_lo = st.sb("w_lo", [P, d.KT, 3 * d.E], F32R)
        xn = st.sb("xn", [P, d.TPC, d.E])
        xt_hi = st.sb("xt_hi", [P, 2, d.KT, d.CH], F32R)
        xt_lo = st.sb("xt_lo", [P, 2, d.KT, d.CH], F32R)
        NQ = 2 * d.E // P
        qk_hi = st.sb("qk_hi", [P, NQ, d.CH], F32R)
        qk_lo = st.sb("qk_lo", [P, NQ, d.CH], F32R)
        v_st = st.sb("v_st", [P, d.TPC, d.H, 32])
        lam_in = st.sb("lam_in", [1, 4, d.E])
        lam_pr = st.sb("lam_pr", [1, 2, d.E])
        lam = st.sb("lam", [1, 8])
        row = st.sb("row", [1, P])
        one = st.sb("one", [1, 2])
        qs = st.sb("qs", [P, 2])
        zero = st.sb("zero", [2, d.G * d.S])
        w = NormWork(st, d.TPC)
        ps_t = st.ps("ps_t", [P, d.KT, d.CH])
        ps_q = st.ps("ps_q", [P, NQ, d.CH])
        ps_v = st.ps("ps_v", [P, 2, 2, d.E])

        x_in = [st.sem(f"x_in{c}") for c in range(d.NC)]
        w_in, lam_s = st.sem("w_in"), st.sem("lam_in")
        dv, gp, w_hi_ok, w_lo_ok = st.sem("dv"), st.sem("gp"), st.sem("w_hi_ok"), st.sem("w_lo_ok")
        dots, exps, row_ok, col_ok, qs_ok = (st.sem(n) for n in ("dots", "exps", "row_ok", "col_ok", "qs_ok"))
        xn_ok, xt_ps, hi_ok, lo_ok = (st.sem(n) for n in ("xn_ok", "xt_ps", "hi_ok", "lo_ok"))
        qk_ps, qk_hi_ok, qk_lo_ok = (st.sem(n) for n in ("qk_ps", "qk_hi_ok", "qk_lo_ok"))
        v_ps, v_ok, v_init, qk_out, v_out, z_ok, z_out = (
            st.sem(n) for n in ("v_ps", "v_ok", "v_init", "qk_out", "v_out", "z_ok", "z_out"))
        id_ok = st.sem("id_ok")
        HD2 = d.HD // 2
        scale = float(HD2) ** -0.5

        x_tiles = io["L0_attn_x"].rearrange("b (t p) e -> p (b t) e", p=P)
        with nc.Block() as block:
            @block.sync
            def _(sp):
                for c in range(d.NC):
                    sl = slice(c * d.TPC, (c + 1) * d.TPC)
                    sp.dma_start(X[:, sl, :], x_tiles[:, sl, :]).then_inc(x_in[c], 16)
                    if c == 0:
                        sp.dma_start(w_raw[:], io["L0_attn_W_attn"].rearrange("(k p) n -> p k n", p=P))\
                            .then_inc(w_in, 16)
                        for n, name in enumerate(("q1", "k1", "q2", "k2")):
                            sp.dma_start(lam_in[0:1, n, :],
                                         io["L0_attn_lambda_" + name].rearrange("(a e) -> a e", a=1))\
                                .then_inc(lam_s, 16)
                sp.wait_ge(z_ok, 1)
                sp.dma_start(zero_dram, zero[:]).then_inc(z_out, 16)
                for c in range(d.NC):
                    b, t0 = c * d.CH // d.S, c * d.CH % d.S
                    for j in range(NQ):
                        sp.wait_ge(qk_lo_ok, NQ * c + j + 1)
                        sp.wait_ge(qk_hi_ok, NQ * c + j + 1)
                        for part, src in ((0, qk_hi), (1, qk_lo)):
                            sp.dma_start(q_dram[part, b, P * j:P * (j + 1), t0:t0 + d.CH],
                                         as_f32(src[:, j, :])).then_inc(qk_out, 16)
                    sp.wait_ge(v_ok, 2 * (c + 1))
                    for g in range(d.H // d.G):
                        sp.dma_start(v_dram[b, g, :, t0 // P:t0 // P + d.TPC, :],
                                     v_st[:, :, d.G * g:d.G * (g + 1), :].rearrange("p t h c -> p t (h c)"))\
                            .then_inc(v_out, 16)
                sp.wait_ge(z_out, 16)
                sp.wait_ge(qk_out, 32 * NQ * d.NC)
                sp.wait_ge(v_out, 16 * (d.H // d.G) * d.NC)

            @block.gpsimd
            def _(pool):
                link = chain(pool, gp)
                link(nc.gpsimd.memset(ident[:], 0.0))
                nc.gpsimd.affine_select(out=ident[:], in_=ident[:], compare_op=ALU.not_equal, fill=1.0, base=0,
                                        pattern=[[-1, P]], channel_multiplier=1).then_inc(id_ok, 1)
                nc.gpsimd.memset(zero[:], 0.0).then_inc(z_ok, 1)
                link(nc.gpsimd.memset(v_st[:, :, :, :], 0.0))
                nc.gpsimd.memset(v_st[:, :, :, d.HD:d.HD + 1], 1.0).then_inc(v_init, 1)
                pool.wait_ge(w_in, 16)
                for k in range(d.KT):
                    for part in range(2):
                        src = w_raw[:, k, 0:2 * d.E].rearrange("p (a z h e) -> p z h a e", a=2, z=2, e=HD2)[:, part]
                        dst = w_hi[:, k, part * d.E:(part + 1) * d.E].rearrange("p (h a e) -> p h a e", a=2, e=HD2)
                        link(nc.gpsimd.tensor_copy(dst, src))
                        dlo = w_lo[:, k, part * d.E:(part + 1) * d.E].rearrange("p (h a e) -> p h a e", a=2, e=HD2)
                        for a in range(2):
                            ins = nc.gpsimd.tensor_tensor(dlo[:, :, a], src[:, :, a], as_f32(dst)[:, :, a], ALU.subtract)
                    link(nc.gpsimd.tensor_copy(w_hi[:, k, 2 * d.E:], w_raw[:, k, 2 * d.E:]))
                    ins = nc.gpsimd.tensor_tensor(w_lo[:, k, 2 * d.E:], w_raw[:, k, 2 * d.E:],
                                                  as_f32(w_hi[:, k, 2 * d.E:]), ALU.subtract)
                    link(ins)
                nc.gpsimd.memset(lam[0:1, 7:8], 0.0).then_inc(w_lo_ok, 1)

            @block.vector
            def _(dve):
                link = chain(dve, dv)
                nc.vector.memset(one[:], 1.0)
                link(nc.vector.memset(row[:], 1.0))
                tiles = lambda c: [X[:, d.TPC * c + j, :] for j in range(d.TPC)]
                for c in range(d.NC):
                    dve.wait_ge(x_in[c], 16)
                    norm_stats(nc, dve, link, w, tiles(c), c + 1)
                    if c >= 1:
                        dve.wait_ge(xt_ps, d.KT * c)
                    for j in range(d.TPC):
                        ins = norm_apply(nc, w, j, xn[:, j, :], X[:, d.TPC * c + j, :])
                    ins.then_inc(xn_ok, 1)
                    if c == 0:
                        dve.wait_ge(lam_s, 64)
                        link(nc.vector.tensor_tensor(lam_pr[:], lam_in[:, 0::2, :], lam_in[:, 1::2, :], ALU.mult))
                        nc.vector.reduce_sum(lam[0:1, 0:2], lam_pr[:], AX.X).then_inc(dots, 1)
                        dve.wait_ge(exps, 1)
                        link(nc.vector.tensor_tensor(lam[0:1, 4:5], lam[0:1, 2:3], lam[0:1, 3:4], ALU.subtract))
                        link(nc.vector.tensor_scalar(lam[0:1, 5:6], lam[0:1, 4:5], LAMBDA_INIT, -scale,
                                                     ALU.add, ALU.mult))
                        r = row[0:1, :].rearrange("p (h a e) -> p a h e", a=2, e=HD2)
                        nc.vector.tensor_scalar(r[:, 1], r[:, 1], lam[0:1, 5:6], None, ALU.mult)
                        nc.vector.tensor_scalar(r[:, 0], r[:, 0], scale, None, ALU.mult).then_inc(row_ok, 1)
                        dve.wait_ge(col_ok, 1)
                        nc.vector.tensor_copy(qs[:, 0:1], ps_q[:, 0, 0:1]).then_inc(qs_ok, 1)
                    for k in range(d.KT):
                        dve.wait_ge(hi_ok, d.KT * c + k + 1)
                        nc.vector.tensor_tensor(xt_lo[:, c % 2, k, :], ps_t[:, k, :],
                                                as_f32(xt_hi[:, c % 2, k, :]), ALU.subtract).then_inc(lo_ok, 1)
                    for j in range(NQ):
                        dve.wait_ge(qk_hi_ok, NQ * c + j + 1)
                        if c >= 1:
                            dve.wait_ge(qk_out, 32 * (NQ * (c - 1) + NQ))
                        if j < NQ // 2:
                            nc.vector.scalar_tensor_tensor(
                                out=qk_lo[:, j, :], in0=ps_q[:, j, :], scalar=qs[:, 0:1],
                                in1=as_f32(qk_hi[:, j, :]), op0=ALU.mult, op1=ALU.subtract).then_inc(qk_lo_ok, 1)
                        else:
                            nc.vector.tensor_tensor(qk_lo[:, j, :], ps_q[:, j, :], as_f32(qk_hi[:, j, :]),
                                                    ALU.subtract).then_inc(qk_lo_ok, 1)

            @block.scalar
            def _(act):
                for c in range(d.NC):
                    norm_root(nc, act, w, c + 1)
                    for k in range(d.KT):
                        act.wait_ge(xt_ps, d.KT * c + k + 1)
                        if c >= 2:
                            act.wait_ge(v_ps, 2 * (c - 1))
                        nc.scalar.activation(xt_hi[:, c % 2, k, :], ps_t[:, k, :], ACT.Copy).then_inc(hi_ok, 1)
                    if c == 0:
                        act.wait_ge(dots, 1)
                        nc.scalar.activation(lam[0:1, 2:4], lam[0:1, 0:2], ACT.Exp).then_inc(exps, 1)
                        act.wait_ge(qs_ok, 1)
                    for j in range(NQ):
                        act.wait_ge(qk_ps, NQ * c + j + 1)
                        if c >= 1:
                            act.wait_ge(qk_out, 32 * (NQ * (c - 1) + NQ))
                        nc.scalar.activation(qk_hi[:, j, :], ps_q[:, j, :], ACT.Copy,
                                             scale=qs[:, 0:1] if j < NQ // 2 else 1.0).then_inc(qk_hi_ok, 1)
                    for j in range(2):
                        act.wait_ge(v_ps, 2 * c + j + 1)
                        if c == 0:
                            act.wait_ge(v_init, 1)
                        if c >= 1:
                            act.wait_ge(v_out, 16 * (d.H // d.G) * c)
                        nc.scalar.activation(v_st[:, 2 * j:2 * j + 2, :, 0:d.HD],
                                             ps_v[:, j, :, :].rearrange("p t (h e) -> p t h e", e=d.HD),
                                             ACT.Copy).then_inc(v_ok, 1)

            @block.tensor
            def _(pe):
                pe.wait_ge(id_ok, 1)
                for c in range(d.NC):
                    pe.wait_ge(xn_ok, c + 1)
                    if c >= 1:
                        pe.wait_ge(lo_ok, d.KT * c)
                    for k in range(d.KT):
                        for j in range(d.TPC):
                            ins = nc.tensor.transpose(ps_t[:, k, j * P:(j + 1) * P], xn[:, j, k * P:(k + 1) * P],
                                                      ident[:])
                        ins.then_inc(xt_ps, 1)
                    if c == 0:
                        pe.wait_ge(row_ok, 1)
                        nc.tensor.matmul(ps_q[:, 0, 0:1], row[0:1, :], one[0:1, 0:1], start=True, stop=True)\
                            .then_inc(col_ok, 1)
                        pe.wait_ge(w_lo_ok, 1)
                        pe.wait_ge(qs_ok, 1)
                    pe.wait_ge(lo_ok, d.KT * (c + 1))
                    for j in range(NQ):
                        if c >= 1:
                            pe.wait_ge(qk_lo_ok, NQ * (c - 1) + j + 1)
                        for k in range(d.KT):
                            cols = slice(j * P, (j + 1) * P)
                            ins = mm_split(nc, ps_q[:, j, :], w_hi[:, k, cols], w_lo[:, k, cols],
                                           xt_hi[:, c % 2, k, :], xt_lo[:, c % 2, k, :], k == 0, k == d.KT - 1)
                        ins.then_inc(qk_ps, 1)
                    for j in range(2):
                        if c >= 1:
                            pe.wait_ge(v_ok, 2 * (c - 1) + j + 1)
                        for i in range(2):
                            t = slice((2 * j + i) * P, (2 * j + i + 1) * P)
                            for k in range(d.KT):
                                ins = mm_split(nc, ps_v[:, j, i, :], xt_hi[:, c % 2, k, t], xt_lo[:, c % 2, k, t],
                                               w_hi[:, k, 2 * d.E:], w_lo[:, k, 2 * d.E:], k == 0, k == d.KT - 1)
                        ins.then_inc(v_ps, 1)
        st.clear()


def stage_attention(nc, d, io, keep, scratch):
    with ExitStack() as ctx:
        st = Store(nc, ctx, "att")
        AO, ident = keep["AO"], keep["ident"]
        q_dram, v_dram, zero_dram = scratch["qk"], scratch["v"], scratch["zero"]
        NS = d.S // P
        NB = d.S // d.CH
        HD, G = d.HD, d.G
        ROWS = 3 * HD + 2
        RING = 3
        LEAD = 6
        qst = [st.sb(f"qst{i}", [P, G, d.S], F32R) for i in range(RING)]
        kst = [st.sb(f"kst{i}", [P, G, d.S], F32R) for i in range(RING)]
        vst = [st.sb(f"vst{i}", [P, NS, G * 32]) for i in range(RING)]
        prob = st.sb("prob", [P, RING, G, d.S])
        mx = st.sb("mx", [P, 2, G * NS, NB])
        nm = st.sb("nm", [P, G * NS])
        nmt = st.sb("nmt", [P, G * NS])
        nm_hi = st.sb("nm_hi", [P, 2, G * NS], F32R)
        nm_lo = st.sb("nm_lo", [P, 2, G * NS], F32R)
        osb = st.sb("osb", [P, NB, d.CH])
        rs = st.sb("rs", [P, NB, d.TPC * G])
        ps_s = st.ps("ps_s", [P, 2, d.S])
        ps_m = st.ps("ps_m", [P, 2, d.CH])
        ps_o = st.ps("ps_o", [P, NB, d.CH])
        pad_ok = st.sem("pad_ok")
        load = [st.sem(f"load{i}") for i in range(RING)]
        nm_in = [st.sem(f"nm_in{i}") for i in range(2)]
        m_ps, m_rd, nm_ok = st.sem("m_ps"), st.sem("m_rd"), st.sem("nm_ok")
        sc_ps, exp_ok, pv_ok = st.sem("sc_ps"), st.sem("exp_ok"), st.sem("pv_ok")
        o_rd, dv = st.sem("o_rd"), st.sem("dv")
        UPG = NS * G
        MPG = G * NS * NB
        MPU = MPG // UPG
        UN = UPG * d.NG
        LOADS = 8
        NMD = 8

        side = {u: [] for u in range(-1, UN + 2 * G + 3)}
        for g in range(d.NG):
            for m in range(MPG):
                side[max(-1, UPG * (g - 1) - LEAD + m // MPU)].append(("max", g, m))
            for t in range(NB):
                side[UPG * (g + 1) + G + 2 + t].append(("out", g, t))
        items = [(u, x) for u in side for x in side[u]]

        def ready(kind, g, m):
            return [x for _, x in items].index((kind, g, m)) + 1

        with nc.Block() as block:
            @block.sync
            def _(sp):
                def load_group(g):
                    b, i = g // (d.NG // d.B), g % RING
                    h0 = g % (d.NG // d.B) * G
                    if g < RING:
                        sp.wait_ge(pad_ok, i + 1)
                    else:
                        sp.wait_ge(pv_ok, NS * NB * (g - RING + 1))
                    for base, dst, parts in ((0, qst[i], (0, 1, 0)), (d.E, kst[i], (0, 0, 1))):
                        for n, part in enumerate(parts):
                            src = q_dram[part, b, base + h0 * HD:base + (h0 + G) * HD, :]
                            sp.dma_start(as_f32(dst[n * HD:(n + 1) * HD, :, :]),
                                         src.rearrange("(h e) t -> e h t", e=HD)).then_inc(load[i], 16)
                    sp.dma_start(as_f32(qst[i][3 * HD:ROWS, :, :]), zero_dram.rearrange("r (h t) -> r h t", h=G))\
                        .then_inc(load[i], 16)
                    sp.dma_start(vst[i][:], v_dram[b, g % (d.NG // d.B)]).then_inc(load[i], 16)

                for g in range(RING):
                    load_group(g)
                for g in range(d.NG):
                    sp.wait_ge(nm_ok, g + 1)
                    for r, src in ((3 * HD, nm_hi), (3 * HD + 1, nm_lo)):
                        for q in range(4):
                            dst = qst[g % RING][r:r + 1, :, :].rearrange("p h (t q j) -> p (h t) q j", q=4, j=32)
                            sp.dma_start(as_f32(dst[:, :, q]), as_f32(src[32 * q:32 * q + 32, g % 2, :]))\
                                .then_inc(nm_in[g % 2], 16)
                    if g >= 1 and g + 2 < d.NG:
                        load_group(g + 2)

            @block.gpsimd
            def _(pool):
                for i in range(RING):
                    nc.gpsimd.memset(as_f32(qst[i][64:P, :, :]), 0.0)
                    nc.gpsimd.memset(as_f32(kst[i][64:P, :, :]), 0.0)
                    nc.gpsimd.memset(as_f32(qst[i][32:64, :, :]), 0.0)
                    nc.gpsimd.memset(as_f32(kst[i][32:64, :, :]), 1.0).then_inc(pad_ok, 1)

            @block.tensor
            def _(pe):
                done = [0]

                def side_unit(kind, g, m):
                    n = done[0]
                    done[0] += 1
                    if n >= 2:
                        pe.wait_ge(m_rd, n - 1)
                    if kind == "max":
                        h, t, half = m // (NS * NB), m // NB % NS, m % NB
                        if m == 0:
                            pe.wait_ge(load[g % RING], 16 * LOADS * (g // RING + 1))
                        nc.tensor.matmul(ps_m[:, n % 2, :], qst[g % RING][:, h, t * P:(t + 1) * P],
                                         kst[g % RING][:, h, half * d.CH:(half + 1) * d.CH],
                                         start=True, stop=True).then_inc(m_ps, 1)
                    else:
                        pe.wait_ge(o_rd, NB * g + m + 1)
                        for j in range(d.TPC):
                            ins = nc.tensor.transpose(ps_m[:, n % 2, j * P:(j + 1) * P],
                                                      osb[:, m, j * P:(j + 1) * P], ident[:])
                        ins.then_inc(m_ps, 1)

                def score_unit(u):
                    g, s, h = u // UPG, u // G % NS, u % G
                    if u % UPG == 0:
                        pe.wait_ge(nm_in[g % 2], 16 * NMD * (g // 2 + 1))
                    if u >= 2:
                        pe.wait_ge(exp_ok, u - 1)
                    for t in range(NB):
                        ins = nc.tensor.matmul(ps_s[:, u % 2, t * d.CH:(t + 1) * d.CH],
                                               kst[g % RING][:, h, s * P:(s + 1) * P],
                                               qst[g % RING][:, h, t * d.CH:(t + 1) * d.CH], start=True, stop=True)
                    ins.then_inc(sc_ps, 1)

                def value_unit(n, t):
                    g, s = n // NS, n % NS
                    pe.wait_ge(exp_ok, G * (n + 1))
                    if s == 0 and g >= 1:
                        pe.wait_ge(o_rd, NB * (g - 1) + t + 1)
                    for h in range(G):
                        ins = nc.tensor.matmul(ps_o[32 * h:32 * h + 32, t, :],
                                               vst[g % RING][:, s, 32 * h:32 * h + 32],
                                               prob[:, n % RING, h, t * d.CH:(t + 1) * d.CH],
                                               start=s == 0, stop=s == NS - 1)
                    ins.then_inc(pv_ok, 1)

                for u in side:
                    todo = side[u]
                    if u >= 0:
                        for x in todo[:1]:
                            side_unit(*x)
                        if u < UN:
                            score_unit(u)
                        todo = todo[1:]
                    for x in todo:
                        side_unit(*x)
                    if u > G and u % G in (1, 3) and u // G - 1 < UN // G:
                        value_unit(u // G - 1, u % G // 2)

            @block.scalar
            def _(act):
                for u in range(UN + G + 3):
                    s, h = u // G, u % G
                    if u < UN:
                        act.wait_ge(sc_ps, u + 1)
                        if h == 0 and s >= RING:
                            act.wait_ge(pv_ok, NB * (s - RING + 1))
                        nc.scalar.activation(prob[:, s % RING, h, :], ps_s[:, u % 2, :], ACT.Exp).then_inc(exp_ok, 1)
                    if u > UPG and u % UPG in (2, 4):
                        g, t = u // UPG - 1, u % UPG // 2 - 1
                        act.wait_ge(pv_ok, NB * (NS * (g + 1) - 1) + t + 1)
                        if g >= 1:
                            act.wait_ge(m_rd, ready("out", g - 1, t))
                        nc.scalar.activation(osb[:, t, :], ps_o[:, t, :], ACT.Copy).then_inc(o_rd, 1)

            @block.vector
            def _(dve):
                link = chain(dve, dv)

                def finish_max(g):
                    link(nc.vector.tensor_reduce(nm[:], mx[:, g % 2], AX.X, ALU.max, negate=True))
                    link(nc.vector.transpose(nmt[:], nm[:]))
                    if g >= 2:
                        dve.wait_ge(nm_in[g % 2], 16 * NMD * (g // 2))
                    link(nc.vector.tensor_copy(nm_hi[:, g % 2, :], nmt[:]))
                    nc.vector.tensor_tensor(nm_lo[:, g % 2, :], nmt[:], as_f32(nm_hi[:, g % 2, :]),
                                            ALU.subtract).then_inc(nm_ok, 1)

                for n, (_, (kind, g, m)) in enumerate(items):
                    dve.wait_ge(m_ps, n + 1)
                    if kind == "max":
                        nc.vector.reduce_max(mx[:, g % 2, m // NB, m % NB:m % NB + 1], ps_m[:, n % 2, :], AX.X)\
                            .then_inc(m_rd, 1)
                        if m == MPG - 1:
                            dve.wait_ge(m_rd, n + 1)
                            finish_max(g)
                    else:
                        b, h0, t0 = g // (d.NG // d.B), g % (d.NG // d.B) * G, m * d.TPC
                        o = ps_m[:, n % 2, :].rearrange("p (j h e) -> p j h e", h=G, e=32)
                        r = rs[:, m, :].rearrange("p (j h) -> p j h", h=G)
                        link(nc.vector.reciprocal(r, o[:, :, :, HD]))
                        link(nc.vector.tensor_scalar(r, r, 1.0 - LAMBDA_INIT, None, ALU.mult))
                        dst = AO[:, b * NS + t0:b * NS + t0 + d.TPC, h0 * HD:(h0 + G) * HD]
                        nc.vector.tensor_tensor(dst.rearrange("p j (h e) -> p j h e", e=HD), o[:, :, :, 0:HD],
                                                r.unsqueeze(3).to_broadcast([P, d.TPC, G, HD]),
                                                ALU.mult).then_inc(m_rd, 1)


def stage_mlp(nc, d, io, keep):
    with ExitStack() as ctx:
        st = Store(nc, ctx, "mlp")
        X, AO, ident = keep["X"], keep["AO"], keep["ident"]
        KEEP = max(1, int(d.N * (1.0 - 0.9)))
        LOW = KEEP - 8
        NN = d.N // P
        NH = d.N // d.CH
        ROUNDS = 4
        SPREAD0, SLOPE = 1.3095, 173.0
        XN = st.sb("xn", [P, d.NT, d.E])
        Z = st.sb("z", [P, d.NT, d.N])
        wp_raw = st.sb("wp_raw", [P, d.KT, d.E])
        wp_hi = st.sb("wp_hi", [P, d.KT, d.E], F32R)
        wp_lo = st.sb("wp_lo", [P, d.KT, d.E], F32R)
        ws_raw = st.sb("ws_raw", [P, NN, d.E])
        wo_raw = st.sb("wo_raw", [P, d.KT, d.N])
        ws_t = st.sb("ws_t", [P, d.KT, d.N], F32R)
        wo_t = st.sb("wo_t", [P, NN, d.E], F32R)
        bs = st.sb("bs", [P, d.N])
        vecs = st.sb("vecs", [P, 3, d.E])
        ones = st.sb("ones", [P, P])
        abs_sum = st.sb("abs_sum", [P, 2])
        sc = st.sb("sc", [P, 2])
        inv = st.sb("inv", [P, 2])
        xt_hi = st.sb("xt_hi", [P, d.KT, d.CH], F32R)
        xt_lo = st.sb("xt_lo", [P, d.KT, d.CH], F32R)
        zst = st.sb("zst", [P, d.NT, NH, 6])
        zmv = st.sb("zmv", [P, d.NT, 2])
        zsd = st.sb("zsd", [P, d.NT])
        lev = st.sb("lev", [P, d.NT])
        nlev = st.sb("nlev", [P, d.NT])
        sgn = st.sb("sgn", [P, d.NT])
        cnt = st.sb("cnt", [P, d.NT])
        lo, hi, clo, chi = (st.sb(n, [P, d.NT]) for n in ("lo", "hi", "clo", "chi"))
        t1, t2, t3 = (st.sb(n, [P, d.NT]) for n in ("t1", "t2", "t3"))
        msk = st.sb("msk", [P, d.NT])
        msk2 = st.sb("msk2", [P, d.NT])
        junk = st.sb("junk", [P, 2, d.N], mybir.dt.bfloat16)
        below = st.sb("below", [P, 2, d.N])
        top = st.sb("top", [P, d.NT, 8])
        pick = st.sb("pick", [P, d.NT, 8])
        iota8 = st.sb("iota8", [P, 8])
        iota_i = st.sb("iota_i", [P, 8], mybir.dt.int32)
        thr = st.sb("thr", [P, d.NT])
        flag = st.sb("flag", [P, 2])
        flag_i = st.sb("flag_i", [P, 1], mybir.dt.int32)
        ht_hi = st.sb("ht_hi", [P, d.N], F32R)
        ht_lo = st.sb("ht_lo", [P, d.N], F32R)
        y = st.sb("y", [P, d.TPC, d.E])
        w1, w2 = NormWork(st, d.TPC, "1"), NormWork(st, d.TPC, "2")
        ps_t = st.ps("ps_t", [P, d.KT, d.CH])
        ps_p = st.ps("ps_p", [P, 2, 2, d.E])
        ps_z = st.ps("ps_z", [P, 2, d.N])

        w_in = [st.sem(f"w_in{i}") for i in range(4)]
        dv, gp, on = st.sem("dv"), st.sem("gp"), st.sem("on")
        wp_ok, tern_ok, tern_ps, tern_rd = (st.sem(n) for n in ("wp_ok", "tern_ok", "tern_ps", "tern_rd"))
        sum_ok, sum_ps = st.sem("sum_ok"), st.sem("sum_ps")
        at_ps, hi_ok, lo_ok = st.sem("at_ps"), st.sem("hi_ok"), st.sem("lo_ok")
        pr_ps, pr_rd, xn_ok = st.sem("pr_ps"), st.sem("pr_rd"), st.sem("xn_ok")
        z_ps, z_ok = st.sem("z_ps"), st.sem("z_ok")
        zvar, zroot, lev_ok, cnt_ok = (st.sem(n) for n in ("zvar", "zroot", "lev_ok", "cnt_ok"))
        flag_ok, any_ok = st.sem("flag_ok"), st.sem("any_ok")
        h_ok, h_ps, h_hi, h_lo, o_ps, o_rd = (st.sem(n) for n in ("h_ok", "h_ps", "h_hi", "h_lo", "o_ps", "o_rd"))
        xb_ok, y_ok, x_ok = st.sem("xb_ok"), st.sem("y_ok"), st.sem("x_ok")

        with nc.Block() as block:
            @block.sync
            def _(sp):
                sp.dma_start(wp_raw[:], io["L0_attn_W_proj"].rearrange("(k p) n -> p k n", p=P)).then_inc(w_in[0], 16)
                sp.dma_start(ws_raw[:], io["L0_ffn_W_syn"].rearrange("(a p) n -> p a n", p=P)).then_inc(w_in[1], 16)
                sp.dma_start(wo_raw[:], io["L0_ffn_W_out"].rearrange("(a p) n -> p a n", p=P)).then_inc(w_in[1], 16)
                sp.dma_start(bs[:], io["L0_ffn_b_syn"].rearrange("(a n) -> a n", a=1).to_broadcast([P, d.N]))\
                    .then_inc(w_in[2], 16)
                for i, name in enumerate(("b_out", "gamma", "beta")):
                    src = io["L0_ffn_" + name].rearrange("(a n) -> a n", a=1)
                    sp.dma_start(vecs[:, i, :], src.to_broadcast([P, d.E])).then_inc(w_in[3], 16)

            @block.gpsimd
            def _(pool):
                link = chain(pool, gp)
                nc.gpsimd.memset(ones[:], 1.0).then_inc(on, 1)
                nc.gpsimd.iota(iota_i[:], pattern=[[1, 8]], base=0, channel_multiplier=0).then_inc(on, 1)
                pool.wait_ge(w_in[0], 16)
                link(nc.gpsimd.tensor_copy(wp_hi[:], wp_raw[:]))
                nc.gpsimd.tensor_tensor(wp_lo[:], wp_raw[:], as_f32(wp_hi[:]), ALU.subtract).then_inc(wp_ok, 1)
                pool.wait_ge(flag_ok, 1)
                nc.gpsimd.partition_all_reduce(flag[:, 1:2], flag[:, 0:1], P, bass.bass_isa.ReduceOp.max)\
                    .then_inc(any_ok, 1)
                pool.wait_ge(w_in[3], 48)
                for c in range(d.NC):
                    pool.wait_ge(z_ps, d.NT)
                    for j in range(d.TPC):
                        t = d.TPC * c + j
                        ins = nc.gpsimd.tensor_tensor(XN[:, t, :], XN[:, t, :], vecs[:, 0, :], ALU.add)
                    ins.then_inc(xb_ok, 1)
                for c in range(d.NC):
                    pool.wait_ge(y_ok, c + 1)
                    for j in range(d.TPC):
                        ins = nc.gpsimd.tensor_tensor(y[:, j, :], y[:, j, :], vecs[:, 1, :], ALU.mult)
                    link(ins)
                    for j in range(d.TPC):
                        ins = nc.gpsimd.tensor_tensor(y[:, j, :], y[:, j, :], vecs[:, 2, :], ALU.add)
                    link(ins)
                    for j in range(d.TPC):
                        t = d.TPC * c + j
                        ins = nc.gpsimd.tensor_tensor(X[:, t, :], X[:, t, :], y[:, j, :], ALU.add)
                    ins.then_inc(x_ok, 1)

            @block.vector
            def _(dve):
                link = chain(dve, dv)
                dve.wait_ge(w_in[1], 32)
                nc.vector.tensor_reduce(abs_sum[:, 0:1], ws_raw[:].rearrange("p a n -> p (a n)"), AX.X, ALU.add,
                                        apply_absolute_value=True)
                nc.vector.tensor_reduce(abs_sum[:, 1:2], wo_raw[:].rearrange("p a n -> p (a n)"), AX.X, ALU.add,
                                        apply_absolute_value=True).then_inc(sum_ok, 1)
                dve.wait_ge(sum_ps, 1)
                link(nc.vector.tensor_scalar(sc[:], ps_p[:, 0, 0, 0:2], 1.0 / (d.N * d.E), None, ALU.mult))
                link(nc.vector.tensor_scalar(inv[:], sc[:], 1e-8, None, ALU.add))
                link(nc.vector.reciprocal(inv[:], inv[:]))
                for i, raw in enumerate((ws_raw, wo_raw)):
                    flat = raw[:].rearrange("p a n -> p (a n)")
                    a = Z[:, 0:2, :].rearrange("p a n -> p (a n)")
                    b = Z[:, 2:4, :].rearrange("p a n -> p (a n)")
                    nc.vector.tensor_scalar(a, flat, inv[:, i:i + 1], 0.5, ALU.mult, ALU.is_gt)
                    link(nc.vector.tensor_scalar(b, flat, inv[:, i:i + 1], -0.5, ALU.mult, ALU.is_lt))
                    link(nc.vector.tensor_tensor(flat, a, b, ALU.subtract))
                nc.vector.memset(flag[:, 0:1], 0.0).then_inc(tern_ok, 1)
                dve.wait_ge(w_in[2], 16)
                for c in range(d.NC):
                    for k in range(d.KT):
                        dve.wait_ge(hi_ok, 2 * d.KT * c + k + 1)
                        nc.vector.tensor_tensor(xt_lo[:, k, :], ps_t[:, k, :], as_f32(xt_hi[:, k, :]),
                                                ALU.subtract).then_inc(lo_ok, 1)
                    for j in range(2):
                        dve.wait_ge(pr_ps, 2 * c + j + 1)
                        t = d.TPC * c + 2 * j
                        ins = nc.vector.tensor_tensor(X[:, t:t + 2, :], X[:, t:t + 2, :], ps_p[:, j, :, :], ALU.add)
                        ins.then_inc(pr_rd, 1)
                    dve.wait_ge(pr_rd, 2 * (c + 1))
                    norm_stats(nc, dve, link, w1, [X[:, d.TPC * c + j, :] for j in range(d.TPC)], c + 1)
                    for j in range(d.TPC):
                        t = d.TPC * c + j
                        ins = norm_apply(nc, w1, j, XN[:, t, :], X[:, t, :])
                    ins.then_inc(xn_ok, 1)
                    for k in range(d.KT):
                        dve.wait_ge(hi_ok, 2 * d.KT * c + d.KT + k + 1)
                        nc.vector.tensor_tensor(xt_lo[:, k, :], ps_t[:, k, :], as_f32(xt_hi[:, k, :]),
                                                ALU.subtract).then_inc(lo_ok, 1)
                    for j in range(d.TPC):
                        t = d.TPC * c + j
                        dve.wait_ge(z_ps, t + 1)
                        nc.vector.scalar_tensor_tensor(out=Z[:, t, :], in0=ps_z[:, t % 2, :], scalar=sc[:, 0:1],
                                                       in1=bs[:], op0=ALU.mult, op1=ALU.add).then_inc(z_ok, 1)
                        dve.wait_ge(z_ok, t + 1)
                        for n in range(NH):
                            ins = nc.vector.bn_stats(zst[:, t, n, :], Z[:, t, n * d.CH:(n + 1) * d.CH])
                link(ins)
                for t in range(d.NT):
                    ins = nc.vector.bn_aggr(zmv[:, t, :], zst[:, t].rearrange("p a b -> p (a b)"))
                ins.then_inc(zvar, 1)
                dve.wait_ge(zroot, 1)
                dve.wait_ge(on, 2)
                nc.vector.tensor_copy(iota8[:], iota_i[:])
                link(nc.vector.scalar_tensor_tensor(out=lev[:], in0=zsd[:], scalar=SPREAD0, in1=zmv[:, :, 0],
                                                    op0=ALU.mult, op1=ALU.add))
                nc.vector.tensor_scalar(nlev[:], lev[:], -1.0, None, ALU.mult).then_inc(lev_ok, 1)
                link(nc.vector.scalar_tensor_tensor(out=lo[:], in0=zsd[:], scalar=-0.6, in1=lev[:],
                                                    op0=ALU.mult, op1=ALU.add))
                link(nc.vector.scalar_tensor_tensor(out=hi[:], in0=zsd[:], scalar=0.6, in1=lev[:],
                                                    op0=ALU.mult, op1=ALU.add))
                nc.vector.memset(clo[:], 122.0)
                link(nc.vector.memset(chi[:], -68.0))
                AIM = KEEP - 4.0
                for r in range(ROUNDS):
                    dve.wait_ge(cnt_ok, d.NT * (r + 1))
                    link(nc.vector.tensor_scalar(cnt[:], sgn[:], 0.5, d.N / 2 - AIM, ALU.mult, ALU.add))
                    link(nc.vector.tensor_tensor(t1[:], cnt[:], cnt[:], ALU.mult))
                    link(nc.vector.tensor_scalar(msk2[:], t1[:], 16.5, None, ALU.is_gt))
                    if r == ROUNDS - 1:
                        break
                    m = msk[:].bitcast(U32)
                    link(nc.vector.tensor_scalar(msk[:], cnt[:], 0.0, None, ALU.is_gt))
                    nc.vector.copy_predicated(lo[:], m, lev[:])
                    link(nc.vector.copy_predicated(clo[:], m, cnt[:]))
                    link(nc.vector.tensor_scalar(msk[:], cnt[:], 0.0, None, ALU.is_le))
                    nc.vector.copy_predicated(hi[:], m, lev[:])
                    link(nc.vector.copy_predicated(chi[:], m, cnt[:]))
                    if r == 0:
                        link(nc.vector.scalar_tensor_tensor(out=t1[:], in0=cnt[:], scalar=1.0 / SLOPE, in1=zsd[:],
                                                            op0=ALU.mult, op1=ALU.mult))
                        link(nc.vector.tensor_tensor(t1[:], t1[:], lev[:], ALU.add))
                    else:
                        link(nc.vector.tensor_tensor(t1[:], clo[:], chi[:], ALU.subtract))
                        link(nc.vector.reciprocal(t1[:], t1[:]))
                        link(nc.vector.tensor_tensor(t2[:], hi[:], lo[:], ALU.subtract))
                        link(nc.vector.tensor_tensor(t2[:], t2[:], clo[:], ALU.mult))
                        link(nc.vector.tensor_tensor(t2[:], t2[:], t1[:], ALU.mult))
                        link(nc.vector.tensor_tensor(t1[:], t2[:], lo[:], ALU.add))
                    link(nc.vector.copy_predicated(lev[:], msk2[:].bitcast(U32), t1[:]))
                    nc.vector.tensor_scalar(nlev[:], lev[:], -1.0, None, ALU.mult).then_inc(lev_ok, 1)
                for t in range(d.NT):
                    ins = nc.vector.scalar_tensor_tensor(out=below[:, t % 2, :], in0=Z[:, t, :],
                                                         scalar=lev[:, t:t + 1], in1=Z[:, t, :],
                                                         op0=ALU.is_le, op1=ALU.mult)
                    link(ins)
                    ins = nc.vector.max(top[:, t, :], below[:, t % 2, :])
                link(ins)
                link(nc.vector.tensor_scalar(t1[:], cnt[:], -1.0, 3.0, ALU.mult, ALU.add))
                link(nc.vector.tensor_tensor(pick[:], t1[:].unsqueeze(2).to_broadcast([P, d.NT, 8]),
                                             iota8[:].unsqueeze(1).to_broadcast([P, d.NT, 8]), ALU.is_equal))
                link(nc.vector.tensor_tensor(pick[:], pick[:], top[:], ALU.mult))
                link(nc.vector.tensor_reduce(thr[:], pick[:], AX.X, ALU.add))
                link(nc.vector.tensor_scalar(t2[:], t1[:], -1.0, None, ALU.is_equal))
                link(nc.vector.tensor_tensor(t2[:], t2[:], lev[:], ALU.mult))
                link(nc.vector.tensor_tensor(thr[:], thr[:], t2[:], ALU.add))
                link(nc.vector.tensor_scalar(t2[:], lev[:], 0.0, None, ALU.is_le))
                link(nc.vector.tensor_tensor(t3[:], top[:, :, 0], lev[:], ALU.is_equal))
                link(nc.vector.tensor_tensor(t2[:], t2[:], t3[:], ALU.max))
                link(nc.vector.tensor_tensor(t2[:], t2[:], msk2[:], ALU.max))
                nc.vector.reduce_max(flag[:, 0:1], t2[:], AX.X).then_inc(flag_ok, 1)
                dve.wait_ge(any_ok, 1)
                link(nc.vector.tensor_copy(flag_i[:], flag[:, 1:2]))
                some = dve.value_load(flag_i[0:1, 0:1], min_val=0, max_val=1)
                with dve.If(some):
                    general_threshold(nc, dve, d, Z, below, top, thr, KEEP)
                dve.drain()
                dve.wait_ge(xb_ok, d.NC)
                for t in range(d.NT):
                    if t == 0:
                        link(nc.vector.tensor_scalar(thr[:], thr[:], 0.0, None, ALU.max))
                    if t >= 2:
                        dve.wait_ge(h_ps, t - 1)
                    nc.vector.scalar_tensor_tensor(out=below[:, t % 2, :], in0=Z[:, t, :], scalar=thr[:, t:t + 1],
                                                   in1=Z[:, t, :], op0=ALU.is_ge, op1=ALU.mult).then_inc(h_ok, 1)
                    dve.wait_ge(h_hi, t + 1)
                    nc.vector.tensor_tensor(ht_lo[:], ps_z[:, t % 2, :], as_f32(ht_hi[:]),
                                            ALU.subtract).then_inc(h_lo, 1)
                    dve.wait_ge(o_ps, t + 1)
                    nc.vector.scalar_tensor_tensor(out=XN[:, t, :], in0=ps_p[:, t % 2, 0, :], scalar=sc[:, 1:2],
                                                   in1=XN[:, t, :], op0=ALU.mult, op1=ALU.add).then_inc(o_rd, 1)
                    if t % d.TPC == d.TPC - 1:
                        c = t // d.TPC
                        dve.wait_ge(o_rd, t + 1)
                        norm_stats(nc, dve, link, w2, [XN[:, d.TPC * c + j, :] for j in range(d.TPC)], c + 1)
                        if c >= 1:
                            dve.wait_ge(x_ok, c)
                        for j in range(d.TPC):
                            ins = norm_apply(nc, w2, j, y[:, j, :], XN[:, d.TPC * c + j, :])
                        ins.then_inc(y_ok, 1)

            @block.scalar
            def _(act):
                for i, dst in enumerate((ws_t, wo_t)):
                    for k in range(2):
                        act.wait_ge(tern_ps, 2 * i + k + 1)
                        flat = dst[:].rearrange("p a n -> p (a n)")[:, k * d.N:(k + 1) * d.N]
                        nc.scalar.activation(flat, ps_z[:, k, :], ACT.Copy).then_inc(tern_rd, 1)
                for c in range(d.NC):
                    for half in range(2):
                        if half:
                            norm_root(nc, act, w1, c + 1)
                        for k in range(d.KT):
                            n = 2 * d.KT * c + d.KT * half + k
                            act.wait_ge(at_ps, n + 1)
                            if half:
                                act.wait_ge(pr_ps, 2 * (c + 1))
                            elif c:
                                act.wait_ge(z_ps, d.TPC * c)
                            nc.scalar.activation(xt_hi[:, k, :], ps_t[:, k, :], ACT.Copy).then_inc(hi_ok, 1)
                act.wait_ge(zvar, 1)
                nc.scalar.activation(zsd[:], zmv[:, :, 1], ACT.Sqrt).then_inc(zroot, 1)
                for r in range(ROUNDS):
                    act.wait_ge(lev_ok, r + 1)
                    for t in range(d.NT):
                        n = d.NT * r + t
                        if n >= 2:
                            act.wait_ge(cnt_ok, n - 1)
                        nc.scalar.activation(junk[:, n % 2, :], Z[:, t, :], ACT.Sign, bias=nlev[:, t:t + 1],
                                             accum_out=sgn[:, t:t + 1]).then_inc(cnt_ok, 1)
                for t in range(d.NT):
                    act.wait_ge(h_ps, t + 1)
                    if t >= 1:
                        act.wait_ge(o_ps, t)
                    nc.scalar.activation(ht_hi[:], ps_z[:, t % 2, :], ACT.Copy).then_inc(h_hi, 1)
                    if t % d.TPC == d.TPC - 1:
                        norm_root(nc, act, w2, t // d.TPC + 1)

            @block.tensor
            def _(pe):
                pe.wait_ge(on, 1)
                pe.wait_ge(sum_ok, 1)
                nc.tensor.matmul(ps_p[:, 0, 0, 0:2], ones[:], abs_sum[:], start=True, stop=True).then_inc(sum_ps, 1)
                pe.wait_ge(tern_ok, 1)
                for k in range(d.KT):
                    for a in range(NN):
                        ins = nc.tensor.transpose(ps_z[:, k, a * P:(a + 1) * P], ws_raw[:, a, k * P:(k + 1) * P],
                                                  ident[:])
                    ins.then_inc(tern_ps, 1)
                for k in range(2):
                    pe.wait_ge(tern_rd, k + 1)
                    for a in range(NN // 2):
                        for e in range(d.KT):
                            n = k * (NN // 2) + a
                            ins = nc.tensor.transpose(ps_z[:, k, a * d.E + e * P:a * d.E + (e + 1) * P],
                                                      wo_raw[:, e, n * P:(n + 1) * P], ident[:])
                    ins.then_inc(tern_ps, 1)
                pe.wait_ge(tern_rd, 4)
                pe.wait_ge(wp_ok, 1)
                for c in range(d.NC):
                    for half, src in ((0, AO), (1, XN)):
                        if half:
                            pe.wait_ge(xn_ok, c + 1)
                        n = 2 * d.KT * c + d.KT * half
                        if n:
                            pe.wait_ge(lo_ok, n)
                        for k in range(d.KT):
                            for j in range(d.TPC):
                                ins = nc.tensor.transpose(ps_t[:, k, j * P:(j + 1) * P],
                                                          src[:, d.TPC * c + j, k * P:(k + 1) * P], ident[:])
                            ins.then_inc(at_ps, 1)
                        pe.wait_ge(lo_ok, n + d.KT)
                        if half == 0:
                            for j in range(2):
                                if c:
                                    pe.wait_ge(pr_rd, 2 * (c - 1) + j + 1)
                                for i in range(2):
                                    t = slice((2 * j + i) * P, (2 * j + i + 1) * P)
                                    for k in range(d.KT):
                                        ins = mm_split(nc, ps_p[:, j, i, :], xt_hi[:, k, t], xt_lo[:, k, t],
                                                       wp_hi[:, k, :], wp_lo[:, k, :], k == 0, k == d.KT - 1)
                                ins.then_inc(pr_ps, 1)
                        else:
                            for j in range(d.TPC):
                                t = d.TPC * c + j
                                if t >= 2:
                                    pe.wait_ge(z_ok, t - 1)
                                for n in range(NH):
                                    cols = slice(n * d.CH, (n + 1) * d.CH)
                                    for k in range(d.KT):
                                        ins = mm_split(nc, ps_z[:, t % 2, cols], xt_hi[:, k, j * P:(j + 1) * P],
                                                       xt_lo[:, k, j * P:(j + 1) * P], ws_t[:, k, cols], None,
                                                       k == 0, k == d.KT - 1)
                                ins.then_inc(z_ps, 1)
                pe.wait_ge(z_ok, d.NT)
                pe.wait_ge(pr_rd, 2 * d.NC)
                for t in range(d.NT):
                    pe.wait_ge(h_ok, t + 1)
                    if t >= 2:
                        pe.wait_ge(h_lo, t - 1)
                    for n in range(NN):
                        ins = nc.tensor.transpose(ps_z[:, t % 2, n * P:(n + 1) * P],
                                                  below[:, t % 2, n * P:(n + 1) * P], ident[:])
                    ins.then_inc(h_ps, 1)
                    pe.wait_ge(h_lo, t + 1)
                    if t >= 2:
                        pe.wait_ge(o_rd, t - 1)
                    for n in range(NN):
                        ins = mm_split(nc, ps_p[:, t % 2, 0, :], ht_hi[:, n * P:(n + 1) * P],
                                       ht_lo[:, n * P:(n + 1) * P], wo_t[:, n, :], None, n == 0, n == NN - 1)
                    ins.then_inc(o_ps, 1)


def general_threshold(nc, dve, d, Z, work, top, thr, keep):
    with dve.Fori(0, d.NT) as t:
        dve.drain()
        nc.vector.tensor_copy(work[:, 0, :], Z[:, bass.ds(t, 1), :].rearrange("p a n -> p (a n)"))
        for r in range((keep - 1) // 8):
            dve.drain()
            nc.vector.max(top[:, 0, :], work[:, r % 2, :])
            dve.drain()
            nc.vector.match_replace(out=work[:, (r + 1) % 2, :], in_to_replace=top[:, 0, :],
                                    in_values=work[:, r % 2, :], imm_value=-3.0e38)
        r = (keep - 1) // 8
        dve.drain()
        nc.vector.max(top[:, 0, :], work[:, r % 2, :])
        dve.drain()
        nc.vector.tensor_copy(thr[:, bass.ds(t, 1)], top[:, 0, (keep - 1) % 8:(keep - 1) % 8 + 1])


def stage_keys(nc, d, io, keep):
    with ExitStack() as ctx:
        st = Store(nc, ctx, "key")
        X, ident = keep["X"], keep["ident"]
        xt_hi, xt_lo, M, ksum, mask = (keep[n] for n in ("xt_hi", "xt_lo", "M", "ksum", "mask"))
        NI = d.INNER // d.CH
        CPB = d.CH // P
        TPB = d.S // P
        HW = P // 2
        xn = st.sb("xn", [P, d.TPC, d.E])
        xk_hi = st.sb("xk_hi", [P, d.NT, d.E], F32R)
        xk_lo = st.sb("xk_lo", [P, d.NT, d.E], F32R)
        raw = st.sb("raw", [P, 2, 2 * d.CH])
        w_hi = [st.sb(f"w_hi{n}", [P, 2 * d.CH], F32R) for n in range(3)]
        w_lo = [st.sb(f"w_lo{n}", [P, 2 * d.CH], F32R) for n in range(3)]
        k_hi = st.sb("k_hi", [P, 2, d.CH], F32R)
        k_lo = st.sb("k_lo", [P, 2, d.CH], F32R)
        g_hi = st.sb("g_hi", [P, d.KT, d.CH], F32R)
        g_lo = st.sb("g_lo", [P, d.KT, d.CH], F32R)
        bd = st.sb("bd", [P, d.CH])
        bd_hi = st.sb("bd_hi", [P, d.CH], F32R)
        bd_lo = st.sb("bd_lo", [P, d.CH], F32R)
        srow = st.sb("srow", [1, d.CH])
        ones = st.sb("ones", [P, P])
        ones_r = st.sb("ones_r", [P, P], F32R)
        w = NormWork(st, d.TPC)
        ps_k = st.ps("ps_k", [P, 2, d.CH])
        ps_g = st.ps("ps_g", [P, d.KT, d.CH])
        ps_s = st.ps("ps_s", [P, d.CH])
        ps_v = st.ps("ps_v", [P, d.CH])
        ps_m = st.ps("ps_m", [P, 2, 2, d.E])

        w_in = [st.sem(f"w_in{i}") for i in range(2)]
        dv, gp, one_r = st.sem("dv"), st.sem("gp"), st.sem("one_r")
        w_ok = st.sem("w_ok")
        xn_ok, t_ps, hi_ok, lo_ok, xk_h, xk_ok = (st.sem(n) for n in ("xn_ok", "t_ps", "hi_ok", "lo_ok", "xk_h", "xk_ok"))
        k_ps, k_h, k_ok, g_ps, g_h, g_ok = (st.sem(n) for n in ("k_ps", "k_h", "k_ok", "g_ps", "g_h", "g_ok"))
        s_rd, s_col, s_ok = st.sem("s_rd"), st.sem("s_col"), st.sem("s_ok")
        v_ps, bd_ok, bd_h, bd_l, m_ps, m_ok = (st.sem(n) for n in ("v_ps", "bd_ok", "bd_h", "bd_l", "m_ps", "m_ok"))
        UN = NI * d.B

        with nc.Block() as block:
            @block.sync
            def _(sp):
                for n in range(NI):
                    for i, name in enumerate(("Wk", "Wv", "Wo")):
                        u = 3 * n + i
                        if u >= 2:
                            sp.wait_ge(w_ok, u - 1)
                        src = io["L1_attn_" + name]
                        if i < 2:
                            sp.dma_start(raw[:, u % 2, :].rearrange("p (k n) -> p k n", k=d.KT),
                                         src[:, n * d.CH:(n + 1) * d.CH].rearrange("(k p) n -> p k n", p=P))\
                                .then_inc(w_in[u % 2], 16)
                        else:
                            sp.dma_start(raw[:, u % 2, :].rearrange("p (c n) -> p c n", c=CPB),
                                         src[n * d.CH:(n + 1) * d.CH, :].rearrange("(c p) n -> p c n", p=P))\
                                .then_inc(w_in[u % 2], 16)

            @block.gpsimd
            def _(pool):
                link = chain(pool, gp)
                link(nc.gpsimd.memset(ones[:], 1.0))
                link(nc.gpsimd.memset(mask[:], 0.0))
                link(nc.gpsimd.memset(mask[0:HW, 0:HW], 1.0))
                link(nc.gpsimd.memset(mask[HW:P, HW:P], 1.0))
                link(nc.gpsimd.memset(srow[:], 0.0))
                nc.gpsimd.tensor_copy(ones_r[:], ones[:]).then_inc(one_r, 1)
                pool.wait_ge(one_r, 1)
                for n in range(NI):
                    for i in range(3):
                        u = 3 * n + i
                        pool.wait_ge(w_in[u % 2], 16 * (u // 2 + 1))
                        if n >= 1:
                            if i == 0:
                                pool.wait_ge(k_ps, TPB * d.B * n)
                            elif i == 1:
                                pool.wait_ge(v_ps, d.B * n)
                            else:
                                pool.wait_ge(m_ps, 2 * d.B * n)
                        link(nc.gpsimd.tensor_copy(w_hi[i][:], raw[:, u % 2, :]))
                        nc.gpsimd.tensor_tensor(w_lo[i][:], raw[:, u % 2, :], as_f32(w_hi[i][:]),
                                                ALU.subtract).then_inc(w_ok, 1)

            @block.vector
            def _(dve):
                link = chain(dve, dv)
                dve.wait_ge(one_r, 1)
                for c in range(d.NC):
                    norm_stats(nc, dve, link, w, [X[:, d.TPC * c + j, :] for j in range(d.TPC)], c + 1)
                    if c >= 1:
                        dve.wait_ge(t_ps, d.KT * c)
                        dve.wait_ge(xk_h, d.TPC * c)
                    for j in range(d.TPC):
                        ins = norm_apply(nc, w, j, xn[:, j, :], X[:, d.TPC * c + j, :])
                    ins.then_inc(xn_ok, 1)
                    for j in range(d.TPC):
                        t = d.TPC * c + j
                        dve.wait_ge(xk_h, t + 1)
                        nc.vector.tensor_tensor(xk_lo[:, t, :], xn[:, j, :], as_f32(xk_hi[:, t, :]),
                                                ALU.subtract).then_inc(xk_ok, 1)
                    for k in range(d.KT):
                        dve.wait_ge(hi_ok, d.KT * c + k + 1)
                        nc.vector.tensor_tensor(xt_lo[:, k, c * d.CH:(c + 1) * d.CH], ps_k[:, k, :],
                                                as_f32(xt_hi[:, k, c * d.CH:(c + 1) * d.CH]),
                                                ALU.subtract).then_inc(lo_ok, 1)
                for u in range(UN):
                    n, b = u // d.B, u % d.B
                    for t in range(TPB):
                        i = TPB * u + t
                        dve.wait_ge(k_h, i + 1)
                        nc.vector.scalar_tensor_tensor(out=k_lo[:, i % 2, :], in0=ps_k[:, i % 2, :], scalar=0.0,
                                                       in1=as_f32(k_hi[:, i % 2, :]), op0=ALU.max,
                                                       op1=ALU.subtract).then_inc(k_ok, 1)
                    for k in range(d.KT):
                        dve.wait_ge(g_h, d.KT * u + k + 1)
                        nc.vector.tensor_tensor(g_lo[:, k, :], ps_g[:, k, :], as_f32(g_hi[:, k, :]),
                                                ALU.subtract).then_inc(g_ok, 1)
                    dve.wait_ge(s_col, u + 1)
                    nc.vector.tensor_copy(ksum[:, b, CPB * n:CPB * (n + 1)], ps_s[:, 0:CPB]).then_inc(s_ok, 1)
                    dve.wait_ge(v_ps, u + 1)
                    if u >= 1:
                        dve.wait_ge(bd_l, u)
                    nc.vector.tensor_tensor(bd[:].rearrange("p (c m) -> p c m", m=P),
                                            ps_v[:].rearrange("p (c m) -> p c m", m=P),
                                            mask[:].unsqueeze(1).to_broadcast([P, CPB, P]),
                                            ALU.mult).then_inc(bd_ok, 1)
                    dve.wait_ge(bd_h, u + 1)
                    if u >= 1:
                        dve.wait_ge(m_ps, 2 * u)
                    nc.vector.tensor_tensor(bd_lo[:], bd[:], as_f32(bd_hi[:]), ALU.subtract).then_inc(bd_l, 1)

            @block.scalar
            def _(act):
                for c in range(d.NC):
                    norm_root(nc, act, w, c + 1)
                    act.wait_ge(xn_ok, c + 1)
                    for j in range(d.TPC):
                        t = d.TPC * c + j
                        nc.scalar.activation(xk_hi[:, t, :], xn[:, j, :], ACT.Copy).then_inc(xk_h, 1)
                    for k in range(d.KT):
                        act.wait_ge(t_ps, d.KT * c + k + 1)
                        nc.scalar.activation(xt_hi[:, k, c * d.CH:(c + 1) * d.CH], ps_k[:, k, :], ACT.Copy)\
                            .then_inc(hi_ok, 1)
                for u in range(UN):
                    n, b = u // d.B, u % d.B
                    for t in range(TPB):
                        i = TPB * u + t
                        act.wait_ge(k_ps, i + 1)
                        if i >= 2:
                            act.wait_ge(g_ps, i - 1)
                        nc.scalar.activation(k_hi[:, i % 2, :], ps_k[:, i % 2, :], ACT.Relu).then_inc(k_h, 1)
                    act.wait_ge(g_ps, TPB * (u + 1))
                    if u >= 1:
                        act.wait_ge(v_ps, u)
                    for k in range(d.KT):
                        nc.scalar.activation(g_hi[:, k, :], ps_g[:, k, :], ACT.Copy).then_inc(g_h, 1)
                    act.wait_ge(one_r, 1)
                    if u >= 1:
                        act.wait_ge(s_col, u)
                    nc.scalar.activation(srow[0:1, :], ps_s[0:1, :], ACT.Copy).then_inc(s_rd, 1)
                    act.wait_ge(bd_ok, u + 1)
                    if u >= 1:
                        act.wait_ge(m_ps, 2 * u)
                    nc.scalar.activation(bd_hi[:], bd[:], ACT.Copy).then_inc(bd_h, 1)
                    for j in range(2):
                        act.wait_ge(m_ps, 2 * u + j + 1)
                        nc.scalar.activation(M[:, b, CPB * n + 2 * j:CPB * n + 2 * j + 2, :], ps_m[:, j, :, :],
                                             ACT.Copy).then_inc(m_ok, 1)

            @block.tensor
            def _(pe):
                for c in range(d.NC):
                    pe.wait_ge(xn_ok, c + 1)
                    if c:
                        pe.wait_ge(lo_ok, d.KT * c)
                    for k in range(d.KT):
                        for j in range(d.TPC):
                            ins = nc.tensor.transpose(ps_k[:, k, j * P:(j + 1) * P], xn[:, j, k * P:(k + 1) * P],
                                                      ident[:])
                        ins.then_inc(t_ps, 1)
                pe.wait_ge(lo_ok, d.KT * d.NC)
                pe.wait_ge(xk_ok, d.NT)
                pe.wait_ge(one_r, 1)

                def keys(i):
                    u, t = i // TPB, i % TPB
                    n, b = u // d.B, u % d.B
                    if i % (TPB * d.B) == 0:
                        pe.wait_ge(w_ok, 3 * n + 1)
                    if i >= 2:
                        pe.wait_ge(k_ok, i - 1)
                    tok = slice((b * TPB + t) * P, (b * TPB + t + 1) * P)
                    for k in range(d.KT):
                        ins = mm_split(nc, ps_k[:, i % 2, :], xt_hi[:, k, tok], xt_lo[:, k, tok],
                                       w_hi[0][:, k * d.CH:(k + 1) * d.CH], w_lo[0][:, k * d.CH:(k + 1) * d.CH],
                                       k == 0, k == d.KT - 1)
                    ins.then_inc(k_ps, 1)

                def sums(i):
                    u, t = i // TPB, i % TPB
                    b = u % d.B
                    pe.wait_ge(k_ok, i + 1)
                    if t == 0 and u >= 1:
                        pe.wait_ge(g_ok, d.KT * u)
                        pe.wait_ge(s_ok, u)
                    kh, kl = k_hi[:, i % 2, :], k_lo[:, i % 2, :]
                    for m in range(d.KT):
                        x = slice(m * P, (m + 1) * P)
                        mm_split(nc, ps_g[:, m, :], xk_hi[:, b * TPB + t, x], xk_lo[:, b * TPB + t, x], kh, kl,
                                 t == 0, t == TPB - 1)
                    mm_split(nc, ps_s[:], ones_r[:], None, kh, kl, t == 0, t == TPB - 1).then_inc(g_ps, 1)

                keys(0)
                for u in range(UN):
                    n, b = u // d.B, u % d.B
                    for t in range(TPB):
                        i = TPB * u + t
                        if i + 1 < TPB * UN:
                            keys(i + 1)
                        sums(i)
                    pe.wait_ge(s_rd, u + 1)
                    for c in range(CPB):
                        ins = nc.tensor.matmul(ps_s[:, c:c + 1], srow[0:1, c * P:(c + 1) * P], ones[0:1, 0:1],
                                               start=True, stop=True)
                    ins.then_inc(s_col, 1)
                    pe.wait_ge(g_ok, d.KT * (u + 1))
                    pe.wait_ge(w_ok, 3 * n + 2)
                    if u >= 1:
                        pe.wait_ge(bd_ok, u)
                    for c in range(CPB):
                        cols = slice(c * P, (c + 1) * P)
                        for k in range(d.KT):
                            wv = slice(k * d.CH + c * P, k * d.CH + (c + 1) * P)
                            ins = mm_split(nc, ps_v[:, cols], w_hi[1][:, wv], w_lo[1][:, wv], g_hi[:, k, cols],
                                           g_lo[:, k, cols], k == 0, k == d.KT - 1)
                    ins.then_inc(v_ps, 1)
                    pe.wait_ge(bd_l, u + 1)
                    pe.wait_ge(w_ok, 3 * n + 3)
                    for c in range(CPB):
                        if c % 2 == 0 and u >= 1:
                            pe.wait_ge(m_ok, 2 * (u - 1) + c // 2 + 1)
                        cols, wo = slice(c * P, (c + 1) * P), slice(c * d.E, (c + 1) * d.E)
                        ins = mm_split(nc, ps_m[:, c // 2, c % 2, :], bd_hi[:, cols], bd_lo[:, cols],
                                       w_hi[2][:, wo], w_lo[2][:, wo], True, True)
                        if c % 2:
                            ins.then_inc(m_ps, 1)


def stage_queries(nc, d, io, keep):
    with ExitStack() as ctx:
        st = Store(nc, ctx, "qry")
        X, ident = keep["X"], keep["ident"]
        xt_hi, xt_lo, M, ksum, mask = (keep[n] for n in ("xt_hi", "xt_lo", "M", "ksum", "mask"))
        raw = st.sb("raw", [P, 2, d.INNER // 2])
        w_hi = st.sb("w_hi", [P, d.KT, d.INNER], F32R)
        w_lo = st.sb("w_lo", [P, d.KT, d.INNER], F32R)
        m_hi = st.sb("m_hi", [P, d.NCH, d.E], F32R)
        m_lo = st.sb("m_lo", [P, d.NCH, d.E], F32R)
        l_hi = st.sb("l_hi", [P, 2, P], F32R)
        l_lo = st.sb("l_lo", [P, 2, P], F32R)
        q_hi = st.sb("q_hi", [P, 2, d.CH], F32R)
        q_lo = st.sb("q_lo", [P, 2, d.CH], F32R)
        rec = st.sb("rec", [P, 2, d.CH])
        qn = st.sb("qn", [P, 2, d.CH])
        qr = st.sb("qr", [P, 2, d.CH])
        n_hi = st.sb("n_hi", [P, 2, d.CH], F32R)
        n_lo = st.sb("n_lo", [P, 2, d.CH], F32R)
        bo = st.sb("bo", [P, d.E])
        ot = st.sb("ot", [P, d.KT, d.CH])
        ps_q = st.ps("ps_q", [P, 2, d.CH])
        ps_n = st.ps("ps_n", [P, 2, d.CH])
        ps_o = st.ps("ps_o", [P, d.KT, d.CH])
        ps_x = st.ps("ps_x", [P, 2, 2, d.E])
        w_in = [st.sem(f"w_in{i}") for i in range(2)]
        b_in, xb_ok, w_ok, gp, dv = st.sem("b_in"), st.sem("xb_ok"), st.sem("w_ok"), st.sem("gp"), st.sem("dv")
        m_h, m_l, l_h, l_ok = st.sem("m_h"), st.sem("m_l"), st.sem("l_h"), st.sem("l_ok")
        q_ps, q_h, q_ok, n_ps, rec_ok, qn_ok, qr_ok, n_h, n_ok = (
            st.sem(n) for n in ("q_ps", "q_h", "q_ok", "n_ps", "rec_ok", "qn_ok", "qr_ok", "n_h", "n_ok"))
        o_ps, ot_ok, x_ps, x_rd = st.sem("o_ps"), st.sem("ot_ok"), st.sem("x_ps"), st.sem("x_rd")
        NJ = d.S // d.CH
        UN = d.NC * d.NCH
        PIECES = 4

        with nc.Block() as block:
            def m_part(nc, pool, b):
                pool.wait_ge(m_h, b + 1)
                nc.gpsimd.tensor_tensor(m_lo[:], M[:, b], as_f32(m_hi[:]), ALU.subtract).then_inc(m_l, 1)

            def add(nc, dve, c):
                dve.wait_ge(xb_ok, 1)
                for j in range(2):
                    dve.wait_ge(x_ps, 2 * c + j + 1)
                    t = d.TPC * c + 2 * j
                    nc.vector.tensor_tensor(X[:, t:t + 2, :], X[:, t:t + 2, :], ps_x[:, j], ALU.add).then_inc(x_rd, 1)

            @block.sync
            def _(sp):
                for i in range(PIECES):
                    if i >= 2:
                        sp.wait_ge(w_ok, i - 1)
                    k, half = i % 2, i // 2
                    cols = slice(half * d.INNER // 2, (half + 1) * d.INNER // 2)
                    sp.dma_start(raw[:, i % 2, :], io["L1_attn_Wq"][k * P:(k + 1) * P, cols]).then_inc(w_in[i % 2], 16)
                    if i == 0:
                        sp.dma_start(bo[:], io["L1_attn_bo"].rearrange("(a n) -> a n", a=1).to_broadcast([P, d.E]))\
                            .then_inc(b_in, 16)

            @block.gpsimd
            def _(pool):
                link = chain(pool, gp)
                for i in range(PIECES):
                    k, half = i % 2, i // 2
                    cols = slice(half * d.INNER // 2, (half + 1) * d.INNER // 2)
                    pool.wait_ge(w_in[i % 2], 16 * (i // 2 + 1))
                    link(nc.gpsimd.tensor_copy(w_hi[:, k, cols], raw[:, i % 2, :]))
                    nc.gpsimd.tensor_tensor(w_lo[:, k, cols], raw[:, i % 2, :], as_f32(w_hi[:, k, cols]),
                                            ALU.subtract).then_inc(w_ok, 1)
                    if i == 1:
                        m_part(nc, pool, 0)
                pool.wait_ge(b_in, 16)
                for t in range(d.NT):
                    ins = nc.gpsimd.tensor_tensor(X[:, t, :], X[:, t, :], bo[:], ALU.add)
                ins.then_inc(xb_ok, 1)
                for u in range(UN):
                    pool.wait_ge(n_h, u + 1)
                    if u >= 2:
                        pool.wait_ge(o_ps, u - 1)
                    nc.gpsimd.tensor_tensor(n_lo[:, u % 2, :], qr[:, u % 2, :], as_f32(n_hi[:, u % 2, :]),
                                            ALU.subtract).then_inc(n_ok, 1)
                    if u == UN // 2 - 1:
                        m_part(nc, pool, 1)

            @block.vector
            def _(dve):
                def low(u):
                    b, c = u // (NJ * d.NCH), u % d.NCH
                    dve.wait_ge(l_h, u + 1)
                    nc.vector.scalar_tensor_tensor(out=l_lo[:, u % 2, :], in0=mask[:], scalar=ksum[:, b, c:c + 1],
                                                   in1=as_f32(l_hi[:, u % 2, :]), op0=ALU.mult,
                                                   op1=ALU.subtract).then_inc(l_ok, 1)
                    dve.wait_ge(q_h, u + 1)
                    nc.vector.scalar_tensor_tensor(out=q_lo[:, u % 2, :], in0=ps_q[:, u % 2, :], scalar=0.0,
                                                   in1=as_f32(q_hi[:, u % 2, :]), op0=ALU.max,
                                                   op1=ALU.subtract).then_inc(q_ok, 1)

                def divide(u):
                    dve.wait_ge(n_ps, u + 1)
                    if u >= 2:
                        dve.wait_ge(qn_ok, u - 1)
                    nc.vector.reciprocal(rec[:, u % 2, :], ps_n[:, u % 2, :]).then_inc(rec_ok, 1)
                    dve.wait_ge(rec_ok, u + 1)
                    if u >= 2:
                        dve.wait_ge(n_h, u - 1)
                    nc.vector.scalar_tensor_tensor(out=qn[:, u % 2, :], in0=rec[:, u % 2, :], scalar=1e6,
                                                   in1=ps_q[:, u % 2, :], op0=ALU.min, op1=ALU.mult)\
                        .then_inc(qn_ok, 1)

                for u in range(UN):
                    low(u)
                    if u >= 1:
                        divide(u - 1)
                    if u % d.NCH == 2 and u > d.NCH:
                        add(nc, dve, u // d.NCH - 1)
                divide(UN - 1)
                add(nc, dve, d.NC - 1)

            @block.scalar
            def _(act):
                def high(u):
                    b, c = u // (NJ * d.NCH), u % d.NCH
                    if u >= 2:
                        act.wait_ge(n_ps, u - 1)
                    nc.scalar.activation(l_hi[:, u % 2, :], mask[:], ACT.Copy, scale=ksum[:, b, c:c + 1])\
                        .then_inc(l_h, 1)
                    act.wait_ge(q_ps, u + 1)
                    nc.scalar.activation(q_hi[:, u % 2, :], ps_q[:, u % 2, :], ACT.Relu).then_inc(q_h, 1)

                def high_n(u):
                    act.wait_ge(qn_ok, u + 1)
                    if u >= 2:
                        act.wait_ge(n_ok, u - 1)
                        act.wait_ge(o_ps, u - 1)
                    nc.scalar.activation(qr[:, u % 2, :], qn[:, u % 2, :], ACT.Relu).then_inc(qr_ok, 1)
                    nc.scalar.activation(n_hi[:, u % 2, :], qn[:, u % 2, :], ACT.Relu).then_inc(n_h, 1)

                def turn(c):
                    act.wait_ge(o_ps, d.NCH * (c + 1))
                    if c:
                        act.wait_ge(x_ps, 2 * c)
                    for m in range(d.KT):
                        nc.scalar.activation(ot[:, m, :], ps_o[:, m, :], ACT.Copy).then_inc(ot_ok, 1)

                for u in range(UN):
                    high(u)
                    if u >= 1:
                        high_n(u - 1)
                    if u % (NJ * d.NCH) == 0:
                        b = u // (NJ * d.NCH)
                        if b:
                            act.wait_ge(o_ps, u)
                        nc.scalar.activation(m_hi[:], M[:, b], ACT.Copy).then_inc(m_h, 1)
                    if u % d.NCH == 1 and u > d.NCH:
                        turn(u // d.NCH - 1)
                high_n(UN - 1)
                turn(d.NC - 1)

            @block.tensor
            def _(pe):
                def query(u):
                    j, c = u // d.NCH, u % d.NCH
                    if u < d.NCH:
                        pe.wait_ge(w_ok, 2 * (c // (d.NCH // 2)) + 2)
                    if u >= 2:
                        pe.wait_ge(qn_ok, u - 1)
                    cols, tok = slice(c * P, (c + 1) * P), slice(j * d.CH, (j + 1) * d.CH)
                    for k in range(d.KT):
                        ins = mm_split(nc, ps_q[:, u % 2, :], w_hi[:, k, cols], w_lo[:, k, cols],
                                       xt_hi[:, k, tok], xt_lo[:, k, tok], k == 0, k == d.KT - 1)
                    ins.then_inc(q_ps, 1)

                def normal(u):
                    pe.wait_ge(q_ok, u + 1)
                    pe.wait_ge(l_ok, u + 1)
                    if u >= 2:
                        pe.wait_ge(rec_ok, u - 1)
                    mm_split(nc, ps_n[:, u % 2, :], l_hi[:, u % 2, :], l_lo[:, u % 2, :], q_hi[:, u % 2, :],
                             q_lo[:, u % 2, :], True, True).then_inc(n_ps, 1)

                def result(u):
                    j, c = u // d.NCH, u % d.NCH
                    if u % (NJ * d.NCH) == 0:
                        pe.wait_ge(m_l, u // (NJ * d.NCH) + 1)
                    if c == 0 and j:
                        pe.wait_ge(ot_ok, d.KT * j)
                    pe.wait_ge(n_ok, u + 1)
                    for m in range(d.KT):
                        cols = slice(m * P, (m + 1) * P)
                        ins = mm_split(nc, ps_o[:, m, :], m_hi[:, c, cols], m_lo[:, c, cols], n_hi[:, u % 2, :],
                                       n_lo[:, u % 2, :], c == 0, c == d.NCH - 1)
                    ins.then_inc(o_ps, 1)

                def back(c):
                    pe.wait_ge(ot_ok, d.KT * (c + 1))
                    for j in range(2):
                        if c:
                            pe.wait_ge(x_rd, 2 * (c - 1) + j + 1)
                        for i in range(2):
                            for m in range(d.KT):
                                t = 2 * j + i
                                ins = nc.tensor.transpose(ps_x[:, j, i, m * P:(m + 1) * P],
                                                          ot[:, m, t * P:(t + 1) * P], ident[:])
                        ins.then_inc(x_ps, 1)

                for u in range(UN):
                    query(u)
                    if u >= 1:
                        normal(u - 1)
                    if u >= 2:
                        result(u - 2)
                    if u % d.NCH == 1 and u > d.NCH:
                        back(u // d.NCH - 1)
                normal(UN - 1)
                result(UN - 2)
                result(UN - 1)
                back(d.NC - 1)


def stage_routed(nc, d, io, keep, out):
    with ExitStack() as ctx:
        st = Store(nc, ctx, "rt")
        X, ident = keep["X"], keep["ident"]
        NE = io["L1_ffn_wr"].shape[0]
        names = ("w1", "w3", "w2")
        raw = st.sb("raw", [P, 3, d.KT, d.E])
        wr_raw = st.sb("wr_raw", [NE, d.E])
        wt_hi = st.sb("wt_hi", [P, 3, d.KT, d.E], F32R)
        wt_lo = st.sb("wt_lo", [P, 3, d.KT, d.E], F32R)
        w2t = st.sb("w2t", [P, d.KT, d.E])
        wr_hi = st.sb("wr_hi", [P, d.KT, NE], F32R)
        wr_lo = st.sb("wr_lo", [P, d.KT, NE], F32R)
        xn = st.sb("xn", [P, d.TPC, d.E])
        xt_hi = st.sb("xt_hi", [P, d.KT, d.CH], F32R)
        xt_lo = st.sb("xt_lo", [P, d.KT, d.CH], F32R)
        h1 = st.sb("h1", [P, d.KT, d.CH])
        h_hi = st.sb("h_hi", [P, d.KT, d.CH], F32R)
        h_lo = st.sb("h_lo", [P, d.KT, d.CH], F32R)
        h2 = st.sb("h2", [P, d.TPC, d.E])
        lg = st.sb("lg", [P, d.TPC, NE])
        lmax = st.sb("lmax", [P, d.TPC])
        ex = st.sb("ex", [P, d.TPC, NE])
        esum = st.sb("esum", [P, d.TPC])
        pr = st.sb("pr", [P, d.TPC, NE])
        best = st.sb("best", [P, d.TPC, 8])
        idx = st.sb("idx", [P, d.TPC, 8], U32)
        idx_f = st.sb("idx_f", [P, d.TPC, 2])
        oh = st.sb("oh", [P, 2, d.TPC, NE])
        gs = st.sb("gs", [P, d.TPC])
        gate = st.sb("gate", [P, d.TPC, NE])
        iota_i = st.sb("iota_i", [P, NE], mybir.dt.int32)
        iota_f = st.sb("iota_f", [P, NE])
        acc = st.sb("acc", [NE, d.E])
        acc_t = st.sb("acc_t", [P, d.KT, NE])
        w = NormWork(st, d.TPC)
        ps_t = st.ps("ps_t", [P, d.KT, d.CH])
        ps_h = st.ps("ps_h", [P, d.KT, d.CH])
        ps_2 = st.ps("ps_2", [P, 2, 2, d.E])
        ps_l = st.ps("ps_l", [P, d.CH])
        ps_a = st.ps("ps_a", [NE, d.E])
        w_in, dv, on, out_s = st.sem("w_in"), st.sem("dv"), st.sem("on"), st.sem("out")
        wt_ps, wt_h, wt_l = st.sem("wt_ps"), st.sem("wt_h"), st.sem("wt_l")
        xn_ok, t_ps, hi_ok, lo_ok = (st.sem(n) for n in ("xn_ok", "t_ps", "hi_ok", "lo_ok"))
        h_ps, h1_ok, hh_ok, hl_ok, l_ps, lmax_ok, ex_ok = (
            st.sem(n) for n in ("h_ps", "h1_ok", "hh_ok", "hl_ok", "l_ps", "lmax_ok", "ex_ok"))
        h2_ps, h2_ok, g_ok, a_ps = st.sem("h2_ps"), st.sem("h2_ok"), st.sem("g_ok"), st.sem("a_ps")
        acc_ok, at_ps, at_ok, fin_ps, fin_ok = (st.sem(n) for n in ("acc_ok", "at_ps", "at_ok", "fin_ps", "fin_ok"))
        out_tiles = out.rearrange("b (t p) e -> p (b t) e", p=P)

        with nc.Block() as block:
            @block.sync
            def _(sp):
                for i, name in enumerate(names):
                    sp.dma_start(raw[:, i], io["L1_ffn_" + name].rearrange("(a p) n -> p a n", p=P)).then_inc(w_in, 16)
                sp.dma_start(wr_raw[:], io["L1_ffn_wr"]).then_inc(w_in, 16)
                sp.dma_start(out_tiles[:, 1:, :], X[:, 1:, :]).then_inc(out_s, 16)
                sp.wait_ge(fin_ok, 1)
                sp.dma_start(out_tiles[:, 0, :], X[:, 0, :]).then_inc(out_s, 16)
                sp.wait_ge(out_s, 32)

            @block.gpsimd
            def _(pool):
                nc.gpsimd.iota(iota_i[:], pattern=[[1, NE]], base=0, channel_multiplier=0).then_inc(on, 1)

            @block.vector
            def _(dve):
                link = chain(dve, dv)
                nc.vector.memset(ps_l[:], 0.0).then_inc(on, 1)
                dve.wait_ge(on, 2)
                nc.vector.tensor_copy(iota_f[:], iota_i[:])
                for i in range(3):
                    dve.wait_ge(wt_h, i + 1)
                    src = ps_h if i % 2 else ps_t
                    flat = src[:].rearrange("p k c -> p (k c)")[:, 0:d.KT * d.E]
                    if i < 2:
                        nc.vector.tensor_tensor(wt_lo[:, i].rearrange("p k n -> p (k n)"), flat,
                                                as_f32(wt_hi[:, i]).rearrange("p k n -> p (k n)"),
                                                ALU.subtract).then_inc(wt_l, 1)
                    else:
                        nc.vector.tensor_copy(w2t[:].rearrange("p k n -> p (k n)"), flat).then_inc(wt_l, 1)
                dve.wait_ge(wt_h, 4)
                nc.vector.tensor_tensor(wr_lo[:], ps_l[:, 0:d.KT * NE].rearrange("p (k n) -> p k n", n=NE),
                                        as_f32(wr_hi[:]), ALU.subtract).then_inc(wt_l, 1)
                for c in range(d.NC):
                    norm_stats(nc, dve, link, w, [X[:, d.TPC * c + j, :] for j in range(d.TPC)], c + 1)
                    if c >= 1:
                        dve.wait_ge(t_ps, d.KT * c)
                    for j in range(d.TPC):
                        ins = norm_apply(nc, w, j, xn[:, j, :], X[:, d.TPC * c + j, :])
                    ins.then_inc(xn_ok, 1)
                    for k in range(d.KT):
                        dve.wait_ge(hi_ok, d.KT * c + k + 1)
                        nc.vector.tensor_tensor(xt_lo[:, k, :], ps_t[:, k, :], as_f32(xt_hi[:, k, :]),
                                                ALU.subtract).then_inc(lo_ok, 1)
                    dve.wait_ge(l_ps, c + 1)
                    link(nc.vector.tensor_copy(lg[:].rearrange("p j e -> p (j e)"), ps_l[:, 0:d.TPC * NE]))
                    link(nc.vector.tensor_reduce(lmax[:], lg[:], AX.X, ALU.max))
                    nc.vector.tensor_tensor(lg[:], lg[:], lmax[:].unsqueeze(2).to_broadcast([P, d.TPC, NE]),
                                            ALU.subtract).then_inc(lmax_ok, 1)
                    for m in range(d.KT):
                        dve.wait_ge(hh_ok, d.KT * c + m + 1)
                        nc.vector.tensor_tensor(h_lo[:, m, :], h1[:, m, :], as_f32(h_hi[:, m, :]),
                                                ALU.subtract).then_inc(hl_ok, 1)
                    dve.wait_ge(ex_ok, c + 1)
                    link(nc.vector.tensor_reduce(esum[:], ex[:], AX.X, ALU.add))
                    link(nc.vector.reciprocal(esum[:], esum[:]))
                    link(nc.vector.tensor_tensor(pr[:], ex[:], esum[:].unsqueeze(2).to_broadcast([P, d.TPC, NE]),
                                                 ALU.mult))
                    for j in range(d.TPC):
                        ins = nc.vector.max(best[:, j, :], pr[:, j, :])
                    link(ins)
                    for j in range(d.TPC):
                        ins = nc.vector.max_index(idx[:, j, :], best[:, j, :], pr[:, j, :])
                    link(ins)
                    link(nc.vector.tensor_copy(idx_f[:], idx[:, :, 0:2]))
                    for i in range(2):
                        ins = nc.vector.tensor_tensor(oh[:, i], idx_f[:, :, i:i + 1].to_broadcast([P, d.TPC, NE]),
                                                      iota_f[:].unsqueeze(1).to_broadcast([P, d.TPC, NE]),
                                                      ALU.is_equal)
                    link(ins)
                    for i in range(2):
                        ins = nc.vector.tensor_tensor(oh[:, i], oh[:, i],
                                                      best[:, :, i:i + 1].to_broadcast([P, d.TPC, NE]), ALU.mult)
                    link(ins)
                    nc.vector.tensor_tensor(gs[:], best[:, :, 0], best[:, :, 1], ALU.add)
                    link(nc.vector.tensor_tensor(oh[:, 0], oh[:, 0], oh[:, 1], ALU.add))
                    link(nc.vector.reciprocal(gs[:], gs[:]))
                    if c >= 1:
                        dve.wait_ge(a_ps, c)
                    nc.vector.tensor_tensor(gate[:], oh[:, 0], gs[:].unsqueeze(2).to_broadcast([P, d.TPC, NE]),
                                            ALU.mult).then_inc(g_ok, 1)
                dve.wait_ge(a_ps, d.NC)
                nc.vector.tensor_copy(acc[:], ps_a[:]).then_inc(acc_ok, 1)
                dve.wait_ge(at_ps, 1)
                nc.vector.tensor_copy(acc_t[:].rearrange("p k e -> p (k e)"), ps_l[:, 0:d.KT * NE]).then_inc(at_ok, 1)
                dve.wait_ge(fin_ps, 1)
                nc.vector.tensor_tensor(X[0:NE, 0, :], X[0:NE, 0, :], ps_a[:], ALU.add).then_inc(fin_ok, 1)

            @block.scalar
            def _(act):
                for i in range(3):
                    act.wait_ge(wt_ps, i + 1)
                    src = ps_h if i % 2 else ps_t
                    flat = src[:].rearrange("p k c -> p (k c)")[:, 0:d.KT * d.E]
                    nc.scalar.activation(wt_hi[:, i].rearrange("p k n -> p (k n)"), flat, ACT.Copy).then_inc(wt_h, 1)
                act.wait_ge(wt_ps, 4)
                nc.scalar.activation(wr_hi[:].rearrange("p k n -> p (k n)"), ps_l[:, 0:d.KT * NE], ACT.Copy)\
                    .then_inc(wt_h, 1)
                for c in range(d.NC):
                    norm_root(nc, act, w, c + 1)
                    for k in range(d.KT):
                        act.wait_ge(t_ps, d.KT * c + k + 1)
                        if c:
                            act.wait_ge(l_ps, c)
                            act.wait_ge(h_ps, d.KT * c)
                        nc.scalar.activation(xt_hi[:, k, :], ps_t[:, k, :], ACT.Copy).then_inc(hi_ok, 1)
                    for m in range(d.KT):
                        act.wait_ge(h_ps, d.KT * c + m + 1)
                        if c:
                            act.wait_ge(hl_ok, d.KT * c)
                            act.wait_ge(h2_ps, 2 * c)
                        nc.scalar.activation(h1[:, m, :], ps_h[:, m, :], ACT.Silu).then_inc(h1_ok, 1)
                        act.wait_ge(h1_ok, d.KT * c + m + 1)
                        nc.scalar.activation(h_hi[:, m, :], h1[:, m, :], ACT.Copy).then_inc(hh_ok, 1)
                    for j in range(2):
                        act.wait_ge(h2_ps, 2 * c + j + 1)
                        if c:
                            act.wait_ge(a_ps, c)
                        nc.scalar.activation(h2[:, 2 * j:2 * j + 2, :], ps_2[:, j], ACT.Silu).then_inc(h2_ok, 1)
                    act.wait_ge(lmax_ok, c + 1)
                    nc.scalar.activation(ex[:], lg[:], ACT.Exp).then_inc(ex_ok, 1)

            @block.tensor
            def _(pe):
                pe.wait_ge(w_in, 64)
                for i in range(3):
                    dst = ps_h if i % 2 else ps_t
                    flat = dst[:].rearrange("p k c -> p (k c)")
                    if i == 2:
                        pe.wait_ge(wt_l, 1)
                    for k in range(d.KT):
                        for a in range(d.KT):
                            ins = nc.tensor.transpose(flat[:, k * d.E + a * P:k * d.E + (a + 1) * P],
                                                      raw[:, i, a, k * P:(k + 1) * P], ident[:])
                    ins.then_inc(wt_ps, 1)
                pe.wait_ge(on, 2)
                for k in range(d.KT):
                    ins = nc.tensor.transpose(ps_l[:, k * NE:(k + 1) * NE], wr_raw[:, k * P:(k + 1) * P],
                                              ident[0:NE, 0:NE])
                ins.then_inc(wt_ps, 1)
                pe.wait_ge(wt_l, 4)
                for c in range(d.NC):
                    pe.wait_ge(xn_ok, c + 1)
                    if c:
                        pe.wait_ge(lo_ok, d.KT * c)
                    for k in range(d.KT):
                        for j in range(d.TPC):
                            ins = nc.tensor.transpose(ps_t[:, k, j * P:(j + 1) * P], xn[:, j, k * P:(k + 1) * P],
                                                      ident[:])
                        ins.then_inc(t_ps, 1)
                    pe.wait_ge(lo_ok, d.KT * (c + 1))
                    for j in range(d.TPC):
                        t = slice(j * P, (j + 1) * P)
                        if c and j == 0:
                            pe.wait_ge(lmax_ok, c)
                        for k in range(d.KT):
                            ins = mm_split(nc, ps_l[:, j * NE:(j + 1) * NE], xt_hi[:, k, t], xt_lo[:, k, t],
                                           wr_hi[:, k, :], wr_lo[:, k, :], k == 0, k == d.KT - 1)
                    ins.then_inc(l_ps, 1)
                    for m in range(d.KT):
                        cols = slice(m * P, (m + 1) * P)
                        if c:
                            pe.wait_ge(h1_ok, d.KT * (c - 1) + m + 1)
                        for k in range(d.KT):
                            ins = mm_split(nc, ps_h[:, m, :], wt_hi[:, 0, k, cols], wt_lo[:, 0, k, cols],
                                           xt_hi[:, k, :], xt_lo[:, k, :], k == 0, k == d.KT - 1)
                        ins.then_inc(h_ps, 1)
                    pe.wait_ge(hl_ok, d.KT * (c + 1))
                    for j in range(2):
                        if c:
                            pe.wait_ge(h2_ok, 2 * (c - 1) + j + 1)
                        for i in range(2):
                            t = slice((2 * j + i) * P, (2 * j + i + 1) * P)
                            for k in range(d.KT):
                                ins = mm_split(nc, ps_2[:, j, i, :], h_hi[:, k, t], h_lo[:, k, t],
                                               wt_hi[:, 1, k, :], wt_lo[:, 1, k, :], k == 0, k == d.KT - 1)
                        ins.then_inc(h2_ps, 1)
                    pe.wait_ge(g_ok, c + 1)
                    pe.wait_ge(h2_ok, 2 * (c + 1))
                    for j in range(d.TPC):
                        ins = nc.tensor.matmul(ps_a[:], gate[:, j, :], h2[:, j, :], start=c == 0 and j == 0,
                                               stop=c == d.NC - 1 and j == d.TPC - 1)
                    ins.then_inc(a_ps, 1)
                pe.wait_ge(acc_ok, 1)
                for k in range(d.KT):
                    ins = nc.tensor.transpose(ps_l[:, k * NE:(k + 1) * NE], acc[:, k * P:(k + 1) * P],
                                              ident[0:NE, 0:NE])
                ins.then_inc(at_ps, 1)
                pe.wait_ge(at_ok, 1)
                for k in range(d.KT):
                    ins = nc.tensor.matmul(ps_a[:], acc_t[:, k, :], w2t[:, k, :], start=k == 0, stop=k == d.KT - 1)
                ins.then_inc(fin_ps, 1)


INS = ["L0_attn_x", "L0_attn_W_attn", "L0_attn_W_proj", "L0_attn_lambda_q1", "L0_attn_lambda_k1",
       "L0_attn_lambda_q2", "L0_attn_lambda_k2", "L0_ffn_W_syn", "L0_ffn_b_syn", "L0_ffn_W_out", "L0_ffn_b_out",
       "L0_ffn_gamma", "L0_ffn_beta", "L1_attn_Wq", "L1_attn_Wk", "L1_attn_Wv", "L1_attn_Wo", "L1_attn_bo",
       "L1_ffn_w1", "L1_ffn_w3", "L1_ffn_w2", "L1_ffn_wr"]


def two_layers(nc, io, out, dump=None):
    d = Dims(io["L0_attn_x"], io["L0_ffn_W_syn"], io["L1_attn_Wq"])
    with ExitStack() as ctx:
        keep = {
            "X": ctx.enter_context(nc.sbuf_tensor("residual", [P, d.NT, d.E], F32)),
            "ident": ctx.enter_context(nc.sbuf_tensor("ident", [P, P], F32)),
        }
        with ExitStack() as att:
            keep["AO"] = att.enter_context(nc.sbuf_tensor("att_out", [P, d.NT, d.E], F32))
            scratch = {
                "qk": nc.dram_tensor("qk_parts", [2, d.B, 2 * d.E, d.S], F32).ap(),
                "v": nc.dram_tensor("v_rows", [d.B, d.H // d.G, P, d.S // P, d.G * 32], F32).ap(),
                "zero": nc.dram_tensor("zero_rows", [2, d.G * d.S], F32).ap(),
            }
            stage_qkv(nc, d, io, keep, scratch)
            stage_attention(nc, d, io, keep, scratch)
            if dump == "att":
                return dump_tile(nc, d, keep["AO"], out)
            stage_mlp(nc, d, io, keep)
        if dump == "x2":
            return dump_tile(nc, d, keep["X"], out)
        with ExitStack() as lin:
            def sb(name, shape, dt=F32):
                return lin.enter_context(nc.sbuf_tensor("lin_" + name, shape, dt))
            keep["xt_hi"] = sb("xt_hi", [P, d.KT, d.TOK], F32R)
            keep["xt_lo"] = sb("xt_lo", [P, d.KT, d.TOK], F32R)
            keep["M"] = sb("m", [P, d.B, d.NCH, d.E])
            keep["ksum"] = sb("ksum", [P, d.B, d.NCH])
            keep["mask"] = sb("mask", [P, P])
            stage_keys(nc, d, io, keep)
            stage_queries(nc, d, io, keep)
        if dump == "x3":
            return dump_tile(nc, d, keep["X"], out)
        stage_routed(nc, d, io, keep, out)


def kernel(**inputs):
    import numpy as np
    import concourse.bacc as bacc
    from concourse.bass_utils import run_bass_kernel_spmd

    nc = bacc.Bacc("TRN2", target_bir_lowering=False, num_devices=1)
    arrays, io = {}, {}
    for name in INS:
        a = np.ascontiguousarray(inputs[name])
        arrays[name] = a
        io[name] = nc.dram_tensor(name, a.shape, mybir.dt.from_np(a.dtype), kind="ExternalInput").ap()
    shape = arrays["L0_attn_x"].shape
    out = nc.dram_tensor("out", shape, F32, kind="ExternalOutput").ap()
    two_layers(nc, io, out)
    r = run_bass_kernel_spmd(nc, [arrays], core_ids=[0])
    return r.results[0]["out"]
```

```python
import math
from contextlib import ExitStack

import concourse.bass as bass
from concourse import mybir

F32 = mybir.dt.float32
F32R = mybir.dt.float32r
U32 = mybir.dt.uint32
ALU = mybir.AluOpType
ACT = mybir.ActivationFunctionType
AX = mybir.AxisListType

P = 128
EPS = 1e-5
LAMBDA_INIT = 0.8 - 0.6 * math.exp(-0.3 * 0)


def as_f32(ap):
    return ap.bitcast(F32)


class Dims:

    def __init__(self, x, w_syn, wq):
        self.B, self.S, self.E = x.shape
        self.TOK = self.B * self.S
        self.NT = self.TOK // P
        self.CH = 512
        self.TPC = self.CH // P
        self.NC = self.TOK // self.CH
        self.KT = self.E // P
        self.H = 16
        self.HD = self.E // self.H
        self.G = 4
        self.NG = self.H // self.G * self.B
        self.N = w_syn.shape[0]
        self.INNER = wq.shape[1]
        self.NCH = self.INNER // P


class Store:

    def __init__(self, nc, ctx, stage):
        self.nc, self.ctx, self.stage = nc, ctx, stage
        self.sems = []

    def sb(self, name, shape, dt=F32):
        return self.ctx.enter_context(self.nc.sbuf_tensor(f"{self.stage}_{name}", shape, dt))

    def ps(self, name, shape):
        return self.ctx.enter_context(self.nc.psum_tensor(f"{self.stage}_{name}", shape, F32))

    def sem(self, name):
        s = self.ctx.enter_context(self.nc.semaphore(f"{self.stage}_{name}"))
        self.sems.append(s.num)
        return s

    def clear(self):
        nc, first, last = self.nc, min(self.sems), max(self.sems)
        assert last - first + 1 == len(self.sems)
        with nc.Block() as block:
            @block.sync
            def _(sp):
                sp.sem_clear(range(first, last + 1))


def chain(eng, sem):
    done = [0]

    def link(ins):
        done[0] += 1
        ins.then_inc(sem, 1)
        eng.wait_ge(sem, done[0])
    return link


class NormWork:

    def __init__(self, st, tiles, tag=""):
        self.stats = st.sb("stats" + tag, [P, tiles, 6])
        self.mv = st.sb("mv" + tag, [P, tiles, 2])
        self.ve = st.sb("ve" + tag, [P, tiles])
        self.sd = st.sb("sd" + tag, [P, tiles])
        self.r0 = st.sb("r0" + tag, [P, tiles])
        self.t0 = st.sb("t0" + tag, [P, tiles])
        self.rstd = st.sb("rstd" + tag, [P, tiles])
        self.var_ready = st.sem("var_ready" + tag)
        self.sd_ready = st.sem("sd_ready" + tag)


def norm_stats(nc, dve, link, w, tiles, nth):
    for j, x in enumerate(tiles):
        ins = nc.vector.bn_stats(w.stats[:, j, :], x)
    link(ins)
    for j in range(len(tiles)):
        ins = nc.vector.bn_aggr(w.mv[:, j, :], w.stats[:, j, :])
    link(ins)
    nc.vector.tensor_scalar(w.ve[:], w.mv[:, :, 1], EPS, None, ALU.add).then_inc(w.var_ready, 1)
    dve.wait_ge(w.sd_ready, nth)
    link(nc.vector.reciprocal(w.r0[:], w.sd[:]))
    link(nc.vector.tensor_tensor(w.t0[:], w.r0[:], w.r0[:], ALU.mult))
    link(nc.vector.tensor_tensor(w.t0[:], w.t0[:], w.ve[:], ALU.mult))
    link(nc.vector.tensor_scalar(w.t0[:], w.t0[:], -0.5, 1.5, ALU.mult, ALU.add))
    link(nc.vector.tensor_tensor(w.rstd[:], w.t0[:], w.r0[:], ALU.mult))


def norm_root(nc, act, w, nth):
    act.wait_ge(w.var_ready, nth)
    nc.scalar.activation(w.sd[:], w.ve[:], ACT.Sqrt).then_inc(w.sd_ready, 1)


def norm_apply(nc, w, j, out, x):
    return nc.vector.tensor_scalar(out, x, w.mv[:, j, 0:1], w.rstd[:, j:j + 1], ALU.subtract, ALU.mult)


def mm_split(nc, out, lhs_hi, lhs_lo, rhs_hi, rhs_lo, first, last):
    terms = [(lhs_hi, rhs_hi)]
    if rhs_lo is not None:
        terms.append((lhs_hi, rhs_lo))
    if lhs_lo is not None:
        terms.append((lhs_lo, rhs_hi))
    for n, (a, b) in enumerate(terms):
        ins = nc.tensor.matmul(out, a, b, start=first and n == 0, stop=last and n == len(terms) - 1)
    return ins


def stage_qkv(nc, d, io, keep, scratch):
    with ExitStack() as ctx:
        st = Store(nc, ctx, "qkv")
        X, ident = keep["X"], keep["ident"]
        q_dram, v_dram, zero_dram = scratch["qk"], scratch["v"], scratch["zero"]
        w_raw = st.sb("w_raw", [P, d.KT, 3 * d.E])
        w_hi = st.sb("w_hi", [P, d.KT, 3 * d.E], F32R)
        w_lo = st.sb("w_lo", [P, d.KT, 3 * d.E], F32R)
        xn = st.sb("xn", [P, d.TPC, d.E])
        xt_hi = st.sb("xt_hi", [P, 2, d.KT, d.CH], F32R)
        xt_lo = st.sb("xt_lo", [P, 2, d.KT, d.CH], F32R)
        NQ = 2 * d.E // P
        qk_hi = st.sb("qk_hi", [P, NQ, d.CH], F32R)
        qk_lo = st.sb("qk_lo", [P, NQ, d.CH], F32R)
        v_st = st.sb("v_st", [P, d.TPC, d.H, 32])
        lam_in = st.sb("lam_in", [1, 4, d.E])
        lam_pr = st.sb("lam_pr", [1, 2, d.E])
        lam = st.sb("lam", [1, 8])
        row = st.sb("row", [1, P])
        one = st.sb("one", [1, 2])
        qs = st.sb("qs", [P, 2])
        zero = st.sb("zero", [2, d.G * d.S])
        w = NormWork(st, d.TPC)
        ps_t = st.ps("ps_t", [P, d.KT, d.CH])
        ps_q = st.ps("ps_q", [P, NQ, d.CH])
        ps_v = st.ps("ps_v", [P, 2, 2, d.E])

        x_in = [st.sem(f"x_in{c}") for c in range(d.NC)]
        w_in, lam_s = st.sem("w_in"), st.sem("lam_in")
        dv, gp, w_hi_ok, w_lo_ok = st.sem("dv"), st.sem("gp"), st.sem("w_hi_ok"), st.sem("w_lo_ok")
        dots, exps, row_ok, col_ok, qs_ok = (st.sem(n) for n in ("dots", "exps", "row_ok", "col_ok", "qs_ok"))
        xn_ok, xt_ps, hi_ok, lo_ok = (st.sem(n) for n in ("xn_ok", "xt_ps", "hi_ok", "lo_ok"))
        qk_ps, qk_hi_ok, qk_lo_ok = (st.sem(n) for n in ("qk_ps", "qk_hi_ok", "qk_lo_ok"))
        v_ps, v_ok, v_init, qk_out, v_out, z_ok, z_out = (
            st.sem(n) for n in ("v_ps", "v_ok", "v_init", "qk_out", "v_out", "z_ok", "z_out"))
        id_ok = st.sem("id_ok")
        HD2 = d.HD // 2
        scale = float(HD2) ** -0.5

        x_tiles = io["L0_attn_x"].rearrange("b (t p) e -> p (b t) e", p=P)
        with nc.Block() as block:
            @block.sync
            def _(sp):
                for c in range(d.NC):
                    sl = slice(c * d.TPC, (c + 1) * d.TPC)
                    sp.dma_start(X[:, sl, :], x_tiles[:, sl, :]).then_inc(x_in[c], 16)
                    if c == 0:
                        sp.dma_start(w_raw[:], io["L0_attn_W_attn"].rearrange("(k p) n -> p k n", p=P))\
                            .then_inc(w_in, 16)
                        for n, name in enumerate(("q1", "k1", "q2", "k2")):
                            sp.dma_start(lam_in[0:1, n, :],
                                         io["L0_attn_lambda_" + name].rearrange("(a e) -> a e", a=1))\
                                .then_inc(lam_s, 16)
                sp.wait_ge(z_ok, 1)
                sp.dma_start(zero_dram, zero[:]).then_inc(z_out, 16)
                for c in range(d.NC):
                    b, t0 = c * d.CH // d.S, c * d.CH % d.S
                    for j in range(NQ):
                        sp.wait_ge(qk_lo_ok, NQ * c + j + 1)
                        sp.wait_ge(qk_hi_ok, NQ * c + j + 1)
                        for part, src in ((0, qk_hi), (1, qk_lo)):
                            sp.dma_start(q_dram[part, b, P * j:P * (j + 1), t0:t0 + d.CH],
                                         as_f32(src[:, j, :])).then_inc(qk_out, 16)
                    sp.wait_ge(v_ok, 2 * (c + 1))
                    for g in range(d.H // d.G):
                        sp.dma_start(v_dram[b, g, :, t0 // P:t0 // P + d.TPC, :],
                                     v_st[:, :, d.G * g:d.G * (g + 1), :].rearrange("p t h c -> p t (h c)"))\
                            .then_inc(v_out, 16)
                sp.wait_ge(z_out, 16)
                sp.wait_ge(qk_out, 32 * NQ * d.NC)
                sp.wait_ge(v_out, 16 * (d.H // d.G) * d.NC)

            @block.gpsimd
            def _(pool):
                link = chain(pool, gp)
                link(nc.gpsimd.memset(ident[:], 0.0))
                nc.gpsimd.affine_select(out=ident[:], in_=ident[:], compare_op=ALU.not_equal, fill=1.0, base=0,
                                        pattern=[[-1, P]], channel_multiplier=1).then_inc(id_ok, 1)
                nc.gpsimd.memset(zero[:], 0.0).then_inc(z_ok, 1)
                link(nc.gpsimd.memset(v_st[:, :, :, :], 0.0))
                nc.gpsimd.memset(v_st[:, :, :, d.HD:d.HD + 1], 1.0).then_inc(v_init, 1)
                pool.wait_ge(w_in, 16)
                for k in range(d.KT):
                    for part in range(2):
                        src = w_raw[:, k, 0:2 * d.E].rearrange("p (a z h e) -> p z h a e", a=2, z=2, e=HD2)[:, part]
                        dst = w_hi[:, k, part * d.E:(part + 1) * d.E].rearrange("p (h a e) -> p h a e", a=2, e=HD2)
                        link(nc.gpsimd.tensor_copy(dst, src))
                        dlo = w_lo[:, k, part * d.E:(part + 1) * d.E].rearrange("p (h a e) -> p h a e", a=2, e=HD2)
                        for a in range(2):
                            ins = nc.gpsimd.tensor_tensor(dlo[:, :, a], src[:, :, a], as_f32(dst)[:, :, a], ALU.subtract)
                    link(nc.gpsimd.tensor_copy(w_hi[:, k, 2 * d.E:], w_raw[:, k, 2 * d.E:]))
                    ins = nc.gpsimd.tensor_tensor(w_lo[:, k, 2 * d.E:], w_raw[:, k, 2 * d.E:],
                                                  as_f32(w_hi[:, k, 2 * d.E:]), ALU.subtract)
                    link(ins)
                nc.gpsimd.memset(lam[0:1, 7:8], 0.0).then_inc(w_lo_ok, 1)

            @block.vector
            def _(dve):
                link = chain(dve, dv)
                nc.vector.memset(one[:], 1.0)
                link(nc.vector.memset(row[:], 1.0))
                tiles = lambda c: [X[:, d.TPC * c + j, :] for j in range(d.TPC)]
                for c in range(d.NC):
                    dve.wait_ge(x_in[c], 16)
                    norm_stats(nc, dve, link, w, tiles(c), c + 1)
                    if c >= 1:
                        dve.wait_ge(xt_ps, d.KT * c)
                    for j in range(d.TPC):
                        ins = norm_apply(nc, w, j, xn[:, j, :], X[:, d.TPC * c + j, :])
                    ins.then_inc(xn_ok, 1)
                    if c == 0:
                        dve.wait_ge(lam_s, 64)
                        link(nc.vector.tensor_tensor(lam_pr[:], lam_in[:, 0::2, :], lam_in[:, 1::2, :], ALU.mult))
                        nc.vector.reduce_sum(lam[0:1, 0:2], lam_pr[:], AX.X).then_inc(dots, 1)
                        dve.wait_ge(exps, 1)
                        link(nc.vector.tensor_tensor(lam[0:1, 4:5], lam[0:1, 2:3], lam[0:1, 3:4], ALU.subtract))
                        link(nc.vector.tensor_scalar(lam[0:1, 5:6], lam[0:1, 4:5], LAMBDA_INIT, -scale,
                                                     ALU.add, ALU.mult))
                        r = row[0:1, :].rearrange("p (h a e) -> p a h e", a=2, e=HD2)
                        nc.vector.tensor_scalar(r[:, 1], r[:, 1], lam[0:1, 5:6], None, ALU.mult)
                        nc.vector.tensor_scalar(r[:, 0], r[:, 0], scale, None, ALU.mult).then_inc(row_ok, 1)
                        dve.wait_ge(col_ok, 1)
                        nc.vector.tensor_copy(qs[:, 0:1], ps_q[:, 0, 0:1]).then_inc(qs_ok, 1)
                    for k in range(d.KT):
                        dve.wait_ge(hi_ok, d.KT * c + k + 1)
                        nc.vector.tensor_tensor(xt_lo[:, c % 2, k, :], ps_t[:, k, :],
                                                as_f32(xt_hi[:, c % 2, k, :]), ALU.subtract).then_inc(lo_ok, 1)
                    for j in range(NQ):
                        dve.wait_ge(qk_hi_ok, NQ * c + j + 1)
                        if c >= 1:
                            dve.wait_ge(qk_out, 32 * (NQ * (c - 1) + NQ))
                        if j < NQ // 2:
                            nc.vector.scalar_tensor_tensor(
                                out=qk_lo[:, j, :], in0=ps_q[:, j, :], scalar=qs[:, 0:1],
                                in1=as_f32(qk_hi[:, j, :]), op0=ALU.mult, op1=ALU.subtract).then_inc(qk_lo_ok, 1)
                        else:
                            nc.vector.tensor_tensor(qk_lo[:, j, :], ps_q[:, j, :], as_f32(qk_hi[:, j, :]),
                                                    ALU.subtract).then_inc(qk_lo_ok, 1)

            @block.scalar
            def _(act):
                for c in range(d.NC):
                    norm_root(nc, act, w, c + 1)
                    for k in range(d.KT):
                        act.wait_ge(xt_ps, d.KT * c + k + 1)
                        if c >= 2:
                            act.wait_ge(v_ps, 2 * (c - 1))
                        nc.scalar.activation(xt_hi[:, c % 2, k, :], ps_t[:, k, :], ACT.Copy).then_inc(hi_ok, 1)
                    if c == 0:
                        act.wait_ge(dots, 1)
                        nc.scalar.activation(lam[0:1, 2:4], lam[0:1, 0:2], ACT.Exp).then_inc(exps, 1)
                        act.wait_ge(qs_ok, 1)
                    for j in range(NQ):
                        act.wait_ge(qk_ps, NQ * c + j + 1)
                        if c >= 1:
                            act.wait_ge(qk_out, 32 * (NQ * (c - 1) + NQ))
                        nc.scalar.activation(qk_hi[:, j, :], ps_q[:, j, :], ACT.Copy,
                                             scale=qs[:, 0:1] if j < NQ // 2 else 1.0).then_inc(qk_hi_ok, 1)
                    for j in range(2):
                        act.wait_ge(v_ps, 2 * c + j + 1)
                        if c == 0:
                            act.wait_ge(v_init, 1)
                        if c >= 1:
                            act.wait_ge(v_out, 16 * (d.H // d.G) * c)
                        nc.scalar.activation(v_st[:, 2 * j:2 * j + 2, :, 0:d.HD],
                                             ps_v[:, j, :, :].rearrange("p t (h e) -> p t h e", e=d.HD),
                                             ACT.Copy).then_inc(v_ok, 1)

            @block.tensor
            def _(pe):
                pe.wait_ge(id_ok, 1)
                for c in range(d.NC):
                    pe.wait_ge(xn_ok, c + 1)
                    if c >= 1:
                        pe.wait_ge(lo_ok, d.KT * c)
                    for k in range(d.KT):
                        for j in range(d.TPC):
                            ins = nc.tensor.transpose(ps_t[:, k, j * P:(j + 1) * P], xn[:, j, k * P:(k + 1) * P],
                                                      ident[:])
                        ins.then_inc(xt_ps, 1)
                    if c == 0:
                        pe.wait_ge(row_ok, 1)
                        nc.tensor.matmul(ps_q[:, 0, 0:1], row[0:1, :], one[0:1, 0:1], start=True, stop=True)\
                            .then_inc(col_ok, 1)
                        pe.wait_ge(w_lo_ok, 1)
                        pe.wait_ge(qs_ok, 1)
                    pe.wait_ge(lo_ok, d.KT * (c + 1))
                    for j in range(NQ):
                        if c >= 1:
                            pe.wait_ge(qk_lo_ok, NQ * (c - 1) + j + 1)
                        for k in range(d.KT):
                            cols = slice(j * P, (j + 1) * P)
                            ins = mm_split(nc, ps_q[:, j, :], w_hi[:, k, cols], w_lo[:, k, cols],
                                           xt_hi[:, c % 2, k, :], xt_lo[:, c % 2, k, :], k == 0, k == d.KT - 1)
                        ins.then_inc(qk_ps, 1)
                    for j in range(2):
                        if c >= 1:
                            pe.wait_ge(v_ok, 2 * (c - 1) + j + 1)
                        for i in range(2):
                            t = slice((2 * j + i) * P, (2 * j + i + 1) * P)
                            for k in range(d.KT):
                                ins = mm_split(nc, ps_v[:, j, i, :], xt_hi[:, c % 2, k, t], xt_lo[:, c % 2, k, t],
                                               w_hi[:, k, 2 * d.E:], w_lo[:, k, 2 * d.E:], k == 0, k == d.KT - 1)
                        ins.then_inc(v_ps, 1)
        st.clear()


def stage_attention(nc, d, io, keep, scratch):
    with ExitStack() as ctx:
        st = Store(nc, ctx, "att")
        AO, ident = keep["AO"], keep["ident"]
        q_dram, v_dram, zero_dram = scratch["qk"], scratch["v"], scratch["zero"]
        NS = d.S // P
        NB = d.S // d.CH
        HD, G = d.HD, d.G
        ROWS = 3 * HD + 2
        RING = 3
        LEAD = 6
        qst = [st.sb(f"qst{i}", [P, G, d.S], F32R) for i in range(RING)]
        kst = [st.sb(f"kst{i}", [P, G, d.S], F32R) for i in range(RING)]
        vst = [st.sb(f"vst{i}", [P, NS, G * 32]) for i in range(RING)]
        prob = st.sb("prob", [P, RING, G, d.S])
        mx = st.sb("mx", [P, 2, G * NS, NB])
        nm = st.sb("nm", [P, G * NS])
        nmt = st.sb("nmt", [P, G * NS])
        nm_hi = st.sb("nm_hi", [P, 2, G * NS], F32R)
        nm_lo = st.sb("nm_lo", [P, 2, G * NS], F32R)
        osb = st.sb("osb", [P, NB, d.CH])
        rs = st.sb("rs", [P, NB, d.TPC * G])
        ps_s = st.ps("ps_s", [P, 2, d.S])
        ps_m = st.ps("ps_m", [P, 2, d.CH])
        ps_o = st.ps("ps_o", [P, NB, d.CH])
        pad_ok = st.sem("pad_ok")
        load = [st.sem(f"load{i}") for i in range(RING)]
        nm_in = [st.sem(f"nm_in{i}") for i in range(2)]
        m_ps, m_rd, nm_ok = st.sem("m_ps"), st.sem("m_rd"), st.sem("nm_ok")
        sc_ps, exp_ok, pv_ok = st.sem("sc_ps"), st.sem("exp_ok"), st.sem("pv_ok")
        o_rd, dv = st.sem("o_rd"), st.sem("dv")
        UPG = NS * G
        MPG = G * NS * NB
        MPU = MPG // UPG
        UN = UPG * d.NG
        LOADS = 8
        NMD = 8

        side = {u: [] for u in range(-1, UN + 2 * G + 3)}
        for g in range(d.NG):
            for m in range(MPG):
                side[max(-1, UPG * (g - 1) - LEAD + m // MPU)].append(("max", g, m))
            for t in range(NB):
                side[UPG * (g + 1) + G + 2 + t].append(("out", g, t))
        items = [(u, x) for u in side for x in side[u]]

        def ready(kind, g, m):
            return [x for _, x in items].index((kind, g, m)) + 1

        with nc.Block() as block:
            @block.sync
            def _(sp):
                def load_group(g):
                    b, i = g // (d.NG // d.B), g % RING
                    h0 = g % (d.NG // d.B) * G
                    if g < RING:
                        sp.wait_ge(pad_ok, i + 1)
                    else:
                        sp.wait_ge(pv_ok, NS * NB * (g - RING + 1))
                    for base, dst, parts in ((0, qst[i], (0, 1, 0)), (d.E, kst[i], (0, 0, 1))):
                        for n, part in enumerate(parts):
                            src = q_dram[part, b, base + h0 * HD:base + (h0 + G) * HD, :]
                            sp.dma_start(as_f32(dst[n * HD:(n + 1) * HD, :, :]),
                                         src.rearrange("(h e) t -> e h t", e=HD)).then_inc(load[i], 16)
                    sp.dma_start(as_f32(qst[i][3 * HD:ROWS, :, :]), zero_dram.rearrange("r (h t) -> r h t", h=G))\
                        .then_inc(load[i], 16)
                    sp.dma_start(vst[i][:], v_dram[b, g % (d.NG // d.B)]).then_inc(load[i], 16)

                for g in range(RING):
                    load_group(g)
                for g in range(d.NG):
                    sp.wait_ge(nm_ok, g + 1)
                    for r, src in ((3 * HD, nm_hi), (3 * HD + 1, nm_lo)):
                        for q in range(4):
                            dst = qst[g % RING][r:r + 1, :, :].rearrange("p h (t q j) -> p (h t) q j", q=4, j=32)
                            sp.dma_start(as_f32(dst[:, :, q]), as_f32(src[32 * q:32 * q + 32, g % 2, :]))\
                                .then_inc(nm_in[g % 2], 16)
                    if g >= 1 and g + 2 < d.NG:
                        load_group(g + 2)

            @block.gpsimd
            def _(pool):
                for i in range(RING):
                    nc.gpsimd.memset(as_f32(qst[i][64:P, :, :]), 0.0)
                    nc.gpsimd.memset(as_f32(kst[i][64:P, :, :]), 0.0)
                    nc.gpsimd.memset(as_f32(qst[i][32:64, :, :]), 0.0)
                    nc.gpsimd.memset(as_f32(kst[i][32:64, :, :]), 1.0).then_inc(pad_ok, 1)

            @block.tensor
            def _(pe):
                done = [0]

                def side_unit(kind, g, m):
                    n = done[0]
                    done[0] += 1
                    if n >= 2:
                        pe.wait_ge(m_rd, n - 1)
                    if kind == "max":
                        h, t, half = m // (NS * NB), m // NB % NS, m % NB
                        if m == 0:
                            pe.wait_ge(load[g % RING], 16 * LOADS * (g // RING + 1))
                        nc.tensor.matmul(ps_m[:, n % 2, :], qst[g % RING][:, h, t * P:(t + 1) * P],
                                         kst[g % RING][:, h, half * d.CH:(half + 1) * d.CH],
                                         start=True, stop=True).then_inc(m_ps, 1)
                    else:
                        pe.wait_ge(o_rd, NB * g + m + 1)
                        for j in range(d.TPC):
                            ins = nc.tensor.transpose(ps_m[:, n % 2, j * P:(j + 1) * P],
                                                      osb[:, m, j * P:(j + 1) * P], ident[:])
                        ins.then_inc(m_ps, 1)

                def score_unit(u):
                    g, s, h = u // UPG, u // G % NS, u % G
                    if u % UPG == 0:
                        pe.wait_ge(nm_in[g % 2], 16 * NMD * (g // 2 + 1))
                    if u >= 2:
                        pe.wait_ge(exp_ok, u - 1)
                    for t in range(NB):
                        ins = nc.tensor.matmul(ps_s[:, u % 2, t * d.CH:(t + 1) * d.CH],
                                               kst[g % RING][:, h, s * P:(s + 1) * P],
                                               qst[g % RING][:, h, t * d.CH:(t + 1) * d.CH], start=True, stop=True)
                    ins.then_inc(sc_ps, 1)

                def value_unit(n, t):
                    g, s = n // NS, n % NS
                    pe.wait_ge(exp_ok, G * (n + 1))
                    if s == 0 and g >= 1:
                        pe.wait_ge(o_rd, NB * (g - 1) + t + 1)
                    for h in range(G):
                        ins = nc.tensor.matmul(ps_o[32 * h:32 * h + 32, t, :],
                                               vst[g % RING][:, s, 32 * h:32 * h + 32],
                                               prob[:, n % RING, h, t * d.CH:(t + 1) * d.CH],
                                               start=s == 0, stop=s == NS - 1)
                    ins.then_inc(pv_ok, 1)

                for u in side:
                    todo = side[u]
                    if u >= 0:
                        for x in todo[:1]:
                            side_unit(*x)
                        if u < UN:
                            score_unit(u)
                        todo = todo[1:]
                    for x in todo:
                        side_unit(*x)
                    if u > G and u % G in (1, 3) and u // G - 1 < UN // G:
                        value_unit(u // G - 1, u % G // 2)

            @block.scalar
            def _(act):
                for u in range(UN + G + 3):
                    s, h = u // G, u % G
                    if u < UN:
                        act.wait_ge(sc_ps, u + 1)
                        if h == 0 and s >= RING:
                            act.wait_ge(pv_ok, NB * (s - RING + 1))
                        nc.scalar.activation(prob[:, s % RING, h, :], ps_s[:, u % 2, :], ACT.Exp).then_inc(exp_ok, 1)
                    if u > UPG and u % UPG in (2, 4):
                        g, t = u // UPG - 1, u % UPG // 2 - 1
                        act.wait_ge(pv_ok, NB * (NS * (g + 1) - 1) + t + 1)
                        if g >= 1:
                            act.wait_ge(m_rd, ready("out", g - 1, t))
                        nc.scalar.activation(osb[:, t, :], ps_o[:, t, :], ACT.Copy).then_inc(o_rd, 1)

            @block.vector
            def _(dve):
                link = chain(dve, dv)

                def finish_max(g):
                    link(nc.vector.tensor_reduce(nm[:], mx[:, g % 2], AX.X, ALU.max, negate=True))
                    link(nc.vector.transpose(nmt[:], nm[:]))
                    if g >= 2:
                        dve.wait_ge(nm_in[g % 2], 16 * NMD * (g // 2))
                    link(nc.vector.tensor_copy(nm_hi[:, g % 2, :], nmt[:]))
                    nc.vector.tensor_tensor(nm_lo[:, g % 2, :], nmt[:], as_f32(nm_hi[:, g % 2, :]),
                                            ALU.subtract).then_inc(nm_ok, 1)

                for n, (_, (kind, g, m)) in enumerate(items):
                    dve.wait_ge(m_ps, n + 1)
                    if kind == "max":
                        nc.vector.reduce_max(mx[:, g % 2, m // NB, m % NB:m % NB + 1], ps_m[:, n % 2, :], AX.X)\
                            .then_inc(m_rd, 1)
                        if m == MPG - 1:
                            dve.wait_ge(m_rd, n + 1)
                            finish_max(g)
                    else:
                        b, h0, t0 = g // (d.NG // d.B), g % (d.NG // d.B) * G, m * d.TPC
                        o = ps_m[:, n % 2, :].rearrange("p (j h e) -> p j h e", h=G, e=32)
                        r = rs[:, m, :].rearrange("p (j h) -> p j h", h=G)
                        link(nc.vector.reciprocal(r, o[:, :, :, HD]))
                        link(nc.vector.tensor_scalar(r, r, 1.0 - LAMBDA_INIT, None, ALU.mult))
                        dst = AO[:, b * NS + t0:b * NS + t0 + d.TPC, h0 * HD:(h0 + G) * HD]
                        nc.vector.tensor_tensor(dst.rearrange("p j (h e) -> p j h e", e=HD), o[:, :, :, 0:HD],
                                                r.unsqueeze(3).to_broadcast([P, d.TPC, G, HD]),
                                                ALU.mult).then_inc(m_rd, 1)


def stage_mlp(nc, d, io, keep):
    with ExitStack() as ctx:
        st = Store(nc, ctx, "mlp")
        X, AO, ident = keep["X"], keep["AO"], keep["ident"]
        KEEP = max(1, int(d.N * (1.0 - 0.9)))
        LOW = KEEP - 8
        NN = d.N // P
        NH = d.N // d.CH
        ROUNDS = 4
        SPREAD0, SLOPE = 1.3095, 173.0
        XN = st.sb("xn", [P, d.NT, d.E])
        Z = st.sb("z", [P, d.NT, d.N])
        wp_raw = st.sb("wp_raw", [P, d.KT, d.E])
        wp_hi = st.sb("wp_hi", [P, d.KT, d.E], F32R)
        wp_lo = st.sb("wp_lo", [P, d.KT, d.E], F32R)
        ws_raw = st.sb("ws_raw", [P, NN, d.E])
        wo_raw = st.sb("wo_raw", [P, d.KT, d.N])
        ws_t = st.sb("ws_t", [P, d.KT, d.N], F32R)
        wo_t = st.sb("wo_t", [P, NN, d.E], F32R)
        bs = st.sb("bs", [P, d.N])
        vecs = st.sb("vecs", [P, 3, d.E])
        ones = st.sb("ones", [P, P])
        abs_sum = st.sb("abs_sum", [P, 2])
        sc = st.sb("sc", [P, 2])
        inv = st.sb("inv", [P, 2])
        xt_hi = st.sb("xt_hi", [P, d.KT, d.CH], F32R)
        xt_lo = st.sb("xt_lo", [P, d.KT, d.CH], F32R)
        zst = st.sb("zst", [P, d.NT, NH, 6])
        zmv = st.sb("zmv", [P, d.NT, 2])
        zsd = st.sb("zsd", [P, d.NT])
        lev = st.sb("lev", [P, d.NT])
        nlev = st.sb("nlev", [P, d.NT])
        sgn = st.sb("sgn", [P, d.NT])
        cnt = st.sb("cnt", [P, d.NT])
        lo, hi, clo, chi = (st.sb(n, [P, d.NT]) for n in ("lo", "hi", "clo", "chi"))
        t1, t2, t3 = (st.sb(n, [P, d.NT]) for n in ("t1", "t2", "t3"))
        msk = st.sb("msk", [P, d.NT])
        msk2 = st.sb("msk2", [P, d.NT])
        junk = st.sb("junk", [P, 2, d.N], mybir.dt.bfloat16)
        below = st.sb("below", [P, 2, d.N])
        top = st.sb("top", [P, d.NT, 8])
        pick = st.sb("pick", [P, d.NT, 8])
        iota8 = st.sb("iota8", [P, 8])
        iota_i = st.sb("iota_i", [P, 8], mybir.dt.int32)
        thr = st.sb("thr", [P, d.NT])
        flag = st.sb("flag", [P, 2])
        flag_i = st.sb("flag_i", [P, 1], mybir.dt.int32)
        ht_hi = st.sb("ht_hi", [P, d.N], F32R)
        ht_lo = st.sb("ht_lo", [P, d.N], F32R)
        y = st.sb("y", [P, d.TPC, d.E])
        w1, w2 = NormWork(st, d.TPC, "1"), NormWork(st, d.TPC, "2")
        ps_t = st.ps("ps_t", [P, d.KT, d.CH])
        ps_p = st.ps("ps_p", [P, 2, 2, d.E])
        ps_z = st.ps("ps_z", [P, 2, d.N])

        w_in = [st.sem(f"w_in{i}") for i in range(4)]
        dv, gp, on = st.sem("dv"), st.sem("gp"), st.sem("on")
        wp_ok, tern_ok, tern_ps, tern_rd = (st.sem(n) for n in ("wp_ok", "tern_ok", "tern_ps", "tern_rd"))
        sum_ok, sum_ps = st.sem("sum_ok"), st.sem("sum_ps")
        at_ps, hi_ok, lo_ok = st.sem("at_ps"), st.sem("hi_ok"), st.sem("lo_ok")
        pr_ps, pr_rd, xn_ok = st.sem("pr_ps"), st.sem("pr_rd"), st.sem("xn_ok")
        z_ps, z_ok = st.sem("z_ps"), st.sem("z_ok")
        zvar, zroot, lev_ok, cnt_ok = (st.sem(n) for n in ("zvar", "zroot", "lev_ok", "cnt_ok"))
        flag_ok, any_ok = st.sem("flag_ok"), st.sem("any_ok")
        h_ok, h_ps, h_hi, h_lo, o_ps, o_rd = (st.sem(n) for n in ("h_ok", "h_ps", "h_hi", "h_lo", "o_ps", "o_rd"))
        xb_ok, y_ok, x_ok = st.sem("xb_ok"), st.sem("y_ok"), st.sem("x_ok")

        with nc.Block() as block:
            @block.sync
            def _(sp):
                sp.dma_start(wp_raw[:], io["L0_attn_W_proj"].rearrange("(k p) n -> p k n", p=P)).then_inc(w_in[0], 16)
                sp.dma_start(ws_raw[:], io["L0_ffn_W_syn"].rearrange("(a p) n -> p a n", p=P)).then_inc(w_in[1], 16)
                sp.dma_start(wo_raw[:], io["L0_ffn_W_out"].rearrange("(a p) n -> p a n", p=P)).then_inc(w_in[1], 16)
                sp.dma_start(bs[:], io["L0_ffn_b_syn"].rearrange("(a n) -> a n", a=1).to_broadcast([P, d.N]))\
                    .then_inc(w_in[2], 16)
                for i, name in enumerate(("b_out", "gamma", "beta")):
                    src = io["L0_ffn_" + name].rearrange("(a n) -> a n", a=1)
                    sp.dma_start(vecs[:, i, :], src.to_broadcast([P, d.E])).then_inc(w_in[3], 16)

            @block.gpsimd
            def _(pool):
                link = chain(pool, gp)
                nc.gpsimd.memset(ones[:], 1.0).then_inc(on, 1)
                nc.gpsimd.iota(iota_i[:], pattern=[[1, 8]], base=0, channel_multiplier=0).then_inc(on, 1)
                pool.wait_ge(w_in[0], 16)
                link(nc.gpsimd.tensor_copy(wp_hi[:], wp_raw[:]))
                nc.gpsimd.tensor_tensor(wp_lo[:], wp_raw[:], as_f32(wp_hi[:]), ALU.subtract).then_inc(wp_ok, 1)
                pool.wait_ge(flag_ok, 1)
                nc.gpsimd.partition_all_reduce(flag[:, 1:2], flag[:, 0:1], P, bass.bass_isa.ReduceOp.max)\
                    .then_inc(any_ok, 1)
                pool.wait_ge(w_in[3], 48)
                for c in range(d.NC):
                    pool.wait_ge(z_ps, d.NT)
                    for j in range(d.TPC):
                        t = d.TPC * c + j
                        ins = nc.gpsimd.tensor_tensor(XN[:, t, :], XN[:, t, :], vecs[:, 0, :], ALU.add)
                    ins.then_inc(xb_ok, 1)
                for c in range(d.NC):
                    pool.wait_ge(y_ok, c + 1)
                    for j in range(d.TPC):
                        ins = nc.gpsimd.tensor_tensor(y[:, j, :], y[:, j, :], vecs[:, 1, :], ALU.mult)
                    link(ins)
                    for j in range(d.TPC):
                        ins = nc.gpsimd.tensor_tensor(y[:, j, :], y[:, j, :], vecs[:, 2, :], ALU.add)
                    link(ins)
                    for j in range(d.TPC):
                        t = d.TPC * c + j
                        ins = nc.gpsimd.tensor_tensor(X[:, t, :], X[:, t, :], y[:, j, :], ALU.add)
                    ins.then_inc(x_ok, 1)

            @block.vector
            def _(dve):
                link = chain(dve, dv)
                dve.wait_ge(w_in[1], 32)
                nc.vector.tensor_reduce(abs_sum[:, 0:1], ws_raw[:].rearrange("p a n -> p (a n)"), AX.X, ALU.add,
                                        apply_absolute_value=True)
                nc.vector.tensor_reduce(abs_sum[:, 1:2], wo_raw[:].rearrange("p a n -> p (a n)"), AX.X, ALU.add,
                                        apply_absolute_value=True).then_inc(sum_ok, 1)
                dve.wait_ge(sum_ps, 1)
                link(nc.vector.tensor_scalar(sc[:], ps_p[:, 0, 0, 0:2], 1.0 / (d.N * d.E), None, ALU.mult))
                link(nc.vector.tensor_scalar(inv[:], sc[:], 1e-8, None, ALU.add))
                link(nc.vector.reciprocal(inv[:], inv[:]))
                for i, raw in enumerate((ws_raw, wo_raw)):
                    flat = raw[:].rearrange("p a n -> p (a n)")
                    a = Z[:, 0:2, :].rearrange("p a n -> p (a n)")
                    b = Z[:, 2:4, :].rearrange("p a n -> p (a n)")
                    nc.vector.tensor_scalar(a, flat, inv[:, i:i + 1], 0.5, ALU.mult, ALU.is_gt)
                    link(nc.vector.tensor_scalar(b, flat, inv[:, i:i + 1], -0.5, ALU.mult, ALU.is_lt))
                    link(nc.vector.tensor_tensor(flat, a, b, ALU.subtract))
                nc.vector.memset(flag[:, 0:1], 0.0).then_inc(tern_ok, 1)
                dve.wait_ge(w_in[2], 16)
                for c in range(d.NC):
                    for k in range(d.KT):
                        dve.wait_ge(hi_ok, 2 * d.KT * c + k + 1)
                        nc.vector.tensor_tensor(xt_lo[:, k, :], ps_t[:, k, :], as_f32(xt_hi[:, k, :]),
                                                ALU.subtract).then_inc(lo_ok, 1)
                    for j in range(2):
                        dve.wait_ge(pr_ps, 2 * c + j + 1)
                        t = d.TPC * c + 2 * j
                        ins = nc.vector.tensor_tensor(X[:, t:t + 2, :], X[:, t:t + 2, :], ps_p[:, j, :, :], ALU.add)
                        ins.then_inc(pr_rd, 1)
                    dve.wait_ge(pr_rd, 2 * (c + 1))
                    norm_stats(nc, dve, link, w1, [X[:, d.TPC * c + j, :] for j in range(d.TPC)], c + 1)
                    for j in range(d.TPC):
                        t = d.TPC * c + j
                        ins = norm_apply(nc, w1, j, XN[:, t, :], X[:, t, :])
                    ins.then_inc(xn_ok, 1)
                    for k in range(d.KT):
                        dve.wait_ge(hi_ok, 2 * d.KT * c + d.KT + k + 1)
                        nc.vector.tensor_tensor(xt_lo[:, k, :], ps_t[:, k, :], as_f32(xt_hi[:, k, :]),
                                                ALU.subtract).then_inc(lo_ok, 1)
                    for j in range(d.TPC):
                        t = d.TPC * c + j
                        dve.wait_ge(z_ps, t + 1)
                        nc.vector.scalar_tensor_tensor(out=Z[:, t, :], in0=ps_z[:, t % 2, :], scalar=sc[:, 0:1],
                                                       in1=bs[:], op0=ALU.mult, op1=ALU.add).then_inc(z_ok, 1)
                        dve.wait_ge(z_ok, t + 1)
                        for n in range(NH):
                            ins = nc.vector.bn_stats(zst[:, t, n, :], Z[:, t, n * d.CH:(n + 1) * d.CH])
                link(ins)
                for t in range(d.NT):
                    ins = nc.vector.bn_aggr(zmv[:, t, :], zst[:, t].rearrange("p a b -> p (a b)"))
                ins.then_inc(zvar, 1)
                dve.wait_ge(zroot, 1)
                dve.wait_ge(on, 2)
                nc.vector.tensor_copy(iota8[:], iota_i[:])
                link(nc.vector.scalar_tensor_tensor(out=lev[:], in0=zsd[:], scalar=SPREAD0, in1=zmv[:, :, 0],
                                                    op0=ALU.mult, op1=ALU.add))
                nc.vector.tensor_scalar(nlev[:], lev[:], -1.0, None, ALU.mult).then_inc(lev_ok, 1)
                link(nc.vector.scalar_tensor_tensor(out=lo[:], in0=zsd[:], scalar=-0.6, in1=lev[:],
                                                    op0=ALU.mult, op1=ALU.add))
                link(nc.vector.scalar_tensor_tensor(out=hi[:], in0=zsd[:], scalar=0.6, in1=lev[:],
                                                    op0=ALU.mult, op1=ALU.add))
                nc.vector.memset(clo[:], 122.0)
                link(nc.vector.memset(chi[:], -68.0))
                AIM = KEEP - 4.0
                for r in range(ROUNDS):
                    dve.wait_ge(cnt_ok, d.NT * (r + 1))
                    link(nc.vector.tensor_scalar(cnt[:], sgn[:], 0.5, d.N / 2 - AIM, ALU.mult, ALU.add))
                    link(nc.vector.tensor_tensor(t1[:], cnt[:], cnt[:], ALU.mult))
                    link(nc.vector.tensor_scalar(msk2[:], t1[:], 16.5, None, ALU.is_gt))
                    if r == ROUNDS - 1:
                        break
                    m = msk[:].bitcast(U32)
                    link(nc.vector.tensor_scalar(msk[:], cnt[:], 0.0, None, ALU.is_gt))
                    nc.vector.copy_predicated(lo[:], m, lev[:])
                    link(nc.vector.copy_predicated(clo[:], m, cnt[:]))
                    link(nc.vector.tensor_scalar(msk[:], cnt[:], 0.0, None, ALU.is_le))
                    nc.vector.copy_predicated(hi[:], m, lev[:])
                    link(nc.vector.copy_predicated(chi[:], m, cnt[:]))
                    if r == 0:
                        link(nc.vector.scalar_tensor_tensor(out=t1[:], in0=cnt[:], scalar=1.0 / SLOPE, in1=zsd[:],
                                                            op0=ALU.mult, op1=ALU.mult))
                        link(nc.vector.tensor_tensor(t1[:], t1[:], lev[:], ALU.add))
                    else:
                        link(nc.vector.tensor_tensor(t1[:], clo[:], chi[:], ALU.subtract))
                        link(nc.vector.reciprocal(t1[:], t1[:]))
                        link(nc.vector.tensor_tensor(t2[:], hi[:], lo[:], ALU.subtract))
                        link(nc.vector.tensor_tensor(t2[:], t2[:], clo[:], ALU.mult))
                        link(nc.vector.tensor_tensor(t2[:], t2[:], t1[:], ALU.mult))
                        link(nc.vector.tensor_tensor(t1[:], t2[:], lo[:], ALU.add))
                    link(nc.vector.copy_predicated(lev[:], msk2[:].bitcast(U32), t1[:]))
                    nc.vector.tensor_scalar(nlev[:], lev[:], -1.0, None, ALU.mult).then_inc(lev_ok, 1)
                for t in range(d.NT):
                    ins = nc.vector.scalar_tensor_tensor(out=below[:, t % 2, :], in0=Z[:, t, :],
                                                         scalar=lev[:, t:t + 1], in1=Z[:, t, :],
                                                         op0=ALU.is_le, op1=ALU.mult)
                    link(ins)
                    ins = nc.vector.max(top[:, t, :], below[:, t % 2, :])
                link(ins)
                link(nc.vector.tensor_scalar(t1[:], cnt[:], -1.0, 3.0, ALU.mult, ALU.add))
                link(nc.vector.tensor_tensor(pick[:], t1[:].unsqueeze(2).to_broadcast([P, d.NT, 8]),
                                             iota8[:].unsqueeze(1).to_broadcast([P, d.NT, 8]), ALU.is_equal))
                link(nc.vector.tensor_tensor(pick[:], pick[:], top[:], ALU.mult))
                link(nc.vector.tensor_reduce(thr[:], pick[:], AX.X, ALU.add))
                link(nc.vector.tensor_scalar(t2[:], t1[:], -1.0, None, ALU.is_equal))
                link(nc.vector.tensor_tensor(t2[:], t2[:], lev[:], ALU.mult))
                link(nc.vector.tensor_tensor(thr[:], thr[:], t2[:], ALU.add))
                link(nc.vector.tensor_scalar(t2[:], lev[:], 0.0, None, ALU.is_le))
                link(nc.vector.tensor_tensor(t3[:], top[:, :, 0], lev[:], ALU.is_equal))
                link(nc.vector.tensor_tensor(t2[:], t2[:], t3[:], ALU.max))
                link(nc.vector.tensor_tensor(t2[:], t2[:], msk2[:], ALU.max))
                nc.vector.reduce_max(flag[:, 0:1], t2[:], AX.X).then_inc(flag_ok, 1)
                dve.wait_ge(any_ok, 1)
                link(nc.vector.tensor_copy(flag_i[:], flag[:, 1:2]))
                some = dve.value_load(flag_i[0:1, 0:1], min_val=0, max_val=1)
                with dve.If(some):
                    general_threshold(nc, dve, d, Z, below, top, thr, KEEP)
                dve.drain()
                dve.wait_ge(xb_ok, d.NC)
                for t in range(d.NT):
                    if t == 0:
                        link(nc.vector.tensor_scalar(thr[:], thr[:], 0.0, None, ALU.max))
                    if t >= 2:
                        dve.wait_ge(h_ps, t - 1)
                    nc.vector.scalar_tensor_tensor(out=below[:, t % 2, :], in0=Z[:, t, :], scalar=thr[:, t:t + 1],
                                                   in1=Z[:, t, :], op0=ALU.is_ge, op1=ALU.mult).then_inc(h_ok, 1)
                    dve.wait_ge(h_hi, t + 1)
                    nc.vector.tensor_tensor(ht_lo[:], ps_z[:, t % 2, :], as_f32(ht_hi[:]),
                                            ALU.subtract).then_inc(h_lo, 1)
                    dve.wait_ge(o_ps, t + 1)
                    nc.vector.scalar_tensor_tensor(out=XN[:, t, :], in0=ps_p[:, t % 2, 0, :], scalar=sc[:, 1:2],
                                                   in1=XN[:, t, :], op0=ALU.mult, op1=ALU.add).then_inc(o_rd, 1)
                    if t % d.TPC == d.TPC - 1:
                        c = t // d.TPC
                        dve.wait_ge(o_rd, t + 1)
                        norm_stats(nc, dve, link, w2, [XN[:, d.TPC * c + j, :] for j in range(d.TPC)], c + 1)
                        if c >= 1:
                            dve.wait_ge(x_ok, c)
                        for j in range(d.TPC):
                            ins = norm_apply(nc, w2, j, y[:, j, :], XN[:, d.TPC * c + j, :])
                        ins.then_inc(y_ok, 1)

            @block.scalar
            def _(act):
                for i, dst in enumerate((ws_t, wo_t)):
                    for k in range(2):
                        act.wait_ge(tern_ps, 2 * i + k + 1)
                        flat = dst[:].rearrange("p a n -> p (a n)")[:, k * d.N:(k + 1) * d.N]
                        nc.scalar.activation(flat, ps_z[:, k, :], ACT.Copy).then_inc(tern_rd, 1)
                for c in range(d.NC):
                    for half in range(2):
                        if half:
                            norm_root(nc, act, w1, c + 1)
                        for k in range(d.KT):
                            n = 2 * d.KT * c + d.KT * half + k
                            act.wait_ge(at_ps, n + 1)
                            if half:
                                act.wait_ge(pr_ps, 2 * (c + 1))
                            elif c:
                                act.wait_ge(z_ps, d.TPC * c)
                            nc.scalar.activation(xt_hi[:, k, :], ps_t[:, k, :], ACT.Copy).then_inc(hi_ok, 1)
                act.wait_ge(zvar, 1)
                nc.scalar.activation(zsd[:], zmv[:, :, 1], ACT.Sqrt).then_inc(zroot, 1)
                for r in range(ROUNDS):
                    act.wait_ge(lev_ok, r + 1)
                    for t in range(d.NT):
                        n = d.NT * r + t
                        if n >= 2:
                            act.wait_ge(cnt_ok, n - 1)
                        nc.scalar.activation(junk[:, n % 2, :], Z[:, t, :], ACT.Sign, bias=nlev[:, t:t + 1],
                                             accum_out=sgn[:, t:t + 1]).then_inc(cnt_ok, 1)
                for t in range(d.NT):
                    act.wait_ge(h_ps, t + 1)
                    if t >= 1:
                        act.wait_ge(o_ps, t)
                    nc.scalar.activation(ht_hi[:], ps_z[:, t % 2, :], ACT.Copy).then_inc(h_hi, 1)
                    if t % d.TPC == d.TPC - 1:
                        norm_root(nc, act, w2, t // d.TPC + 1)

            @block.tensor
            def _(pe):
                pe.wait_ge(on, 1)
                pe.wait_ge(sum_ok, 1)
                nc.tensor.matmul(ps_p[:, 0, 0, 0:2], ones[:], abs_sum[:], start=True, stop=True).then_inc(sum_ps, 1)
                pe.wait_ge(tern_ok, 1)
                for k in range(d.KT):
                    for a in range(NN):
                        ins = nc.tensor.transpose(ps_z[:, k, a * P:(a + 1) * P], ws_raw[:, a, k * P:(k + 1) * P],
                                                  ident[:])
                    ins.then_inc(tern_ps, 1)
                for k in range(2):
                    pe.wait_ge(tern_rd, k + 1)
                    for a in range(NN // 2):
                        for e in range(d.KT):
                            n = k * (NN // 2) + a
                            ins = nc.tensor.transpose(ps_z[:, k, a * d.E + e * P:a * d.E + (e + 1) * P],
                                                      wo_raw[:, e, n * P:(n + 1) * P], ident[:])
                    ins.then_inc(tern_ps, 1)
                pe.wait_ge(tern_rd, 4)
                pe.wait_ge(wp_ok, 1)
                for c in range(d.NC):
                    for half, src in ((0, AO), (1, XN)):
                        if half:
                            pe.wait_ge(xn_ok, c + 1)
                        n = 2 * d.KT * c + d.KT * half
                        if n:
                            pe.wait_ge(lo_ok, n)
                        for k in range(d.KT):
                            for j in range(d.TPC):
                                ins = nc.tensor.transpose(ps_t[:, k, j * P:(j + 1) * P],
                                                          src[:, d.TPC * c + j, k * P:(k + 1) * P], ident[:])
                            ins.then_inc(at_ps, 1)
                        pe.wait_ge(lo_ok, n + d.KT)
                        if half == 0:
                            for j in range(2):
                                if c:
                                    pe.wait_ge(pr_rd, 2 * (c - 1) + j + 1)
                                for i in range(2):
                                    t = slice((2 * j + i) * P, (2 * j + i + 1) * P)
                                    for k in range(d.KT):
                                        ins = mm_split(nc, ps_p[:, j, i, :], xt_hi[:, k, t], xt_lo[:, k, t],
                                                       wp_hi[:, k, :], wp_lo[:, k, :], k == 0, k == d.KT - 1)
                                ins.then_inc(pr_ps, 1)
                        else:
                            for j in range(d.TPC):
                                t = d.TPC * c + j
                                if t >= 2:
                                    pe.wait_ge(z_ok, t - 1)
                                for n in range(NH):
                                    cols = slice(n * d.CH, (n + 1) * d.CH)
                                    for k in range(d.KT):
                                        ins = mm_split(nc, ps_z[:, t % 2, cols], xt_hi[:, k, j * P:(j + 1) * P],
                                                       xt_lo[:, k, j * P:(j + 1) * P], ws_t[:, k, cols], None,
                                                       k == 0, k == d.KT - 1)
                                ins.then_inc(z_ps, 1)
                pe.wait_ge(z_ok, d.NT)
                pe.wait_ge(pr_rd, 2 * d.NC)
                for t in range(d.NT):
                    pe.wait_ge(h_ok, t + 1)
                    if t >= 2:
                        pe.wait_ge(h_lo, t - 1)
                    for n in range(NN):
                        ins = nc.tensor.transpose(ps_z[:, t % 2, n * P:(n + 1) * P],
                                                  below[:, t % 2, n * P:(n + 1) * P], ident[:])
                    ins.then_inc(h_ps, 1)
                    pe.wait_ge(h_lo, t + 1)
                    if t >= 2:
                        pe.wait_ge(o_rd, t - 1)
                    for n in range(NN):
                        ins = mm_split(nc, ps_p[:, t % 2, 0, :], ht_hi[:, n * P:(n + 1) * P],
                                       ht_lo[:, n * P:(n + 1) * P], wo_t[:, n, :], None, n == 0, n == NN - 1)
                    ins.then_inc(o_ps, 1)


def general_threshold(nc, dve, d, Z, work, top, thr, keep):
    with dve.Fori(0, d.NT) as t:
        dve.drain()
        nc.vector.tensor_copy(work[:, 0, :], Z[:, bass.ds(t, 1), :].rearrange("p a n -> p (a n)"))
        for r in range((keep - 1) // 8):
            dve.drain()
            nc.vector.max(top[:, 0, :], work[:, r % 2, :])
            dve.drain()
            nc.vector.match_replace(out=work[:, (r + 1) % 2, :], in_to_replace=top[:, 0, :],
                                    in_values=work[:, r % 2, :], imm_value=-3.0e38)
        r = (keep - 1) // 8
        dve.drain()
        nc.vector.max(top[:, 0, :], work[:, r % 2, :])
        dve.drain()
        nc.vector.tensor_copy(thr[:, bass.ds(t, 1)], top[:, 0, (keep - 1) % 8:(keep - 1) % 8 + 1])


def stage_keys(nc, d, io, keep):
    with ExitStack() as ctx:
        st = Store(nc, ctx, "key")
        X, ident = keep["X"], keep["ident"]
        xt_hi, xt_lo, M, ksum, wq_raw = (keep[n] for n in ("xt_hi", "xt_lo", "M", "ksum", "wq_raw"))
        NI = d.INNER // d.CH
        CPB = d.CH // P
        TPB = d.S // P
        HW = P // 2
        UN = NI * d.B
        NP = 2
        xn = st.sb("xn", [P, d.TPC, d.E])
        xk_hi = st.sb("xk_hi", [P, d.NT, d.E], F32R)
        xk_lo = st.sb("xk_lo", [P, d.NT, d.E], F32R)
        raw = wq_raw[:, 2:4]
        w_hi = st.sb("w_hi", [P, 4, 2 * d.CH], F32R)
        w_lo = st.sb("w_lo", [P, 4, 2 * d.CH], F32R)
        k_hi = st.sb("k_hi", [P, 2, d.CH], F32R)
        k_lo = st.sb("k_lo", [P, 2, d.CH], F32R)
        g_hi = st.sb("g_hi", [P, d.KT, d.CH], F32R)
        g_lo = st.sb("g_lo", [P, d.KT, d.CH], F32R)
        bd = st.sb("bd", [P, d.CH])
        bd_hi = st.sb("bd_hi", [P, d.CH], F32R)
        bd_lo = st.sb("bd_lo", [P, d.CH], F32R)
        mask = st.sb("mask", [P, P])
        ones_r = st.sb("ones_r", [P, P], F32R)
        bo = st.sb("bo", [P, d.E])
        w = NormWork(st, d.NT)
        ps_k = st.ps("ps_k", [P, 2, d.CH])
        ps_g = st.ps("ps_g", [P, 2, d.KT, d.CH])
        ps_s = st.ps("ps_s", [P, d.CH])
        ps_v = st.ps("ps_v", [P, d.CH])

        w_in = [st.sem(f"w_in{i}") for i in range(2)]
        wq_in, bo_in = st.sem("wq_in"), st.sem("bo_in")
        dv, gp, const_ok, xb_ok = st.sem("dv"), st.sem("gp"), st.sem("const_ok"), st.sem("xb_ok")
        w_h, w_l = st.sem("w_h"), st.sem("w_l")
        xn_ok, t_ps, hi_ok, lo_ok, xk_h, xk_ok = (st.sem(n) for n in ("xn_ok", "t_ps", "hi_ok", "lo_ok", "xk_h", "xk_ok"))
        k_ps, k_h, k_ok, g_ps, g_h, g_ok = (st.sem(n) for n in ("k_ps", "k_h", "k_ok", "g_ps", "g_h", "g_ok"))
        s_ok, v_ps, bd_ok, bd_h, bd_l, m_ps, m_ok = (
            st.sem(n) for n in ("s_ok", "v_ps", "bd_ok", "bd_h", "bd_l", "m_ps", "m_ok"))

        WV_SPLIT, WO_SPLIT, WK_SPLIT = 4, 1, 6
        PREP = {0: 2, 3: 3}
        V_STEP, M_STEPS = 1, (4, 6)

        def turned(c):
            return ps_k if c < NP else ps_g[:, 1]

        with nc.Block() as block:
            @block.sync
            def _(sp):
                sp.dma_start(bo[:], io["L1_attn_bo"].rearrange("(a n) -> a n", a=1).to_broadcast([P, d.E]))\
                    .then_inc(bo_in, 16)
                for i in range(3 * NI):
                    n, name = i // 3, ("Wk", "Wv", "Wo")[i % 3]
                    src, dst = io["L1_attn_" + name], raw[:, i % 2, :]
                    if i >= 2:
                        sp.wait_ge(w_l, i - 1)
                    if name == "Wo":
                        sp.dma_start(dst.rearrange("p (c n) -> p c n", c=CPB),
                                     src[n * d.CH:(n + 1) * d.CH, :].rearrange("(c p) n -> p c n", p=P))\
                            .then_inc(w_in[i % 2], 16)
                    else:
                        sp.dma_start(dst.rearrange("p (k n) -> p k n", k=d.KT),
                                     src[:, n * d.CH:(n + 1) * d.CH].rearrange("(k p) n -> p k n", p=P))\
                            .then_inc(w_in[i % 2], 16)
                    if i == 1:
                        for q in range(2):
                            sp.dma_start(wq_raw[:, q, :].rearrange("p (k n) -> p k n", k=d.KT),
                                         io["L1_attn_Wq"][:, q * d.CH:(q + 1) * d.CH]
                                         .rearrange("(k p) n -> p k n", p=P)).then_inc(wq_in, 16)
                sp.wait_ge(wq_in, 32)

            @block.gpsimd
            def _(pool):
                link = chain(pool, gp)
                link(nc.gpsimd.memset(mask[:], 0.0))
                link(nc.gpsimd.memset(mask[0:HW, 0:HW], 1.0))
                link(nc.gpsimd.memset(mask[HW:P, HW:P], 1.0))
                nc.gpsimd.memset(as_f32(ones_r[:]), 1.0).then_inc(const_ok, 1)
                pool.wait_ge(bo_in, 16)
                pool.wait_ge(xn_ok, d.NC)
                for t in range(d.NT):
                    ins = nc.gpsimd.tensor_tensor(X[:, t, :], X[:, t, :], bo[:], ALU.add)
                ins.then_inc(xb_ok, 1)

            @block.vector
            def _(dve):
                def split(i, slot):
                    dve.wait_ge(w_h, i + 1)
                    nc.vector.tensor_tensor(w_lo[:, slot, :], raw[:, i % 2, :], as_f32(w_hi[:, slot, :]),
                                            ALU.subtract).then_inc(w_l, 1)

                def normal(c):
                    if c >= 1:
                        dve.wait_ge(t_ps, d.KT * c)
                        dve.wait_ge(xk_h, c)
                        dve.wait_ge(xk_ok, c)
                    for j in range(d.TPC):
                        t = d.TPC * c + j
                        ins = norm_apply(nc, w, t, xn[:, j, :], X[:, t, :])
                    ins.then_inc(xn_ok, 1)
                    dve.wait_ge(xn_ok, c + 1)

                def prepare(c):
                    sl = slice(d.TPC * c, d.TPC * (c + 1))
                    dve.wait_ge(xk_h, c + 1)
                    nc.vector.tensor_tensor(xk_lo[:, sl, :], xn[:], as_f32(xk_hi[:, sl, :]),
                                            ALU.subtract).then_inc(xk_ok, 1)
                    for k in range(d.KT):
                        dve.wait_ge(hi_ok, d.KT * c + k + 1)
                        nc.vector.tensor_tensor(xt_lo[:, k, c * d.CH:(c + 1) * d.CH], turned(c)[:, k, :],
                                                as_f32(xt_hi[:, k, c * d.CH:(c + 1) * d.CH]),
                                                ALU.subtract).then_inc(lo_ok, 1)

                def finish(u, step):
                    if step == 0:
                        for k in range(d.KT):
                            dve.wait_ge(g_h, d.KT * u + k + 1)
                            nc.vector.tensor_tensor(g_lo[:, k, :], ps_g[:, u % 2, k, :], as_f32(g_hi[:, k, :]),
                                                    ALU.subtract).then_inc(g_ok, 1)
                    if step == V_STEP + 1:
                        dve.wait_ge(v_ps, u + 1)
                        dve.wait_ge(const_ok, 1)
                        if u:
                            dve.wait_ge(bd_h, u)
                            dve.wait_ge(bd_l, u)
                        nc.vector.tensor_tensor(bd[:].rearrange("p (c m) -> p c m", m=P),
                                                ps_v[:].rearrange("p (c m) -> p c m", m=P),
                                                mask[:].unsqueeze(1).to_broadcast([P, CPB, P]),
                                                ALU.mult).then_inc(bd_ok, 1)
                        dve.wait_ge(bd_h, u + 1)
                        nc.vector.tensor_tensor(bd_lo[:], bd[:], as_f32(bd_hi[:]), ALU.subtract).then_inc(bd_l, 1)

                link = chain(dve, dv)
                norm_stats(nc, dve, link, w, [X[:, t, :] for t in range(d.NT)], 1)
                normal(0)
                split(0, 0)
                for c in range(NP):
                    prepare(c)
                    if c + 1 < NP:
                        normal(c + 1)
                for u in range(UN):
                    n, b = u // d.B, u % d.B
                    for t in range(TPB):
                        i = TPB * u + t
                        dve.wait_ge(k_h, i + 1)
                        nc.vector.scalar_tensor_tensor(out=k_lo[:, i % 2, :], in0=ps_k[:, i % 2, :], scalar=0.0,
                                                       in1=as_f32(k_hi[:, i % 2, :]), op0=ALU.max,
                                                       op1=ALU.subtract).then_inc(k_ok, 1)
                        if u == 0 and t in PREP:
                            normal(PREP[t])
                            prepare(PREP[t])
                        if u:
                            finish(u - 1, t)
                        if b == 0 and t == WV_SPLIT:
                            split(3 * n + 1, 2)
                        if b == 1 and t == WO_SPLIT:
                            split(3 * n + 2, 3)
                        if b == 1 and t == WK_SPLIT and n + 1 < NI:
                            split(3 * n + 3, (n + 1) % 2)
                for t in range(TPB):
                    finish(UN - 1, t)

            @block.scalar
            def _(act):
                def split(i, slot):
                    act.wait_ge(w_in[i % 2], 16 * (i // 2 + 1))
                    nc.scalar.activation(w_hi[:, slot, :], raw[:, i % 2, :], ACT.Copy).then_inc(w_h, 1)

                def rows(c):
                    act.wait_ge(xn_ok, c + 1)
                    nc.scalar.activation(xk_hi[:, d.TPC * c:d.TPC * (c + 1), :], xn[:], ACT.Copy).then_inc(xk_h, 1)

                def prepare(c):
                    for k in range(d.KT):
                        act.wait_ge(t_ps, d.KT * c + k + 1)
                        nc.scalar.activation(xt_hi[:, k, c * d.CH:(c + 1) * d.CH], turned(c)[:, k, :], ACT.Copy)\
                            .then_inc(hi_ok, 1)

                def finish(u, step):
                    n, b = u // d.B, u % d.B
                    if step == 0:
                        act.wait_ge(g_ps, TPB * (u + 1))
                        nc.scalar.activation(ksum[:, b, d.CH * n:d.CH * (n + 1)], ps_s[:], ACT.Copy).then_inc(s_ok, 1)
                        if u >= 1:
                            act.wait_ge(v_ps, u)
                        for k in range(d.KT):
                            nc.scalar.activation(g_hi[:, k, :], ps_g[:, u % 2, k, :], ACT.Copy).then_inc(g_h, 1)
                    if step == V_STEP + 1:
                        act.wait_ge(bd_ok, u + 1)
                        if u:
                            act.wait_ge(m_ps, 2 * u)
                        nc.scalar.activation(bd_hi[:], bd[:], ACT.Copy).then_inc(bd_h, 1)
                    if step - 1 in M_STEPS:
                        j = M_STEPS.index(step - 1)
                        act.wait_ge(m_ps, 2 * u + j + 1)
                        nc.scalar.activation(M[:, b, CPB * n + 2 * j:CPB * n + 2 * j + 2, :],
                                             ps_v[:].rearrange("p (c e) -> p c e", e=d.E), ACT.Copy).then_inc(m_ok, 1)

                norm_root(nc, act, w, 1)
                split(0, 0)
                for c in range(NP):
                    rows(c)
                    prepare(c)
                for u in range(UN):
                    n, b = u // d.B, u % d.B
                    for t in range(TPB):
                        i = TPB * u + t
                        act.wait_ge(k_ps, i + 1)
                        if i >= 2:
                            act.wait_ge(g_ps, i - 1)
                        nc.scalar.activation(k_hi[:, i % 2, :], ps_k[:, i % 2, :], ACT.Relu).then_inc(k_h, 1)
                        if u == 0 and t in PREP:
                            rows(PREP[t])
                            prepare(PREP[t])
                        if u:
                            finish(u - 1, t)
                        if b == 0 and t == WV_SPLIT:
                            if n:
                                act.wait_ge(v_ps, d.B * n)
                            split(3 * n + 1, 2)
                        if b == 1 and t == WO_SPLIT:
                            if n:
                                act.wait_ge(m_ps, 2 * d.B * n)
                            split(3 * n + 2, 3)
                        if b == 1 and t == WK_SPLIT and n + 1 < NI:
                            if n:
                                act.wait_ge(k_ps, TPB * d.B * n)
                            split(3 * n + 3, (n + 1) % 2)
                for t in range(TPB):
                    finish(UN - 1, t)

            @block.tensor
            def _(pe):
                def prepare(c):
                    pe.wait_ge(xn_ok, c + 1)
                    if 0 < c < NP or c > NP:
                        pe.wait_ge(lo_ok, d.KT * c)
                    for k in range(d.KT):
                        for j in range(d.TPC):
                            ins = nc.tensor.transpose(turned(c)[:, k, j * P:(j + 1) * P],
                                                      xn[:, j, k * P:(k + 1) * P], ident[:])
                        ins.then_inc(t_ps, 1)

                def keys(i):
                    u, t = i // TPB, i % TPB
                    n, b = u // d.B, u % d.B
                    if i % (TPB * d.B) == 0:
                        pe.wait_ge(w_l, 3 * n + 1)
                    if n == 0 and t % d.TPC == 0:
                        pe.wait_ge(lo_ok, d.KT * ((b * TPB + t) // d.TPC + 1))
                    if i < 2:
                        pe.wait_ge(lo_ok, d.KT * NP)
                    if i >= 2:
                        pe.wait_ge(k_ok, i - 1)
                    tok = slice((b * TPB + t) * P, (b * TPB + t + 1) * P)
                    for k in range(d.KT):
                        wk = slice(k * d.CH, (k + 1) * d.CH)
                        ins = mm_split(nc, ps_k[:, i % 2, :], xt_hi[:, k, tok], xt_lo[:, k, tok],
                                       w_hi[:, n % 2, wk], w_lo[:, n % 2, wk], k == 0, k == d.KT - 1)
                    ins.then_inc(k_ps, 1)

                def sums(i):
                    u, t = i // TPB, i % TPB
                    n, b = u // d.B, u % d.B
                    pe.wait_ge(k_ok, i + 1)
                    if n == 0 and t % d.TPC == 0:
                        pe.wait_ge(xk_ok, (b * TPB + t) // d.TPC + 1)
                    if u == 1 and t == 0:
                        pe.wait_ge(lo_ok, d.KT * d.NC)
                    if t == 0 and u >= 1:
                        pe.wait_ge(s_ok, u)
                    if t == 0 and u >= 2:
                        pe.wait_ge(g_ok, d.KT * (u - 1))
                    kh, kl = k_hi[:, i % 2, :], k_lo[:, i % 2, :]
                    for m in range(d.KT):
                        x = slice(m * P, (m + 1) * P)
                        mm_split(nc, ps_g[:, u % 2, m, :], xk_hi[:, b * TPB + t, x], xk_lo[:, b * TPB + t, x], kh, kl,
                                 t == 0, t == TPB - 1)
                    mm_split(nc, ps_s[:], ones_r[:], None, kh, kl, t == 0, t == TPB - 1).then_inc(g_ps, 1)

                def finish(u, step):
                    n = u // d.B
                    if step == V_STEP:
                        pe.wait_ge(g_ok, d.KT * (u + 1))
                        pe.wait_ge(w_l, 3 * n + 2)
                        if u:
                            pe.wait_ge(m_ok, 2 * u)
                        for c in range(CPB):
                            cols = slice(c * P, (c + 1) * P)
                            for k in range(d.KT):
                                wv = slice(k * d.CH + c * P, k * d.CH + (c + 1) * P)
                                ins = mm_split(nc, ps_v[:, cols], w_hi[:, 2, wv], w_lo[:, 2, wv], g_hi[:, k, cols],
                                               g_lo[:, k, cols], k == 0, k == d.KT - 1)
                        ins.then_inc(v_ps, 1)
                    if step in M_STEPS:
                        j = M_STEPS.index(step)
                        pe.wait_ge(bd_l, u + 1)
                        pe.wait_ge(w_l, 3 * n + 3)
                        if j:
                            pe.wait_ge(m_ok, 2 * u + j)
                        for c in (2 * j, 2 * j + 1):
                            cols, wo = slice(c * P, (c + 1) * P), slice(c * d.E, (c + 1) * d.E)
                            ins = mm_split(nc, ps_v[:, (c % 2) * d.E:(c % 2 + 1) * d.E], bd_hi[:, cols],
                                           bd_lo[:, cols], w_hi[:, 3, wo], w_lo[:, 3, wo], True, True)
                        ins.then_inc(m_ps, 1)

                for c in range(NP):
                    prepare(c)
                pe.wait_ge(const_ok, 1)
                keys(0)
                for u in range(UN):
                    for t in range(TPB):
                        i = TPB * u + t
                        if i + 1 < TPB * UN:
                            keys(i + 1)
                        if u == 0 and t in PREP:
                            prepare(PREP[t])
                        sums(i)
                        if u:
                            finish(u - 1, t)
                for t in range(TPB):
                    finish(UN - 1, t)


def stage_queries(nc, d, io, keep):
    with ExitStack() as ctx:
        st = Store(nc, ctx, "qry")
        X, ident = keep["X"], keep["ident"]
        xt_hi, xt_lo, M, ksum, wq_raw = (keep[n] for n in ("xt_hi", "xt_lo", "M", "ksum", "wq_raw"))
        NI = d.INNER // d.CH
        CPB = d.CH // P
        TPB = d.S // P
        HW = P // 2
        HPB = d.CH // HW
        UN = d.NT * NI
        w_hi = st.sb("w_hi", [P, NI, d.KT * d.CH], F32R)
        w_lo = st.sb("w_lo", [P, NI, d.KT * d.CH], F32R)
        m_hi = st.sb("m_hi", [P, d.NCH, d.E], F32R)
        m_lo = st.sb("m_lo", [P, d.NCH, d.E], F32R)
        qr = st.sb("qr", [P, 2, d.CH])
        prod = st.sb("prod", [P, 2, d.CH])
        nrm = st.sb("nrm", [P, HPB])
        rec = st.sb("rec", [P, HPB])
        qn = st.sb("qn", [P, 2, d.CH])
        n_hi = st.sb("n_hi", [P, 2, d.CH], F32R)
        n_lo = st.sb("n_lo", [P, 2, d.CH], F32R)
        ps_q = st.ps("ps_q", [P, 2, d.CH])
        ps_t = st.ps("ps_t", [P, 2, d.CH])
        ps_o = st.ps("ps_o", [P, 2, d.CH])
        w_in = [st.sem(f"w_in{i}") for i in range(2)]
        w_h, w_ok, m_h, m_ok = (st.sem(n) for n in ("w_h", "w_ok", "m_h", "m_ok"))
        q_ps, q_ok, pr_ok, dv, qn_ok, t_ps, n_h, n_ok, o_ps, x_ok = (
            st.sem(n) for n in ("q_ps", "q_ok", "pr_ok", "dv", "qn_ok", "t_ps", "n_h", "n_ok", "o_ps", "x_ok"))

        def cols(n):
            return slice(n * d.CH, (n + 1) * d.CH)

        def split_at(u):
            b, n = u // (NI * TPB), u % (NI * TPB)
            return (b, n) if n < NI and b < d.B else None

        with nc.Block() as block:
            @block.sync
            def _(sp):
                for q in range(2, NI):
                    sp.dma_start(wq_raw[:, q, :].rearrange("p (k n) -> p k n", k=d.KT),
                                 io["L1_attn_Wq"][:, q * d.CH:(q + 1) * d.CH].rearrange("(k p) n -> p k n", p=P))\
                        .then_inc(w_in[q - 2], 16)

            @block.gpsimd
            def _(pool):
                for u in range(UN):
                    b, n = u // (TPB * NI), u % NI
                    pool.wait_ge(q_ok, u + 1)
                    if u >= 2:
                        pool.wait_ge(qn_ok, u - 1)
                    nc.gpsimd.tensor_tensor(prod[:, u % 2, :], qr[:, u % 2, :], ksum[:, b, cols(n)],
                                            ALU.mult).then_inc(pr_ok, 1)

            @block.vector
            def _(dve):
                link = chain(dve, dv)

                def divide(u):
                    dve.wait_ge(pr_ok, u + 1)
                    link(nc.vector.tensor_reduce(nrm[:], prod[:, u % 2, :].rearrange("p (h e) -> p h e", e=HW),
                                                 AX.X, ALU.add))
                    link(nc.vector.reciprocal(rec[:], nrm[:]))
                    if u >= 2:
                        dve.wait_ge(t_ps, u - 1)
                    nc.vector.scalar_tensor_tensor(out=qn[:, u % 2, :].rearrange("p (h e) -> p h e", e=HW),
                                                   in0=rec[:].unsqueeze(2).to_broadcast([P, HPB, HW]), scalar=1e6,
                                                   in1=qr[:, u % 2, :].rearrange("p (h e) -> p h e", e=HW),
                                                   op0=ALU.min, op1=ALU.mult).then_inc(qn_ok, 1)
                    dve.wait_ge(qn_ok, u + 1)

                def low(u):
                    dve.wait_ge(n_h, u + 1)
                    if u >= 2:
                        dve.wait_ge(o_ps, u - 1)
                    nc.vector.tensor_tensor(n_lo[:, u % 2, :], ps_t[:, u % 2, :], as_f32(n_hi[:, u % 2, :]),
                                            ALU.subtract).then_inc(n_ok, 1)

                def add(t):
                    dve.wait_ge(o_ps, NI * (t + 1))
                    nc.vector.tensor_tensor(X[:, t, :], X[:, t, :], ps_o[:, t % 2, 0:d.E], ALU.add).then_inc(x_ok, 1)

                for u in range(UN + 4):
                    if u < NI:
                        dve.wait_ge(w_h, u + 1)
                        nc.vector.tensor_tensor(w_lo[:, u, :], wq_raw[:, u, :], as_f32(w_hi[:, u, :]),
                                                ALU.subtract).then_inc(w_ok, 1)
                    if 1 <= u <= UN:
                        divide(u - 1)
                    if split_at(u):
                        b, n = split_at(u)
                        blk = slice(CPB * n, CPB * (n + 1))
                        dve.wait_ge(m_h, NI * b + n + 1)
                        nc.vector.tensor_tensor(m_lo[:, blk, :], M[:, b, blk, :], as_f32(m_hi[:, blk, :]),
                                                ALU.subtract).then_inc(m_ok, 1)
                    if 2 <= u < UN + 2:
                        low(u - 2)
                    if u >= NI + 3 and (u - 3) % NI == 0:
                        add((u - 3) // NI - 1)

            @block.scalar
            def _(act):
                def high(u):
                    act.wait_ge(t_ps, u + 1)
                    if u >= 2:
                        act.wait_ge(o_ps, u - 1)
                    nc.scalar.activation(n_hi[:, u % 2, :], ps_t[:, u % 2, :], ACT.Copy).then_inc(n_h, 1)

                for u in range(UN + 2):
                    if u < NI:
                        if u >= 2:
                            act.wait_ge(w_in[u - 2], 16)
                        nc.scalar.activation(w_hi[:, u, :], wq_raw[:, u, :], ACT.Copy).then_inc(w_h, 1)
                    if u < UN:
                        act.wait_ge(q_ps, u + 1)
                        if u >= 2:
                            act.wait_ge(qn_ok, u - 1)
                        nc.scalar.activation(qr[:, u % 2, :], ps_q[:, u % 2, :], ACT.Relu).then_inc(q_ok, 1)
                    if split_at(u):
                        b, n = split_at(u)
                        blk = slice(CPB * n, CPB * (n + 1))
                        if b:
                            act.wait_ge(o_ps, u - NI + 1)
                        nc.scalar.activation(m_hi[:, blk, :], M[:, b, blk, :], ACT.Copy).then_inc(m_h, 1)
                    if u >= 2:
                        high(u - 2)

            @block.tensor
            def _(pe):
                def query(u):
                    t, n = u // NI, u % NI
                    if u < NI:
                        pe.wait_ge(w_ok, n + 1)
                    if u >= 2:
                        pe.wait_ge(q_ok, u - 1)
                    tok = slice(t * P, (t + 1) * P)
                    for k in range(d.KT):
                        ins = mm_split(nc, ps_q[:, u % 2, :], xt_hi[:, k, tok], xt_lo[:, k, tok],
                                       w_hi[:, n, cols(k)], w_lo[:, n, cols(k)], k == 0, k == d.KT - 1)
                    ins.then_inc(q_ps, 1)

                def turn(u):
                    pe.wait_ge(qn_ok, u + 1)
                    if u >= 2:
                        pe.wait_ge(n_ok, u - 1)
                    for c in range(CPB):
                        ins = nc.tensor.transpose(ps_t[:, u % 2, c * P:(c + 1) * P], qn[:, u % 2, c * P:(c + 1) * P],
                                                  ident[:])
                    ins.then_inc(t_ps, 1)

                def result(u):
                    t, n = u // NI, u % NI
                    b = t // TPB
                    if t % TPB == 0:
                        pe.wait_ge(m_ok, NI * b + n + 1)
                    if n == 0 and t >= 2:
                        pe.wait_ge(x_ok, t - 1)
                    pe.wait_ge(n_ok, u + 1)
                    for c in range(CPB):
                        q = slice(c * P, (c + 1) * P)
                        ins = mm_split(nc, ps_o[:, t % 2, 0:d.E], n_hi[:, u % 2, q], n_lo[:, u % 2, q],
                                       m_hi[:, CPB * n + c, :], m_lo[:, CPB * n + c, :],
                                       n == 0 and c == 0, n == NI - 1 and c == CPB - 1)
                    ins.then_inc(o_ps, 1)

                for u in range(UN + 3):
                    if u < UN:
                        query(u)
                    if 2 <= u < UN + 2:
                        turn(u - 2)
                    if u >= 3:
                        result(u - 3)


def stage_routed(nc, d, io, keep, out):
    with ExitStack() as ctx:
        st = Store(nc, ctx, "rt")
        X, ident = keep["X"], keep["ident"]
        NE = io["L1_ffn_wr"].shape[0]
        names = ("w1", "w3", "w2")
        raw = st.sb("raw", [P, 3, d.KT, d.E])
        wr_raw = st.sb("wr_raw", [NE, d.E])
        wt_hi = st.sb("wt_hi", [P, 3, d.KT, d.E], F32R)
        wt_lo = st.sb("wt_lo", [P, 3, d.KT, d.E], F32R)
        w2t = st.sb("w2t", [P, d.KT, d.E])
        wr_hi = st.sb("wr_hi", [P, d.KT, NE], F32R)
        wr_lo = st.sb("wr_lo", [P, d.KT, NE], F32R)
        xn = st.sb("xn", [P, d.TPC, d.E])
        xt_hi = st.sb("xt_hi", [P, d.KT, d.CH], F32R)
        xt_lo = st.sb("xt_lo", [P, d.KT, d.CH], F32R)
        h1 = st.sb("h1", [P, d.KT, d.CH])
        h_hi = st.sb("h_hi", [P, d.KT, d.CH], F32R)
        h_lo = st.sb("h_lo", [P, d.KT, d.CH], F32R)
        h2 = st.sb("h2", [P, d.TPC, d.E])
        lg = st.sb("lg", [P, d.TPC, NE])
        lmax = st.sb("lmax", [P, d.TPC])
        ex = st.sb("ex", [P, d.TPC, NE])
        esum = st.sb("esum", [P, d.TPC])
        pr = st.sb("pr", [P, d.TPC, NE])
        best = st.sb("best", [P, d.TPC, 8])
        idx = st.sb("idx", [P, d.TPC, 8], U32)
        idx_f = st.sb("idx_f", [P, d.TPC, 2])
        oh = st.sb("oh", [P, 2, d.TPC, NE])
        gs = st.sb("gs", [P, d.TPC])
        gate = st.sb("gate", [P, d.TPC, NE])
        iota_i = st.sb("iota_i", [P, NE], mybir.dt.int32)
        iota_f = st.sb("iota_f", [P, NE])
        acc = st.sb("acc", [NE, d.E])
        acc_t = st.sb("acc_t", [P, d.KT, NE])
        w = NormWork(st, d.TPC)
        ps_t = st.ps("ps_t", [P, d.KT, d.CH])
        ps_h = st.ps("ps_h", [P, d.KT, d.CH])
        ps_2 = st.ps("ps_2", [P, 2, 2, d.E])
        ps_l = st.ps("ps_l", [P, d.CH])
        ps_a = st.ps("ps_a", [NE, d.E])
        w_in, dv, on, out_s = st.sem("w_in"), st.sem("dv"), st.sem("on"), st.sem("out")
        wt_ps, wt_h, wt_l = st.sem("wt_ps"), st.sem("wt_h"), st.sem("wt_l")
        xn_ok, t_ps, hi_ok, lo_ok = (st.sem(n) for n in ("xn_ok", "t_ps", "hi_ok", "lo_ok"))
        h_ps, h1_ok, hh_ok, hl_ok, l_ps, lmax_ok, ex_ok = (
            st.sem(n) for n in ("h_ps", "h1_ok", "hh_ok", "hl_ok", "l_ps", "lmax_ok", "ex_ok"))
        h2_ps, h2_ok, g_ok, a_ps = st.sem("h2_ps"), st.sem("h2_ok"), st.sem("g_ok"), st.sem("a_ps")
        acc_ok, at_ps, at_ok, fin_ps, fin_ok = (st.sem(n) for n in ("acc_ok", "at_ps", "at_ok", "fin_ps", "fin_ok"))
        out_tiles = out.rearrange("b (t p) e -> p (b t) e", p=P)

        with nc.Block() as block:
            @block.sync
            def _(sp):
                for i, name in enumerate(names):
                    sp.dma_start(raw[:, i], io["L1_ffn_" + name].rearrange("(a p) n -> p a n", p=P)).then_inc(w_in, 16)
                sp.dma_start(wr_raw[:], io["L1_ffn_wr"]).then_inc(w_in, 16)
                sp.dma_start(out_tiles[:, 1:, :], X[:, 1:, :]).then_inc(out_s, 16)
                sp.wait_ge(fin_ok, 1)
                sp.dma_start(out_tiles[:, 0, :], X[:, 0, :]).then_inc(out_s, 16)
                sp.wait_ge(out_s, 32)

            @block.gpsimd
            def _(pool):
                nc.gpsimd.iota(iota_i[:], pattern=[[1, NE]], base=0, channel_multiplier=0).then_inc(on, 1)

            @block.vector
            def _(dve):
                link = chain(dve, dv)
                nc.vector.memset(ps_l[:], 0.0).then_inc(on, 1)
                dve.wait_ge(on, 2)
                nc.vector.tensor_copy(iota_f[:], iota_i[:])
                for i in range(3):
                    dve.wait_ge(wt_h, i + 1)
                    src = ps_h if i % 2 else ps_t
                    flat = src[:].rearrange("p k c -> p (k c)")[:, 0:d.KT * d.E]
                    if i < 2:
                        nc.vector.tensor_tensor(wt_lo[:, i].rearrange("p k n -> p (k n)"), flat,
                                                as_f32(wt_hi[:, i]).rearrange("p k n -> p (k n)"),
                                                ALU.subtract).then_inc(wt_l, 1)
                    else:
                        nc.vector.tensor_copy(w2t[:].rearrange("p k n -> p (k n)"), flat).then_inc(wt_l, 1)
                dve.wait_ge(wt_h, 4)
                nc.vector.tensor_tensor(wr_lo[:], ps_l[:, 0:d.KT * NE].rearrange("p (k n) -> p k n", n=NE),
                                        as_f32(wr_hi[:]), ALU.subtract).then_inc(wt_l, 1)
                for c in range(d.NC):
                    norm_stats(nc, dve, link, w, [X[:, d.TPC * c + j, :] for j in range(d.TPC)], c + 1)
                    if c >= 1:
                        dve.wait_ge(t_ps, d.KT * c)
                    for j in range(d.TPC):
                        ins = norm_apply(nc, w, j, xn[:, j, :], X[:, d.TPC * c + j, :])
                    ins.then_inc(xn_ok, 1)
                    for k in range(d.KT):
                        dve.wait_ge(hi_ok, d.KT * c + k + 1)
                        nc.vector.tensor_tensor(xt_lo[:, k, :], ps_t[:, k, :], as_f32(xt_hi[:, k, :]),
                                                ALU.subtract).then_inc(lo_ok, 1)
                    dve.wait_ge(l_ps, c + 1)
                    link(nc.vector.tensor_copy(lg[:].rearrange("p j e -> p (j e)"), ps_l[:, 0:d.TPC * NE]))
                    link(nc.vector.tensor_reduce(lmax[:], lg[:], AX.X, ALU.max))
                    nc.vector.tensor_tensor(lg[:], lg[:], lmax[:].unsqueeze(2).to_broadcast([P, d.TPC, NE]),
                                            ALU.subtract).then_inc(lmax_ok, 1)
                    for m in range(d.KT):
                        dve.wait_ge(hh_ok, d.KT * c + m + 1)
                        nc.vector.tensor_tensor(h_lo[:, m, :], h1[:, m, :], as_f32(h_hi[:, m, :]),
                                                ALU.subtract).then_inc(hl_ok, 1)
                    dve.wait_ge(ex_ok, c + 1)
                    link(nc.vector.tensor_reduce(esum[:], ex[:], AX.X, ALU.add))
                    link(nc.vector.reciprocal(esum[:], esum[:]))
                    link(nc.vector.tensor_tensor(pr[:], ex[:], esum[:].unsqueeze(2).to_broadcast([P, d.TPC, NE]),
                                                 ALU.mult))
                    for j in range(d.TPC):
                        ins = nc.vector.max(best[:, j, :], pr[:, j, :])
                    link(ins)
                    for j in range(d.TPC):
                        ins = nc.vector.max_index(idx[:, j, :], best[:, j, :], pr[:, j, :])
                    link(ins)
                    link(nc.vector.tensor_copy(idx_f[:], idx[:, :, 0:2]))
                    for i in range(2):
                        ins = nc.vector.tensor_tensor(oh[:, i], idx_f[:, :, i:i + 1].to_broadcast([P, d.TPC, NE]),
                                                      iota_f[:].unsqueeze(1).to_broadcast([P, d.TPC, NE]),
                                                      ALU.is_equal)
                    link(ins)
                    for i in range(2):
                        ins = nc.vector.tensor_tensor(oh[:, i], oh[:, i],
                                                      best[:, :, i:i + 1].to_broadcast([P, d.TPC, NE]), ALU.mult)
                    link(ins)
                    nc.vector.tensor_tensor(gs[:], best[:, :, 0], best[:, :, 1], ALU.add)
                    link(nc.vector.tensor_tensor(oh[:, 0], oh[:, 0], oh[:, 1], ALU.add))
                    link(nc.vector.reciprocal(gs[:], gs[:]))
                    if c >= 1:
                        dve.wait_ge(a_ps, c)
                    nc.vector.tensor_tensor(gate[:], oh[:, 0], gs[:].unsqueeze(2).to_broadcast([P, d.TPC, NE]),
                                            ALU.mult).then_inc(g_ok, 1)
                dve.wait_ge(a_ps, d.NC)
                nc.vector.tensor_copy(acc[:], ps_a[:]).then_inc(acc_ok, 1)
                dve.wait_ge(at_ps, 1)
                nc.vector.tensor_copy(acc_t[:].rearrange("p k e -> p (k e)"), ps_l[:, 0:d.KT * NE]).then_inc(at_ok, 1)
                dve.wait_ge(fin_ps, 1)
                nc.vector.tensor_tensor(X[0:NE, 0, :], X[0:NE, 0, :], ps_a[:], ALU.add).then_inc(fin_ok, 1)

            @block.scalar
            def _(act):
                for i in range(3):
                    act.wait_ge(wt_ps, i + 1)
                    src = ps_h if i % 2 else ps_t
                    flat = src[:].rearrange("p k c -> p (k c)")[:, 0:d.KT * d.E]
                    nc.scalar.activation(wt_hi[:, i].rearrange("p k n -> p (k n)"), flat, ACT.Copy).then_inc(wt_h, 1)
                act.wait_ge(wt_ps, 4)
                nc.scalar.activation(wr_hi[:].rearrange("p k n -> p (k n)"), ps_l[:, 0:d.KT * NE], ACT.Copy)\
                    .then_inc(wt_h, 1)
                for c in range(d.NC):
                    norm_root(nc, act, w, c + 1)
                    for k in range(d.KT):
                        act.wait_ge(t_ps, d.KT * c + k + 1)
                        if c:
                            act.wait_ge(l_ps, c)
                            act.wait_ge(h_ps, d.KT * c)
                        nc.scalar.activation(xt_hi[:, k, :], ps_t[:, k, :], ACT.Copy).then_inc(hi_ok, 1)
                    for m in range(d.KT):
                        act.wait_ge(h_ps, d.KT * c + m + 1)
                        if c:
                            act.wait_ge(hl_ok, d.KT * c)
                            act.wait_ge(h2_ps, 2 * c)
                        nc.scalar.activation(h1[:, m, :], ps_h[:, m, :], ACT.Silu).then_inc(h1_ok, 1)
                        act.wait_ge(h1_ok, d.KT * c + m + 1)
                        nc.scalar.activation(h_hi[:, m, :], h1[:, m, :], ACT.Copy).then_inc(hh_ok, 1)
                    for j in range(2):
                        act.wait_ge(h2_ps, 2 * c + j + 1)
                        if c:
                            act.wait_ge(a_ps, c)
                        nc.scalar.activation(h2[:, 2 * j:2 * j + 2, :], ps_2[:, j], ACT.Silu).then_inc(h2_ok, 1)
                    act.wait_ge(lmax_ok, c + 1)
                    nc.scalar.activation(ex[:], lg[:], ACT.Exp).then_inc(ex_ok, 1)

            @block.tensor
            def _(pe):
                pe.wait_ge(w_in, 64)
                for i in range(3):
                    dst = ps_h if i % 2 else ps_t
                    flat = dst[:].rearrange("p k c -> p (k c)")
                    if i == 2:
                        pe.wait_ge(wt_l, 1)
                    for k in range(d.KT):
                        for a in range(d.KT):
                            ins = nc.tensor.transpose(flat[:, k * d.E + a * P:k * d.E + (a + 1) * P],
                                                      raw[:, i, a, k * P:(k + 1) * P], ident[:])
                    ins.then_inc(wt_ps, 1)
                pe.wait_ge(on, 2)
                for k in range(d.KT):
                    ins = nc.tensor.transpose(ps_l[:, k * NE:(k + 1) * NE], wr_raw[:, k * P:(k + 1) * P],
                                              ident[0:NE, 0:NE])
                ins.then_inc(wt_ps, 1)
                pe.wait_ge(wt_l, 4)
                for c in range(d.NC):
                    pe.wait_ge(xn_ok, c + 1)
                    if c:
                        pe.wait_ge(lo_ok, d.KT * c)
                    for k in range(d.KT):
                        for j in range(d.TPC):
                            ins = nc.tensor.transpose(ps_t[:, k, j * P:(j + 1) * P], xn[:, j, k * P:(k + 1) * P],
                                                      ident[:])
                        ins.then_inc(t_ps, 1)
                    pe.wait_ge(lo_ok, d.KT * (c + 1))
                    for j in range(d.TPC):
                        t = slice(j * P, (j + 1) * P)
                        if c and j == 0:
                            pe.wait_ge(lmax_ok, c)
                        for k in range(d.KT):
                            ins = mm_split(nc, ps_l[:, j * NE:(j + 1) * NE], xt_hi[:, k, t], xt_lo[:, k, t],
                                           wr_hi[:, k, :], wr_lo[:, k, :], k == 0, k == d.KT - 1)
                    ins.then_inc(l_ps, 1)
                    for m in range(d.KT):
                        cols = slice(m * P, (m + 1) * P)
                        if c:
                            pe.wait_ge(h1_ok, d.KT * (c - 1) + m + 1)
                        for k in range(d.KT):
                            ins = mm_split(nc, ps_h[:, m, :], wt_hi[:, 0, k, cols], wt_lo[:, 0, k, cols],
                                           xt_hi[:, k, :], xt_lo[:, k, :], k == 0, k == d.KT - 1)
                        ins.then_inc(h_ps, 1)
                    pe.wait_ge(hl_ok, d.KT * (c + 1))
                    for j in range(2):
                        if c:
                            pe.wait_ge(h2_ok, 2 * (c - 1) + j + 1)
                        for i in range(2):
                            t = slice((2 * j + i) * P, (2 * j + i + 1) * P)
                            for k in range(d.KT):
                                ins = mm_split(nc, ps_2[:, j, i, :], h_hi[:, k, t], h_lo[:, k, t],
                                               wt_hi[:, 1, k, :], wt_lo[:, 1, k, :], k == 0, k == d.KT - 1)
                        ins.then_inc(h2_ps, 1)
                    pe.wait_ge(g_ok, c + 1)
                    pe.wait_ge(h2_ok, 2 * (c + 1))
                    for j in range(d.TPC):
                        ins = nc.tensor.matmul(ps_a[:], gate[:, j, :], h2[:, j, :], start=c == 0 and j == 0,
                                               stop=c == d.NC - 1 and j == d.TPC - 1)
                    ins.then_inc(a_ps, 1)
                pe.wait_ge(acc_ok, 1)
                for k in range(d.KT):
                    ins = nc.tensor.transpose(ps_l[:, k * NE:(k + 1) * NE], acc[:, k * P:(k + 1) * P],
                                              ident[0:NE, 0:NE])
                ins.then_inc(at_ps, 1)
                pe.wait_ge(at_ok, 1)
                for k in range(d.KT):
                    ins = nc.tensor.matmul(ps_a[:], acc_t[:, k, :], w2t[:, k, :], start=k == 0, stop=k == d.KT - 1)
                ins.then_inc(fin_ps, 1)


INS = ["L0_attn_x", "L0_attn_W_attn", "L0_attn_W_proj", "L0_attn_lambda_q1", "L0_attn_lambda_k1",
       "L0_attn_lambda_q2", "L0_attn_lambda_k2", "L0_ffn_W_syn", "L0_ffn_b_syn", "L0_ffn_W_out", "L0_ffn_b_out",
       "L0_ffn_gamma", "L0_ffn_beta", "L1_attn_Wq", "L1_attn_Wk", "L1_attn_Wv", "L1_attn_Wo", "L1_attn_bo",
       "L1_ffn_w1", "L1_ffn_w3", "L1_ffn_w2", "L1_ffn_wr"]


def two_layers(nc, io, out, dump=None):
    d = Dims(io["L0_attn_x"], io["L0_ffn_W_syn"], io["L1_attn_Wq"])
    with ExitStack() as ctx:
        keep = {
            "X": ctx.enter_context(nc.sbuf_tensor("residual", [P, d.NT, d.E], F32)),
            "ident": ctx.enter_context(nc.sbuf_tensor("ident", [P, P], F32)),
        }
        with ExitStack() as att:
            keep["AO"] = att.enter_context(nc.sbuf_tensor("att_out", [P, d.NT, d.E], F32))
            scratch = {
                "qk": nc.dram_tensor("qk_parts", [2, d.B, 2 * d.E, d.S], F32).ap(),
                "v": nc.dram_tensor("v_rows", [d.B, d.H // d.G, P, d.S // P, d.G * 32], F32).ap(),
                "zero": nc.dram_tensor("zero_rows", [2, d.G * d.S], F32).ap(),
            }
            stage_qkv(nc, d, io, keep, scratch)
            stage_attention(nc, d, io, keep, scratch)
            if dump == "att":
                return dump_tile(nc, d, keep["AO"], out)
            stage_mlp(nc, d, io, keep)
        if dump == "x2":
            return dump_tile(nc, d, keep["X"], out)
        with ExitStack() as lin:
            def sb(name, shape, dt=F32):
                return lin.enter_context(nc.sbuf_tensor("lin_" + name, shape, dt))
            keep["xt_hi"] = sb("xt_hi", [P, d.KT, d.TOK], F32R)
            keep["xt_lo"] = sb("xt_lo", [P, d.KT, d.TOK], F32R)
            keep["M"] = sb("m", [P, d.B, d.NCH, d.E])
            keep["ksum"] = sb("ksum", [P, d.B, d.INNER])
            keep["wq_raw"] = sb("wq_raw", [P, d.INNER // d.CH, d.KT * d.CH])
            stage_keys(nc, d, io, keep)
            stage_queries(nc, d, io, keep)
        if dump == "x3":
            return dump_tile(nc, d, keep["X"], out)
        stage_routed(nc, d, io, keep, out)


def kernel(**inputs):
    import numpy as np
    import concourse.bacc as bacc
    from concourse.bass_utils import run_bass_kernel_spmd

    nc = bacc.Bacc("TRN2", target_bir_lowering=False, num_devices=1)
    arrays, io = {}, {}
    for name in INS:
        a = np.ascontiguousarray(inputs[name])
        arrays[name] = a
        io[name] = nc.dram_tensor(name, a.shape, mybir.dt.from_np(a.dtype), kind="ExternalInput").ap()
    shape = arrays["L0_attn_x"].shape
    out = nc.dram_tensor("out", shape, F32, kind="ExternalOutput").ap()
    two_layers(nc, io, out)
    r = run_bass_kernel_spmd(nc, [arrays], core_ids=[0])
    return r.results[0]["out"]
```

```python
import math
from contextlib import ExitStack

import concourse.bass as bass
from concourse import mybir

F32 = mybir.dt.float32
F32R = mybir.dt.float32r
U32 = mybir.dt.uint32
ALU = mybir.AluOpType
ACT = mybir.ActivationFunctionType
AX = mybir.AxisListType

P = 128
EPS = 1e-5
LAMBDA_INIT = 0.8 - 0.6 * math.exp(-0.3 * 0)


def as_f32(ap):
    return ap.bitcast(F32)


class Dims:

    def __init__(self, x, w_syn, wq):
        self.B, self.S, self.E = x.shape
        self.TOK = self.B * self.S
        self.NT = self.TOK // P
        self.CH = 512
        self.TPC = self.CH // P
        self.NC = self.TOK // self.CH
        self.KT = self.E // P
        self.H = 16
        self.HD = self.E // self.H
        self.G = 4
        self.NG = self.H // self.G * self.B
        self.N = w_syn.shape[0]
        self.INNER = wq.shape[1]
        self.NCH = self.INNER // P


class Store:

    def __init__(self, nc, ctx, stage):
        self.nc, self.ctx, self.stage = nc, ctx, stage
        self.sems = []

    def sb(self, name, shape, dt=F32):
        return self.ctx.enter_context(self.nc.sbuf_tensor(f"{self.stage}_{name}", shape, dt))

    def ps(self, name, shape):
        return self.ctx.enter_context(self.nc.psum_tensor(f"{self.stage}_{name}", shape, F32))

    def sem(self, name):
        s = self.ctx.enter_context(self.nc.semaphore(f"{self.stage}_{name}"))
        self.sems.append(s.num)
        return s

    def clear(self):
        nc, first, last = self.nc, min(self.sems), max(self.sems)
        assert last - first + 1 == len(self.sems)
        with nc.Block() as block:
            @block.sync
            def _(sp):
                sp.sem_clear(range(first, last + 1))


def chain(eng, sem):
    done = [0]

    def link(ins):
        done[0] += 1
        ins.then_inc(sem, 1)
        eng.wait_ge(sem, done[0])
    return link


class NormWork:

    def __init__(self, st, tiles, tag=""):
        self.stats = st.sb("stats" + tag, [P, tiles, 6])
        self.mv = st.sb("mv" + tag, [P, tiles, 2])
        self.ve = st.sb("ve" + tag, [P, tiles])
        self.sd = st.sb("sd" + tag, [P, tiles])
        self.r0 = st.sb("r0" + tag, [P, tiles])
        self.t0 = st.sb("t0" + tag, [P, tiles])
        self.rstd = st.sb("rstd" + tag, [P, tiles])
        self.var_ready = st.sem("var_ready" + tag)
        self.sd_ready = st.sem("sd_ready" + tag)


def norm_var(nc, link, w, tiles):
    for j, x in enumerate(tiles):
        ins = nc.vector.bn_stats(w.stats[:, j, :], x)
    link(ins)
    for j in range(len(tiles)):
        ins = nc.vector.bn_aggr(w.mv[:, j, :], w.stats[:, j, :])
    link(ins)
    nc.vector.tensor_scalar(w.ve[:], w.mv[:, :, 1], EPS, None, ALU.add).then_inc(w.var_ready, 1)


def norm_rstd(nc, dve, link, w, nth):
    dve.wait_ge(w.sd_ready, nth)
    link(nc.vector.reciprocal(w.r0[:], w.sd[:]))
    link(nc.vector.tensor_tensor(w.t0[:], w.r0[:], w.r0[:], ALU.mult))
    link(nc.vector.tensor_tensor(w.t0[:], w.t0[:], w.ve[:], ALU.mult))
    link(nc.vector.tensor_scalar(w.t0[:], w.t0[:], -0.5, 1.5, ALU.mult, ALU.add))
    link(nc.vector.tensor_tensor(w.rstd[:], w.t0[:], w.r0[:], ALU.mult))


def norm_stats(nc, dve, link, w, tiles, nth):
    norm_var(nc, link, w, tiles)
    norm_rstd(nc, dve, link, w, nth)


def norm_root(nc, act, w, nth):
    act.wait_ge(w.var_ready, nth)
    nc.scalar.activation(w.sd[:], w.ve[:], ACT.Sqrt).then_inc(w.sd_ready, 1)


def norm_apply(nc, w, j, out, x):
    return nc.vector.tensor_scalar(out, x, w.mv[:, j, 0:1], w.rstd[:, j:j + 1], ALU.subtract, ALU.mult)


def mm_split(nc, out, lhs_hi, lhs_lo, rhs_hi, rhs_lo, first, last):
    terms = [(lhs_hi, rhs_hi)]
    if rhs_lo is not None:
        terms.append((lhs_hi, rhs_lo))
    if lhs_lo is not None:
        terms.append((lhs_lo, rhs_hi))
    for n, (a, b) in enumerate(terms):
        ins = nc.tensor.matmul(out, a, b, start=first and n == 0, stop=last and n == len(terms) - 1)
    return ins


def stage_qkv(nc, d, io, keep, scratch):
    with ExitStack() as ctx:
        st = Store(nc, ctx, "qkv")
        X, ident, qst = keep["X"], keep["ident"], keep["qst"]
        q_dram, v_dram, zero_dram = scratch["qk"], scratch["v"], scratch["zero"]
        w_raw = st.sb("w_raw", [P, d.KT, 3 * d.E])
        w_hi = st.sb("w_hi", [P, d.KT, 3 * d.E], F32R)
        w_lo = st.sb("w_lo", [P, d.KT, 3 * d.E], F32R)
        NQ = 2 * d.E // P
        qk_lo = st.sb("qk_lo", [P, 2, NQ, d.CH], F32R)
        v_st = [st.sb("v_st", [P, d.TPC, d.H, 32])[:],
                keep["tern"][:].rearrange("p a n -> p (a n)").bitcast(F32)
                .rearrange("p (t h c) -> p t h c", t=d.TPC, h=d.H)]
        xn = st.sb("xn", [P, 2, d.TPC, d.E])
        xt_hi = st.sb("xt_hi", [P, 2, d.KT, d.CH], F32R)
        xt_lo = st.sb("xt_lo", [P, 2, d.KT, d.CH], F32R)
        VG = d.H // d.G
        qk_hi = keep["AO"][:].bitcast(F32R).rearrange("p (c j a) e -> p c j (a e)", c=2, j=NQ)
        lam_in = xn[0:1, 1]
        lam_pr = st.sb("lam_pr", [1, 2, d.E])
        lam = st.sb("lam", [1, 8])
        row = st.sb("row", [1, P])
        one = st.sb("one", [1, 2])
        qs = st.sb("qs", [P, 2])
        w = [NormWork(st, d.TPC, str(i)) for i in range(2)]
        ps_t = st.ps("ps_t", [P, d.KT, d.CH])
        ps_q = st.ps("ps_q", [P, NQ, d.CH])
        ps_v = st.ps("ps_v", [P, 2, 2, d.E])

        x_in = [st.sem(f"x_in{c}") for c in range(d.NC)]
        w_in, lam_s = st.sem("w_in"), st.sem("lam_in")
        dv, gp, w_hi_ok, w_lo_ok = st.sem("dv"), st.sem("gp"), st.sem("w_hi_ok"), st.sem("w_lo_ok")
        dots, exps, row_ok, col_ok, qs_ok = (st.sem(n) for n in ("dots", "exps", "row_ok", "col_ok", "qs_ok"))
        xn_ok, xt_ps, hi_ok, lo_ok = (st.sem(n) for n in ("xn_ok", "xt_ps", "hi_ok", "lo_ok"))
        qk_ps, qk_hi_ok, qk_lo_ok = (st.sem(n) for n in ("qk_ps", "qk_hi_ok", "qk_lo_ok"))
        qk_out, v_out = scratch["qk_out"], scratch["v_out"]
        v_ps, v_ok, v_init, pad_ok, z_out = (st.sem(n) for n in ("v_ps", "v_ok", "v_init", "pad_ok", "z_out"))
        id_ok, stack_in = st.sem("id_ok"), st.sem("stack_in")
        HD2 = d.HD // 2
        scale = float(HD2) ** -0.5

        x_tiles = io["L0_attn_x"].rearrange("b (t p) e -> p (b t) e", p=P)
        def halves(k, part):
            src = w_raw[:, k, 0:2 * d.E].rearrange("p (a z h e) -> p z h a e", a=2, z=2, e=HD2)[:, part]
            return [src] + [x[:, k, part * d.E:(part + 1) * d.E].rearrange("p (h a e) -> p h a e", a=2, e=HD2)
                            for x in (w_hi, w_lo)]

        with nc.Block() as block:
            @block.sync
            def _(sp):
                for c in range(d.NC):
                    sl = slice(c * d.TPC, (c + 1) * d.TPC)
                    sp.dma_start(X[:, sl, :], x_tiles[:, sl, :]).then_inc(x_in[c], 16)
                    if c == 0:
                        sp.dma_start(w_raw[:], io["L0_attn_W_attn"].rearrange("(k p) n -> p k n", p=P))\
                            .then_inc(w_in, 16)
                        for n, name in enumerate(("q1", "k1", "q2", "k2")):
                            sp.dma_start(lam_in[:, n, :],
                                         io["L0_attn_lambda_" + name].rearrange("(a e) -> a e", a=1))\
                                .then_inc(lam_s, 16)
                sp.wait_ge(pad_ok, 1)
                sp.dma_start(zero_dram, as_f32(qst[0][64:66]).rearrange("r h t -> r (h t)")).then_inc(z_out, 16)
                for c in range(d.NC):
                    b, t0 = c * d.CH // d.S, c * d.CH % d.S
                    for j in range(NQ):
                        sp.wait_ge(qk_lo_ok, NQ * c + j + 1)
                        sp.wait_ge(qk_hi_ok, NQ * c + j + 1)
                        for part, src in ((0, qk_hi), (1, qk_lo)):
                            sp.dma_start(q_dram[part, b, P * j:P * (j + 1), t0:t0 + d.CH],
                                         as_f32(src[:, c % 2, j, :])).then_inc(qk_out[c % 2], 16)
                    sp.wait_ge(v_ok, 2 * (c + 1))
                    for g in range(VG):
                        sp.dma_start(v_dram[b, g, :, t0 // P:t0 // P + d.TPC, :],
                                     v_st[c % 2][:, :, d.G * g:d.G * (g + 1), :].rearrange("p t h c -> p t (h c)"))\
                            .then_inc(v_out[c % 2], 16)
                    if c == d.S // d.CH - 1:
                        sp.wait_ge(z_out, 16)
                        for i in range(d.S // d.CH):
                            sp.wait_ge(qk_out[i], 32 * NQ)
                        load_stack(d, keep, scratch, 0, sp, stack_in)
                sp.wait_ge(stack_in, 16 * STACK_LOADS)

            @block.gpsimd
            def _(pool):
                link = chain(pool, gp)
                link(nc.gpsimd.memset(ident[:], 0.0))
                nc.gpsimd.affine_select(out=ident[:], in_=ident[:], compare_op=ALU.not_equal, fill=1.0, base=0,
                                        pattern=[[-1, P]], channel_multiplier=1).then_inc(id_ok, 1)
                pool.wait_ge(id_ok, 1)
                for i in range(2):
                    link(nc.gpsimd.memset(v_st[i], 0.0))
                    nc.gpsimd.memset(v_st[i][:, :, :, d.HD:d.HD + 1], 1.0).then_inc(v_init, 1)
                    pool.wait_ge(v_init, i + 1)
                for i in range(len(qst) - 1):
                    pad(nc, link, keep, i).then_inc(pad_ok, 1)
                    pool.wait_ge(pad_ok, i + 1)

            @block.vector
            def _(dve):
                link = chain(dve, dv)

                def normal(c):
                    dve.wait_ge(x_in[c], 16)
                    norm_stats(nc, dve, link, w[c % 2], [X[:, d.TPC * c + j, :] for j in range(d.TPC)], c // 2 + 1)
                    if c >= 2:
                        dve.wait_ge(xt_ps, d.KT * (c - 1))
                    for j in range(d.TPC):
                        ins = norm_apply(nc, w[c % 2], j, xn[:, c % 2, j, :], X[:, d.TPC * c + j, :])
                    ins.then_inc(xn_ok, 1)

                def low(c):
                    for k in range(d.KT):
                        dve.wait_ge(hi_ok, d.KT * c + k + 1)
                        nc.vector.tensor_tensor(xt_lo[:, c % 2, k, :], ps_t[:, k, :],
                                                as_f32(xt_hi[:, c % 2, k, :]), ALU.subtract).then_inc(lo_ok, 1)

                def low_qk(c):
                    for j in range(NQ):
                        dve.wait_ge(qk_hi_ok, NQ * c + j + 1)
                        if c >= 2:
                            dve.wait_ge(qk_out[c % 2], 32 * NQ * (c // 2))
                        if j < NQ // 2:
                            nc.vector.scalar_tensor_tensor(
                                out=qk_lo[:, c % 2, j, :], in0=ps_q[:, j, :], scalar=qs[:, 0:1],
                                in1=as_f32(qk_hi[:, c % 2, j, :]), op0=ALU.mult, op1=ALU.subtract)\
                                .then_inc(qk_lo_ok, 1)
                        else:
                            nc.vector.tensor_tensor(qk_lo[:, c % 2, j, :], ps_q[:, j, :],
                                                    as_f32(qk_hi[:, c % 2, j, :]), ALU.subtract).then_inc(qk_lo_ok, 1)

                nc.vector.memset(one[:], 1.0)
                link(nc.vector.memset(row[:], 1.0))
                normal(0)
                dve.wait_ge(lam_s, 64)
                link(nc.vector.tensor_tensor(lam_pr[:], lam_in[:, 0::2, :], lam_in[:, 1::2, :], ALU.mult))
                nc.vector.reduce_sum(lam[0:1, 0:2], lam_pr[:], AX.X).then_inc(dots, 1)
                for k in range(d.KT):
                    dve.wait_ge(w_hi_ok, k + 1)
                    for part in range(2):
                        src, hi, lo = halves(k, part)
                        for a in range(2):
                            nc.vector.tensor_tensor(lo[:, :, a], src[:, :, a], as_f32(hi)[:, :, a], ALU.subtract)
                    nc.vector.tensor_tensor(w_lo[:, k, 2 * d.E:], w_raw[:, k, 2 * d.E:], as_f32(w_hi[:, k, 2 * d.E:]),
                                            ALU.subtract).then_inc(w_lo_ok, 1)
                low(0)
                dve.wait_ge(exps, 1)
                link(nc.vector.tensor_tensor(lam[0:1, 4:5], lam[0:1, 2:3], lam[0:1, 3:4], ALU.subtract))
                link(nc.vector.tensor_scalar(lam[0:1, 5:6], lam[0:1, 4:5], LAMBDA_INIT, -scale, ALU.add, ALU.mult))
                r = row[0:1, :].rearrange("p (h a e) -> p a h e", a=2, e=HD2)
                nc.vector.tensor_scalar(r[:, 1], r[:, 1], lam[0:1, 5:6], None, ALU.mult)
                nc.vector.tensor_scalar(r[:, 0], r[:, 0], scale, None, ALU.mult).then_inc(row_ok, 1)
                dve.wait_ge(col_ok, 1)
                nc.vector.tensor_copy(qs[:, 0:1], ps_v[:, 0, 0, 0:1]).then_inc(qs_ok, 1)
                dve.wait_ge(qs_ok, 1)
                for c in range(d.NC):
                    if c + 1 < d.NC:
                        normal(c + 1)
                    low_qk(c)
                    if c + 1 < d.NC:
                        low(c + 1)

            @block.scalar
            def _(act):
                def high(c):
                    for k in range(d.KT):
                        act.wait_ge(xt_ps, d.KT * c + k + 1)
                        if c >= 2:
                            act.wait_ge(v_ps, 2 * (c - 1))
                        nc.scalar.activation(xt_hi[:, c % 2, k, :], ps_t[:, k, :], ACT.Copy).then_inc(hi_ok, 1)

                norm_root(nc, act, w[0], 1)
                act.wait_ge(w_in, 16)
                for k in range(d.KT):
                    for part in range(2):
                        src, hi, _ = halves(k, part)
                        nc.scalar.activation(hi, src, ACT.Copy)
                    nc.scalar.activation(w_hi[:, k, 2 * d.E:], w_raw[:, k, 2 * d.E:], ACT.Copy).then_inc(w_hi_ok, 1)
                high(0)
                act.wait_ge(dots, 1)
                nc.scalar.activation(lam[0:1, 2:4], lam[0:1, 0:2], ACT.Exp).then_inc(exps, 1)
                for c in range(d.NC):
                    if c + 1 < d.NC:
                        norm_root(nc, act, w[(c + 1) % 2], (c + 1) // 2 + 1)
                    if c == 0:
                        act.wait_ge(qs_ok, 1)
                    for j in range(NQ):
                        act.wait_ge(qk_ps, NQ * c + j + 1)
                        if c >= 2:
                            act.wait_ge(qk_out[c % 2], 32 * NQ * (c // 2))
                        nc.scalar.activation(qk_hi[:, c % 2, j, :], ps_q[:, j, :], ACT.Copy,
                                             scale=qs[:, 0:1] if j < NQ // 2 else 1.0).then_inc(qk_hi_ok, 1)
                    if c + 1 < d.NC:
                        high(c + 1)
                    for j in range(2):
                        act.wait_ge(v_ps, 2 * c + j + 1)
                        if c < 2:
                            act.wait_ge(v_init, c + 1)
                        else:
                            act.wait_ge(v_out[c % 2], 16 * VG * (c // 2))
                        nc.scalar.activation(v_st[c % 2][:, 2 * j:2 * j + 2, :, 0:d.HD],
                                             ps_v[:, j, :, :].rearrange("p t (h e) -> p t h e", e=d.HD),
                                             ACT.Copy).then_inc(v_ok, 1)

            @block.tensor
            def _(pe):
                def turn(c):
                    pe.wait_ge(xn_ok, c + 1)
                    if c >= 1:
                        pe.wait_ge(lo_ok, d.KT * c)
                    for k in range(d.KT):
                        for j in range(d.TPC):
                            ins = nc.tensor.transpose(ps_t[:, k, j * P:(j + 1) * P],
                                                      xn[:, c % 2, j, k * P:(k + 1) * P], ident[:])
                        ins.then_inc(xt_ps, 1)

                pe.wait_ge(id_ok, 1)
                turn(0)
                pe.wait_ge(row_ok, 1)
                nc.tensor.matmul(ps_v[:, 0, 0, 0:1], row[0:1, :], one[0:1, 0:1], start=True, stop=True)\
                    .then_inc(col_ok, 1)
                pe.wait_ge(w_lo_ok, d.KT)
                for c in range(d.NC):
                    pe.wait_ge(lo_ok, d.KT * (c + 1))
                    for j in range(NQ):
                        if c >= 1:
                            pe.wait_ge(qk_lo_ok, NQ * (c - 1) + j + 1)
                        for k in range(d.KT):
                            cols = slice(j * P, (j + 1) * P)
                            ins = mm_split(nc, ps_q[:, j, :], w_hi[:, k, cols], w_lo[:, k, cols],
                                           xt_hi[:, c % 2, k, :], xt_lo[:, c % 2, k, :], k == 0, k == d.KT - 1)
                        ins.then_inc(qk_ps, 1)
                    if c + 1 < d.NC:
                        turn(c + 1)
                    for j in range(2):
                        if c == 0:
                            pe.wait_ge(qs_ok, 1)
                        else:
                            pe.wait_ge(v_ok, 2 * (c - 1) + j + 1)
                        for i in range(2):
                            t = slice((2 * j + i) * P, (2 * j + i + 1) * P)
                            for k in range(d.KT):
                                ins = mm_split(nc, ps_v[:, j, i, :], xt_hi[:, c % 2, k, t], xt_lo[:, c % 2, k, t],
                                               w_hi[:, k, 2 * d.E:], w_lo[:, k, 2 * d.E:], k == 0, k == d.KT - 1)
                        ins.then_inc(v_ps, 1)
        st.clear()


STACK_LOADS = 7


def load_stack(d, keep, scratch, g, sp, sem):
    b, h0 = g // (d.NG // d.B), g % (d.NG // d.B) * d.G
    qst, kst = keep["qst"][g % len(keep["qst"])], keep["kst"][g % len(keep["kst"])]
    for base, dst, parts in ((0, qst, (0, 1, 0)), (d.E, kst, (0, 0, 1))):
        for n, part in enumerate(parts):
            src = scratch["qk"][part, b, base + h0 * d.HD:base + (h0 + d.G) * d.HD, :]
            sp.dma_start(as_f32(dst[n * d.HD:(n + 1) * d.HD, :, :]),
                         src.rearrange("(h e) t -> e h t", e=d.HD)).then_inc(sem, 16)
    sp.dma_start(as_f32(qst[3 * d.HD:3 * d.HD + 2, :, :]), scratch["zero"].rearrange("r (h t) -> r h t", h=d.G))\
        .then_inc(sem, 16)


def pad(nc, link, keep, i):
    qst, kst = keep["qst"][i], keep["kst"][i]
    link(nc.gpsimd.memset(as_f32(qst[64:P, :, :]), 0.0))
    link(nc.gpsimd.memset(as_f32(kst[64:P, :, :]), 0.0))
    link(nc.gpsimd.memset(as_f32(qst[32:64, :, :]), 0.0))
    return nc.gpsimd.memset(as_f32(kst[32:64, :, :]), 1.0)


def stage_attention(nc, d, io, keep, scratch):
    with ExitStack() as ctx:
        st = Store(nc, ctx, "att")
        AO, ident, qst, kst, tern, sc = (keep[n] for n in ("AO", "ident", "qst", "kst", "tern", "sc"))
        NS = d.S // P
        NB = d.S // d.CH
        HD, G = d.HD, d.G
        RING = len(qst)
        LEAD = 6
        SUM_AT, TURN_AT = 34, (64, 71)
        vst = [st.sb(f"vst{i}", [P, NS, G * 32]) for i in range(RING)]
        prob = st.sb("prob", [P, RING, G, d.S])
        mx = st.sb("mx", [P, 2, G * NS, NB])
        nm = st.sb("nm", [P, G * NS])
        nmt = st.sb("nmt", [P, G * NS])
        nm_hi = st.sb("nm_hi", [P, 2, G * NS], F32R)
        nm_lo = st.sb("nm_lo", [P, 2, G * NS], F32R)
        osb = st.sb("osb", [P, NB, d.CH])
        rs = st.sb("rs", [P, NB, d.TPC * G])
        BANKS = 3
        ps_s = st.ps("ps_s", [P, BANKS, d.CH])
        ps_m = st.ps("ps_m", [P, BANKS, d.CH])
        ps_o = st.ps("ps_o", [P, NB, d.CH])
        pad_ok, gp = st.sem("pad_ok"), st.sem("gp")
        load = [st.sem(f"load{i}") for i in range(RING)]
        nm_in = [st.sem(f"nm_in{i}") for i in range(2)]
        m_ps, m_rd, nm_ok = st.sem("m_ps"), st.sem("m_rd"), st.sem("nm_ok")
        sc_ps, exp_ok, pv_ok = st.sem("sc_ps"), st.sem("exp_ok"), st.sem("pv_ok")
        o_rd, dv = st.sem("o_rd"), st.sem("dv")
        spare = prob[:].rearrange("p r h t -> p (r h t)").rearrange("p (i n) -> p i n", n=d.KT * d.N)
        ones = spare[:, 4, 0:P]
        abs_sum = st.sb("abs_sum", [P, 2])
        lim = st.sb("lim", [P, 2, 2])
        wt_in = [st.sem(f"wt_in{i}") for i in range(2)]
        ones_ok, sum_ok, sum_ps, sc_ok, tern_ok, tern_ps, tern_rd = (
            st.sem(n) for n in ("ones_ok", "sum_ok", "sum_ps", "sc_ok", "tern_ok", "tern_ps", "tern_rd"))
        lim_ok, cmp_ok = st.sem("lim_ok"), st.sem("cmp_ok")
        TB = d.KT * d.N // d.CH
        UPG = NS * G
        MPG = G * NS * NB
        MPU = MPG // UPG
        UN = UPG * d.NG
        LOADS = STACK_LOADS + 1
        NMD = 8

        side = {u: [] for u in range(-1, UN + 2 * G + 3)}
        for g in range(d.NG):
            for m in range(MPG):
                side[max(-1, UPG * (g - 1) - LEAD + m // MPU)].append(("max", g, m))
            for t in range(NB):
                side[UPG * (g + 1) + G + 2 + t].append(("out", g, t))
        items = [(u, x) for u in side for x in side[u]]

        def loaded(g):
            return 16 * (LOADS * (g // RING + 1) - (STACK_LOADS if g % RING == 0 else 0))

        def ready(kind, g, m):
            return [x for _, x in items].index((kind, g, m)) + 1

        with nc.Block() as block:
            @block.sync
            def _(sp):
                def load_group(g):
                    i = g % RING
                    if g == RING - 1:
                        sp.wait_ge(pad_ok, 1)
                    elif g >= RING:
                        sp.wait_ge(pv_ok, NS * NB * (g - RING + 1))
                    if g:
                        load_stack(d, keep, scratch, g, sp, load[i])
                    sp.dma_start(vst[i][:], scratch["v"][g // (d.NG // d.B), g % (d.NG // d.B)]).then_inc(load[i], 16)

                for i in range(2):
                    sp.wait_ge(scratch["qk_out"][i], 16 * (2 * d.E // P) * d.NC)
                    sp.wait_ge(scratch["v_out"][i], 16 * (d.H // d.G) * d.NC // 2)
                load_group(0)
                for i, name in enumerate(("W_syn", "W_out")):
                    sp.dma_start(spare[:, i, :].rearrange("p (a n) -> p a n", n=d.E if i == 0 else d.N),
                                 io["L0_ffn_" + name].rearrange("(a p) n -> p a n", p=P)).then_inc(wt_in[i], 16)
                load_group(1)
                for g in range(d.NG):
                    sp.wait_ge(nm_ok, g + 1)
                    for r, src in ((3 * HD, nm_hi), (3 * HD + 1, nm_lo)):
                        for q in range(4):
                            dst = qst[g % RING][r:r + 1, :, :].rearrange("p h (t q j) -> p (h t) q j", q=4, j=32)
                            sp.dma_start(as_f32(dst[:, :, q]), as_f32(src[32 * q:32 * q + 32, g % 2, :]))\
                                .then_inc(nm_in[g % 2], 16)
                    if g + 2 < d.NG:
                        load_group(g + 2)

            @block.gpsimd
            def _(pool):
                link = chain(pool, gp)
                nc.gpsimd.memset(ones, 1.0).then_inc(ones_ok, 1)
                pool.wait_ge(sc_ok, 1)
                link(nc.gpsimd.tensor_scalar(lim[:, 0, :], sc[:], 1e-8, 0.5, ALU.add, ALU.mult))
                nc.gpsimd.tensor_scalar(lim[:, 1, :], lim[:, 0, :], -1.0, None, ALU.mult).then_inc(lim_ok, 1)
                pool.wait_ge(lim_ok, 1)
                link(nc.gpsimd.tensor_scalar(spare[:, 2, :], spare[:, 1, :], lim[:, 0, 1:2], None, ALU.is_gt))
                link(nc.gpsimd.tensor_scalar(spare[:, 3, :], spare[:, 1, :], lim[:, 1, 1:2], None, ALU.is_lt))
                pool.wait_ge(cmp_ok, 4)
                for i, c in ((0, 4), (1, 2)):
                    nc.gpsimd.tensor_tensor(spare[:, i, :], spare[:, c, :], spare[:, c + 1, :], ALU.subtract)\
                        .then_inc(tern_ok, 1)
                    pool.wait_ge(tern_ok, i + 1)
                pad(nc, link, keep, RING - 1).then_inc(pad_ok, 1)

            @block.tensor
            def _(pe):
                done = [0]

                def side_unit(kind, g, m):
                    n = done[0]
                    done[0] += 1
                    if n >= BANKS:
                        pe.wait_ge(m_rd, n - BANKS + 1)
                    if kind == "max":
                        h, t, half = m // (NS * NB), m // NB % NS, m % NB
                        if m == 0 and g:
                            pe.wait_ge(load[g % RING], loaded(g))
                        nc.tensor.matmul(ps_m[:, n % BANKS, :], qst[g % RING][:, h, t * P:(t + 1) * P],
                                         kst[g % RING][:, h, half * d.CH:(half + 1) * d.CH],
                                         start=True, stop=True).then_inc(m_ps, 1)
                    else:
                        pe.wait_ge(o_rd, NB * g + m + 1)
                        for j in range(d.TPC):
                            ins = nc.tensor.transpose(ps_m[:, n % BANKS, j * P:(j + 1) * P],
                                                      osb[:, m, j * P:(j + 1) * P], ident[:])
                        ins.then_inc(m_ps, 1)

                def score_unit(u, t):
                    g, s, h = u // UPG, u // G % NS, u % G
                    n = NB * u + t
                    if u % UPG == 0 and t == 0:
                        pe.wait_ge(nm_in[g % 2], 16 * NMD * (g // 2 + 1))
                    if n < BANKS:
                        pe.wait_ge(tern_rd, 2 * TB)
                    else:
                        pe.wait_ge(exp_ok, n - BANKS + 1)
                    nc.tensor.matmul(ps_s[:, n % BANKS, :], kst[g % RING][:, h, s * P:(s + 1) * P],
                                     qst[g % RING][:, h, t * d.CH:(t + 1) * d.CH], start=True, stop=True)\
                        .then_inc(sc_ps, 1)

                def value_unit(n, t):
                    g, s = n // NS, n % NS
                    pe.wait_ge(exp_ok, NB * G * (n + 1))
                    if n == 0:
                        pe.wait_ge(load[0], loaded(0))
                    if s == 0 and g >= 1:
                        pe.wait_ge(o_rd, NB * (g - 1) + t + 1)
                    for h in range(G):
                        ins = nc.tensor.matmul(ps_o[32 * h:32 * h + 32, t, :],
                                               vst[g % RING][:, s, 32 * h:32 * h + 32],
                                               prob[:, n % RING, h, t * d.CH:(t + 1) * d.CH],
                                               start=s == 0, stop=s == NS - 1)
                    ins.then_inc(pv_ok, 1)

                def weight_sum():
                    pe.wait_ge(ones_ok, 1)
                    pe.wait_ge(sum_ok, 2)
                    nc.tensor.matmul(ps_s[:, 0, 0:2], ones, abs_sum[:], start=True, stop=True).then_inc(sum_ps, 1)

                def turn_weight(i, k):
                    n = TB * i + k
                    pe.wait_ge(tern_ok, i + 1)
                    pe.wait_ge(sc_ok, 1)
                    if n >= BANKS:
                        pe.wait_ge(tern_rd, n - BANKS + 1)
                    for j in range(d.TPC):
                        q = d.TPC * k + j
                        if i == 0:
                            m, a = q // (d.N // P), q % (d.N // P)
                            src = spare[:, 0, a * d.E + m * P:a * d.E + (m + 1) * P]
                        else:
                            a, m = q // d.KT, q % d.KT
                            src = spare[:, 1, m * d.N + a * P:m * d.N + (a + 1) * P]
                        ins = nc.tensor.transpose(ps_s[:, n % BANKS, j * P:(j + 1) * P], src, ident[:])
                    ins.then_inc(tern_ps, 1)

                prologue = {SUM_AT: weight_sum}
                for i in range(2):
                    for k in range(TB):
                        prologue[TURN_AT[i] + k] = lambda i=i, k=k: turn_weight(i, k)
                for n, x in enumerate(side.pop(-1)):
                    side_unit(*x)
                    if n in prologue:
                        prologue[n]()
                for u in side:
                    todo = side[u]
                    for t in range(NB):
                        for x in todo[:1]:
                            side_unit(*x)
                        if u < UN:
                            score_unit(u, t)
                        todo = todo[1:]
                    for x in todo:
                        side_unit(*x)
                    if u > G and u % G in (1, 3) and u // G - 1 < UN // G:
                        value_unit(u // G - 1, u % G // 2)

            @block.scalar
            def _(act):
                for i in range(2):
                    act.wait_ge(wt_in[i], 16)
                    nc.scalar.activation(spare[:, 2 + i, :], spare[:, i, :], ACT.Abs, accum_out=abs_sum[:, i:i + 1])\
                        .then_inc(sum_ok, 1)
                act.wait_ge(sum_ps, 1)
                nc.scalar.activation(sc[:], ps_s[:, 0, 0:2], ACT.Copy, scale=1.0 / (d.N * d.E)).then_inc(sc_ok, 1)
                act.wait_ge(lim_ok, 1)
                for j, sign in ((4, 1.0), (5, -1.0)):
                    nc.scalar.activation(spare[:, j, :], spare[:, 0, :], ACT.Sign, bias=lim[:, 1, 0:1], scale=sign)\
                        .then_inc(cmp_ok, 1)
                for j in (4, 5):
                    act.wait_ge(cmp_ok, j - 3)
                    nc.scalar.activation(spare[:, j, :], spare[:, j, :], ACT.Relu).then_inc(cmp_ok, 1)
                for n in range(2 * TB):
                    act.wait_ge(tern_ps, n + 1)
                    k = n % TB
                    nc.scalar.activation(tern[:, n // TB, k * d.CH:(k + 1) * d.CH], ps_s[:, n % BANKS, :], ACT.Copy)\
                        .then_inc(tern_rd, 1)
                for u in range(UN + G + 3):
                    s, h = u // G, u % G
                    if h == 0 and RING <= s < UN // G:
                        act.wait_ge(pv_ok, NB * (s - RING + 1))
                    for t in range(NB if u < UN else 0):
                        n = NB * u + t
                        act.wait_ge(sc_ps, n + 1)
                        nc.scalar.activation(prob[:, s % RING, h, t * d.CH:(t + 1) * d.CH], ps_s[:, n % BANKS, :],
                                             ACT.Exp).then_inc(exp_ok, 1)
                    if u > UPG and u % UPG in (2, 4):
                        g, t = u // UPG - 1, u % UPG // 2 - 1
                        act.wait_ge(pv_ok, NB * (NS * (g + 1) - 1) + t + 1)
                        if g >= 1:
                            act.wait_ge(m_rd, ready("out", g - 1, t))
                        nc.scalar.activation(osb[:, t, :], ps_o[:, t, :], ACT.Copy).then_inc(o_rd, 1)

            @block.vector
            def _(dve):
                link = chain(dve, dv)

                def finish_max(g):
                    link(nc.vector.tensor_reduce(nm[:], mx[:, g % 2], AX.X, ALU.max, negate=True))
                    link(nc.vector.transpose(nmt[:], nm[:]))
                    if g >= 2:
                        dve.wait_ge(nm_in[g % 2], 16 * NMD * (g // 2))
                    link(nc.vector.tensor_copy(nm_hi[:, g % 2, :], nmt[:]))
                    nc.vector.tensor_tensor(nm_lo[:, g % 2, :], nmt[:], as_f32(nm_hi[:, g % 2, :]),
                                            ALU.subtract).then_inc(nm_ok, 1)

                for n, (_, (kind, g, m)) in enumerate(items):
                    dve.wait_ge(m_ps, n + 1)
                    if kind == "max":
                        nc.vector.reduce_max(mx[:, g % 2, m // NB, m % NB:m % NB + 1], ps_m[:, n % BANKS, :], AX.X)\
                            .then_inc(m_rd, 1)
                        if m == MPG - 1:
                            dve.wait_ge(m_rd, n + 1)
                            finish_max(g)
                    else:
                        b, h0, t0 = g // (d.NG // d.B), g % (d.NG // d.B) * G, m * d.TPC
                        o = ps_m[:, n % BANKS, :].rearrange("p (j h e) -> p j h e", h=G, e=32)
                        r = rs[:, m, :].rearrange("p (j h) -> p j h", h=G)
                        link(nc.vector.reciprocal(r, o[:, :, :, HD]))
                        link(nc.vector.tensor_scalar(r, r, 1.0 - LAMBDA_INIT, None, ALU.mult))
                        dst = AO[:, b * NS + t0:b * NS + t0 + d.TPC, h0 * HD:(h0 + G) * HD]
                        nc.vector.tensor_tensor(dst.rearrange("p j (h e) -> p j h e", e=HD), o[:, :, :, 0:HD],
                                                r.unsqueeze(3).to_broadcast([P, d.TPC, G, HD]),
                                                ALU.mult).then_inc(m_rd, 1)


def stage_mlp(nc, d, io, keep):
    with ExitStack() as ctx:
        st = Store(nc, ctx, "mlp")
        X, AO, ident, sc = (keep[n] for n in ("X", "AO", "ident", "sc"))
        tern = keep["tern"]
        KEEP = max(1, int(d.N * (1.0 - 0.9)))
        NN = d.N // P
        NH = d.N // d.CH
        TPC = d.TPC
        ROUNDS = 4
        AIM = KEEP - 4.0
        SPREAD0, SLOPE = 1.3095, 173.0
        DEPTH = 4
        XN = st.sb("xn", [P, d.NT, d.E])
        Z = st.sb("z", [P, d.NT, d.N])
        ws_t = st.sb("ws_t", [P, d.KT * d.N], F32R)
        wo_t = st.sb("wo_t", [P, d.KT * d.N])
        wp = st.sb("wp", [P, d.KT, d.E])
        bs_hi = st.sb("bs_hi", [P, d.N], F32R)
        bs_lo = st.sb("bs_lo", [P, d.N], F32R)
        vecs = st.sb("vecs", [P, 3, d.E])
        ones = st.sb("ones", [P, P])
        share = st.sb("share", [P, P], F32R)
        at = st.sb("at", [P, d.KT, d.CH])
        xt_hi = st.sb("xt_hi", [P, d.KT, d.CH], F32R)
        xt_lo = st.sb("xt_lo", [P, d.KT, d.CH], F32R)
        zst = st.sb("zst", [P, TPC, NH, 6])
        zmv = st.sb("zmv", [P, TPC, 2])
        zsd = st.sb("zsd", [P, d.NT])
        lev = st.sb("lev", [P, d.NT])
        nlev = st.sb("nlev", [P, d.NT])
        sgn = st.sb("sgn", [P, d.NT])
        cnt = st.sb("cnt", [P, d.NT])
        lo, hi, clo, chi = (st.sb(n, [P, d.NT]) for n in ("lo", "hi", "clo", "chi"))
        missed = st.sb("missed", [P, d.NT])
        t1, t2, t3, msk = (st.sb(n, [P, TPC]) for n in ("t1", "t2", "t3", "msk"))
        junk = st.sb("junk", [P, 2, d.N], mybir.dt.bfloat16)
        below = st.sb("below", [P, 2, d.N])
        hid = st.sb("hid", [P, 2, d.N])
        ht = st.sb("ht", [P, TPC, d.N])
        top = st.sb("top", [P, d.NT, 8])
        pick = st.sb("pick", [P, TPC, 8])
        iota8 = st.sb("iota8", [P, 8])
        iota_i = st.sb("iota_i", [P, 8], mybir.dt.int32)
        thr = st.sb("thr", [P, d.NT])
        flag = st.sb("flag", [P, 2])
        flag_i = st.sb("flag_i", [P, 1], mybir.dt.int32)
        y = st.sb("y", [P, TPC, d.E])
        w1, w2 = NormWork(st, TPC, "1"), NormWork(st, TPC, "2")
        ps_t = st.ps("ps_t", [P, d.KT, d.CH])
        ps_p = st.ps("ps_p", [P, 2, d.CH])
        ps_z = st.ps("ps_z", [P, 2, d.N])

        w_in = [st.sem(f"w_in{i}") for i in range(3)]
        dv, on = st.sem("dv"), st.sem("on")
        gp = st.sem("gp")
        bs_h, bs_ok, ws_ok, wo_ok = (st.sem(n) for n in ("bs_h", "bs_ok", "ws_ok", "wo_ok"))
        at_ps, at_ok, pr_ps, xn_ok, t_ps, hi_ok, lo_ok = (
            st.sem(n) for n in ("at_ps", "at_ok", "pr_ps", "xn_ok", "t_ps", "hi_ok", "lo_ok"))
        ring_ps, ring_rd = st.sem("ring_ps"), st.sem("ring_rd")
        zvar, zroot, lev_ok, cnt_ok = (st.sem(n) for n in ("zvar", "zroot", "lev_ok", "cnt_ok"))
        flag_ok, any_ps, hid_ok, o_ps, o_rd = (st.sem(n) for n in ("flag_ok", "any_ps", "hid_ok", "o_ps", "o_rd"))
        xb_ok, y_ok, x_ok = st.sem("xb_ok"), st.sem("y_ok"), st.sem("x_ok")

        ring = []
        for s in range(d.NC + DEPTH - 1):
            for j0 in (0, 2):
                ring += [(kind, TPC * c + j) for kind, c in (("h", s - 3), ("z", s)) for j in (j0, j0 + 1)
                         if 0 <= c < d.NC]

        def nth(kind, i):
            return ring.index((kind, i)) + 1

        def steps(s):
            return [c if 0 <= c < d.NC else None for c in (s, s - 1, s - 2, s - 3)]

        def out_bank(t):
            last_two = t // TPC + DEPTH - 1 >= d.NC and t % TPC >= 2
            return (ps_t if last_two else ps_p)[:, t % 2, 0:d.E]

        with nc.Block() as block:
            @block.sync
            def _(sp):
                sp.dma_start(wp[:], io["L0_attn_W_proj"].rearrange("(k p) n -> p k n", p=P)).then_inc(w_in[0], 16)
                sp.dma_start(below[:, 0, :], io["L0_ffn_b_syn"].rearrange("(a n) -> a n", a=1)
                             .to_broadcast([P, d.N])).then_inc(w_in[1], 16)
                for i, name in enumerate(("b_out", "gamma", "beta")):
                    src = io["L0_ffn_" + name].rearrange("(a n) -> a n", a=1)
                    sp.dma_start(vecs[:, i, :], src.to_broadcast([P, d.E])).then_inc(w_in[2], 16)

            @block.gpsimd
            def _(pool):
                link = chain(pool, gp)
                nc.gpsimd.tensor_copy(wo_t[:], tern[:, 1, :]).then_inc(wo_ok, 1)
                pool.wait_ge(wo_ok, 1)
                link(nc.gpsimd.memset(ones[:], 1.0))
                link(nc.gpsimd.iota(iota_i[:], pattern=[[1, 8]], base=0, channel_multiplier=0))
                nc.gpsimd.memset(as_f32(share[:]), 1.0 / P).then_inc(on, 1)
                pool.wait_ge(w_in[2], 48)
                for s in range(d.NC + DEPTH - 1):
                    enter, _, _, leave = steps(s)
                    if enter is not None:
                        pool.wait_ge(t_ps, d.KT * (enter + 1))
                        for j in range(TPC):
                            t = TPC * enter + j
                            ins = nc.gpsimd.tensor_tensor(XN[:, t, :], XN[:, t, :], vecs[:, 0, :], ALU.add)
                        ins.then_inc(xb_ok, 1)
                    if leave is not None and leave < d.NC - 1:
                        pool.wait_ge(y_ok, leave + 1)
                        for j in range(TPC):
                            ins = nc.gpsimd.tensor_tensor(y[:, j, :], y[:, j, :], vecs[:, 1, :], ALU.mult)
                        link(ins)
                        for j in range(TPC):
                            ins = nc.gpsimd.tensor_tensor(y[:, j, :], y[:, j, :], vecs[:, 2, :], ALU.add)
                        link(ins)
                        for j in range(TPC):
                            t = TPC * leave + j
                            ins = nc.gpsimd.tensor_tensor(X[:, t, :], X[:, t, :], y[:, j, :], ALU.add)
                        ins.then_inc(x_ok, 1)

            @block.vector
            def _(dve):
                link = chain(dve, dv)

                def residual(c):
                    dve.wait_ge(pr_ps, c + 1)
                    sl = slice(TPC * c, TPC * (c + 1))
                    link(nc.vector.tensor_tensor(X[:, sl, :].rearrange("p j e -> p (j e)"),
                                                 X[:, sl, :].rearrange("p j e -> p (j e)"),
                                                 ps_t[:].rearrange("p k n -> p (k n)"), ALU.add))
                    norm_var(nc, link, w1, [X[:, TPC * c + j, :] for j in range(TPC)])

                def normal(c):
                    norm_rstd(nc, dve, link, w1, c + 1)
                    for j in range(TPC):
                        t = TPC * c + j
                        ins = norm_apply(nc, w1, j, XN[:, t, :], X[:, t, :])
                    ins.then_inc(xn_ok, 1)

                def low(c):
                    for k in range(d.KT):
                        dve.wait_ge(hi_ok, d.KT * c + k + 1)
                        nc.vector.scalar_tensor_tensor(out=xt_lo[:, k, :], in0=ps_t[:, k, :], scalar=sc[:, 0:1],
                                                       in1=as_f32(xt_hi[:, k, :]), op0=ALU.mult,
                                                       op1=ALU.subtract).then_inc(lo_ok, 1)

                def spread(t):
                    dve.wait_ge(ring_rd, nth("z", t))
                    for n in range(NH):
                        ins = nc.vector.bn_stats(zst[:, t % TPC, n, :], Z[:, t, n * d.CH:(n + 1) * d.CH])
                    return ins

                def spreads(c):
                    for j in range(TPC):
                        ins = nc.vector.bn_aggr(zmv[:, j, :], zst[:, j].rearrange("p a b -> p (a b)"))
                    ins.then_inc(zvar, 1)
                    dve.wait_ge(zvar, c + 1)

                def first_level(c):
                    cs = slice(TPC * c, TPC * (c + 1))
                    dve.wait_ge(zroot, c + 1)
                    link(nc.vector.scalar_tensor_tensor(out=lev[:, cs], in0=zsd[:, cs], scalar=SPREAD0,
                                                        in1=zmv[:, :, 0], op0=ALU.mult, op1=ALU.add))
                    nc.vector.tensor_scalar(nlev[:, cs], lev[:, cs], -1.0, None, ALU.mult).then_inc(lev_ok, 1)
                    nc.vector.scalar_tensor_tensor(out=lo[:, cs], in0=zsd[:, cs], scalar=-0.6, in1=lev[:, cs],
                                                   op0=ALU.mult, op1=ALU.add)
                    nc.vector.scalar_tensor_tensor(out=hi[:, cs], in0=zsd[:, cs], scalar=0.6, in1=lev[:, cs],
                                                   op0=ALU.mult, op1=ALU.add)
                    nc.vector.memset(clo[:, cs], 122.0)
                    link(nc.vector.memset(chi[:, cs], -68.0))

                def next_level(c, r):
                    cs = slice(TPC * c, TPC * (c + 1))
                    LEV, CNT = lev[:, cs], cnt[:, cs]
                    dve.wait_ge(cnt_ok, TPC * (ROUNDS * c + r + 1))
                    link(nc.vector.tensor_scalar(CNT, sgn[:, cs], 0.5, d.N / 2 - AIM, ALU.mult, ALU.add))
                    link(nc.vector.tensor_tensor(t1[:], CNT, CNT, ALU.mult))
                    link(nc.vector.tensor_scalar(missed[:, cs], t1[:], 16.5, None, ALU.is_gt))
                    if r == ROUNDS - 1:
                        return
                    m = msk[:].bitcast(U32)
                    link(nc.vector.tensor_scalar(msk[:], CNT, 0.0, None, ALU.is_gt))
                    nc.vector.copy_predicated(lo[:, cs], m, LEV)
                    link(nc.vector.copy_predicated(clo[:, cs], m, CNT))
                    link(nc.vector.tensor_scalar(msk[:], CNT, 0.0, None, ALU.is_le))
                    nc.vector.copy_predicated(hi[:, cs], m, LEV)
                    link(nc.vector.copy_predicated(chi[:, cs], m, CNT))
                    if r == 0:
                        link(nc.vector.scalar_tensor_tensor(out=t1[:], in0=CNT, scalar=1.0 / SLOPE, in1=zsd[:, cs],
                                                            op0=ALU.mult, op1=ALU.mult))
                        link(nc.vector.tensor_tensor(t1[:], t1[:], LEV, ALU.add))
                    else:
                        nc.vector.tensor_tensor(t1[:], clo[:, cs], chi[:, cs], ALU.subtract)
                        link(nc.vector.tensor_tensor(t2[:], hi[:, cs], lo[:, cs], ALU.subtract))
                        nc.vector.reciprocal(t3[:], t1[:])
                        link(nc.vector.tensor_tensor(t2[:], t2[:], clo[:, cs], ALU.mult))
                        link(nc.vector.tensor_tensor(t2[:], t2[:], t3[:], ALU.mult))
                        link(nc.vector.tensor_tensor(t1[:], t2[:], lo[:, cs], ALU.add))
                    link(nc.vector.copy_predicated(LEV, missed[:, cs].bitcast(U32), t1[:]))
                    nc.vector.tensor_scalar(nlev[:, cs], LEV, -1.0, None, ALU.mult).then_inc(lev_ok, 1)

                def eight(c, js):
                    for j in js:
                        t = TPC * c + j
                        ins = nc.vector.scalar_tensor_tensor(out=below[:, t % 2, :], in0=Z[:, t, :],
                                                             scalar=lev[:, t:t + 1], in1=Z[:, t, :],
                                                             op0=ALU.is_le, op1=ALU.mult)
                    link(ins)
                    for j in js:
                        t = TPC * c + j
                        ins = nc.vector.max(top[:, t, :], below[:, t % 2, :])
                    link(ins)

                def threshold(c):
                    cs = slice(TPC * c, TPC * (c + 1))
                    LEV, THR = lev[:, cs], thr[:, cs]
                    link(nc.vector.tensor_scalar(t1[:], cnt[:, cs], -1.0, KEEP - 1 - AIM, ALU.mult, ALU.add))
                    nc.vector.tensor_scalar(t2[:], t1[:], -1.0, None, ALU.is_equal)
                    link(nc.vector.tensor_tensor(pick[:], t1[:].unsqueeze(2).to_broadcast([P, TPC, 8]),
                                                 iota8[:].unsqueeze(1).to_broadcast([P, TPC, 8]), ALU.is_equal))
                    nc.vector.tensor_tensor(t2[:], t2[:], LEV, ALU.mult)
                    link(nc.vector.tensor_tensor(pick[:], pick[:], top[:, cs, :], ALU.mult))
                    nc.vector.tensor_tensor(t3[:], top[:, cs, 0], LEV, ALU.is_equal)
                    link(nc.vector.tensor_reduce(THR, pick[:], AX.X, ALU.add))
                    link(nc.vector.tensor_tensor(THR, THR, t2[:], ALU.add))
                    link(nc.vector.tensor_scalar(t2[:], LEV, 0.0, None, ALU.is_le))
                    link(nc.vector.tensor_tensor(t2[:], t2[:], t3[:], ALU.max))
                    link(nc.vector.tensor_tensor(t2[:], t2[:], missed[:, cs], ALU.max))
                    nc.vector.reduce_max(flag[:, 0:1], t2[:], AX.X).then_inc(flag_ok, 1)

                def settle(c):
                    cs = slice(TPC * c, TPC * (c + 1))
                    dve.wait_ge(any_ps, c + 1)
                    link(nc.vector.tensor_scalar(flag[:, 1:2], ps_p[:, 0, d.E:d.E + 1], 0.5, None, ALU.is_gt))
                    link(nc.vector.tensor_copy(flag_i[:], flag[:, 1:2]))
                    some = dve.value_load(flag_i[0:1, 0:1], min_val=0, max_val=1)
                    with dve.If(some):
                        general_threshold(nc, dve, TPC * c, TPC * (c + 1), Z, below, top, thr, KEEP)
                    dve.drain()
                    link(nc.vector.tensor_scalar(thr[:, cs], thr[:, cs], 0.0, None, ALU.max))

                def hidden(t):
                    if t >= 2:
                        dve.wait_ge(ring_ps, nth("h", t - 2))
                    nc.vector.scalar_tensor_tensor(out=hid[:, t % 2, :], in0=Z[:, t, :], scalar=thr[:, t:t + 1],
                                                   in1=Z[:, t, :], op0=ALU.is_ge, op1=ALU.mult).then_inc(hid_ok, 1)

                def output(t):
                    dve.wait_ge(xb_ok, t // TPC + 1)
                    dve.wait_ge(o_ps, t + 1)
                    nc.vector.scalar_tensor_tensor(out=XN[:, t, :], in0=out_bank(t), scalar=sc[:, 1:2],
                                                   in1=XN[:, t, :], op0=ALU.mult, op1=ALU.add).then_inc(o_rd, 1)

                def closing(c):
                    dve.wait_ge(o_rd, TPC * (c + 1))
                    norm_var(nc, link, w2, [XN[:, TPC * c + j, :] for j in range(TPC)])

                def closed(c):
                    norm_rstd(nc, dve, link, w2, c + 1)
                    if c >= 1:
                        dve.wait_ge(x_ok, c)
                    for j in range(TPC):
                        ins = norm_apply(nc, w2, j, y[:, j, :], XN[:, TPC * c + j, :])
                    ins.then_inc(y_ok, 1)
                    if c == d.NC - 1:
                        dve.wait_ge(y_ok, d.NC)
                        wide = lambda i: vecs[:, i, :].unsqueeze(1).to_broadcast([P, TPC, d.E])
                        sl = slice(TPC * c, TPC * (c + 1))
                        link(nc.vector.tensor_tensor(y[:], y[:], wide(1), ALU.mult))
                        link(nc.vector.tensor_tensor(y[:], y[:], wide(2), ALU.add))
                        nc.vector.tensor_tensor(X[:, sl, :], X[:, sl, :], y[:], ALU.add).then_inc(x_ok, 1)

                residual(0)
                for s in range(d.NC + DEPTH):
                    enter, count, settles, leave = steps(s)
                    if enter is not None:
                        normal(enter)
                    if leave is not None:
                        hidden(TPC * leave)
                        hidden(TPC * leave + 1)
                    if count is not None:
                        next_level(count, 0)
                    if enter is not None:
                        low(enter)
                    if leave is not None:
                        hidden(TPC * leave + 2)
                        hidden(TPC * leave + 3)
                    if s == 0:
                        dve.wait_ge(bs_h, 1)
                        nc.vector.tensor_tensor(bs_lo[:], below[:, 0, :], as_f32(bs_hi[:]), ALU.subtract)\
                            .then_inc(bs_ok, 1)
                        dve.wait_ge(on, 1)
                        link(nc.vector.tensor_copy(iota8[:], iota_i[:]))
                    if settles is not None:
                        eight(settles, (0, 1))
                    if count is not None:
                        next_level(count, 1)
                    if steps(s - 1)[3] is not None:
                        closed(steps(s - 1)[3])
                    if enter is not None:
                        spread(TPC * enter)
                        link(spread(TPC * enter + 1))
                    if leave is not None and enter is None:
                        output(TPC * leave)
                        output(TPC * leave + 1)
                    if settles is not None:
                        eight(settles, (2, 3))
                    if count is not None:
                        next_level(count, 2)
                    if leave is not None and enter is not None:
                        output(TPC * leave)
                        output(TPC * leave + 1)
                    if settles is not None:
                        threshold(settles)
                    if enter is not None:
                        spread(TPC * enter + 2)
                        link(spread(TPC * enter + 3))
                        spreads(enter)
                    if leave is not None:
                        output(TPC * leave + 2)
                    if enter is not None and enter + 1 < d.NC:
                        residual(enter + 1)
                    if count is not None:
                        next_level(count, 3)
                    if enter is not None:
                        first_level(enter)
                    if leave is not None:
                        output(TPC * leave + 3)
                    if leave is not None:
                        closing(leave)
                    if settles is not None:
                        settle(settles)

            @block.scalar
            def _(act):
                def evacuate(items):
                    for kind, i in items:
                        n = ring.index((kind, i))
                        act.wait_ge(ring_ps, n + 1)
                        src = ps_z[:, n % 2, :]
                        if kind == "z":
                            dst = Z[:, i, :]
                        else:
                            dst = ht[:, i % TPC, :]
                            if i >= TPC:
                                act.wait_ge(o_ps, i - TPC + 1)
                        nc.scalar.activation(dst, src, ACT.Copy).then_inc(ring_rd, 1)

                def counts(c, r):
                    act.wait_ge(lev_ok, ROUNDS * c + r + 1)
                    for j in range(TPC):
                        t = TPC * c + j
                        n = TPC * (ROUNDS * c + r) + j
                        if n >= 2:
                            act.wait_ge(cnt_ok, n - 1)
                        nc.scalar.activation(junk[:, n % 2, :], Z[:, t, :], ACT.Sign, bias=nlev[:, t:t + 1],
                                             accum_out=sgn[:, t:t + 1]).then_inc(cnt_ok, 1)

                def attended(c):
                    for k in range(d.KT):
                        act.wait_ge(at_ps, d.KT * c + k + 1)
                        if c:
                            act.wait_ge(pr_ps, c)
                        nc.scalar.activation(at[:, k, :], ps_t[:, k, :], ACT.Copy).then_inc(at_ok, 1)

                def high(c):
                    for k in range(d.KT):
                        act.wait_ge(t_ps, d.KT * c + k + 1)
                        if c:
                            act.wait_ge(ring_ps, nth("z", TPC * c - 1))
                        nc.scalar.activation(xt_hi[:, k, :], ps_t[:, k, :], ACT.Copy, scale=sc[:, 0:1])\
                            .then_inc(hi_ok, 1)

                attended(0)
                norm_root(nc, act, w1, 1)
                nc.scalar.activation(ws_t[:], tern[:, 0, :], ACT.Copy).then_inc(ws_ok, 1)
                act.wait_ge(w_in[1], 16)
                nc.scalar.activation(bs_hi[:], below[:, 0, :], ACT.Copy).then_inc(bs_h, 1)
                for s in range(d.NC + DEPTH - 1):
                    enter, count, _, leave = steps(s)

                    def pair(kind, c, j):
                        if c is not None:
                            evacuate([(kind, TPC * c + j), (kind, TPC * c + j + 1)])

                    if count is not None:
                        counts(count, 0)
                    if enter is not None:
                        high(enter)
                    pair("h", leave, 0)
                    if count is not None:
                        counts(count, 1)
                    pair("z", enter, 0)
                    pair("h", leave, 2)
                    if count is not None:
                        counts(count, 2)
                    pair("z", enter, 2)
                    if enter is not None and enter + 1 < d.NC:
                        attended(enter + 1)
                    if count is not None:
                        counts(count, 3)
                    if enter is not None and enter + 1 < d.NC:
                        norm_root(nc, act, w1, enter + 2)
                    if enter is not None:
                        act.wait_ge(zvar, enter + 1)
                        nc.scalar.activation(zsd[:, TPC * enter:TPC * (enter + 1)], zmv[:, :, 1], ACT.Sqrt)\
                            .then_inc(zroot, 1)
                    if leave is not None:
                        norm_root(nc, act, w2, leave + 1)

            @block.tensor
            def _(pe):
                def slot(kind, i):
                    n = ring.index((kind, i))
                    if n >= 2:
                        pe.wait_ge(ring_rd, n - 1)
                    return ps_z[:, n % 2, :]

                def attended(c):
                    if c:
                        pe.wait_ge(lo_ok, d.KT * c)
                    for k in range(d.KT):
                        for j in range(TPC):
                            ins = nc.tensor.transpose(ps_t[:, k, j * P:(j + 1) * P],
                                                      AO[:, TPC * c + j, k * P:(k + 1) * P], ident[:])
                        ins.then_inc(at_ps, 1)

                def project(c):
                    pe.wait_ge(w_in[0], 16)
                    pe.wait_ge(at_ok, d.KT * (c + 1))
                    for j in range(TPC):
                        out = ps_t[:].rearrange("p k n -> p (k n)")[:, j * d.E:(j + 1) * d.E]
                        for k in range(d.KT):
                            ins = nc.tensor.matmul(out, at[:, k, j * P:(j + 1) * P], wp[:, k, :], start=k == 0,
                                                   stop=k == d.KT - 1)
                    ins.then_inc(pr_ps, 1)

                def turn(c):
                    pe.wait_ge(xn_ok, c + 1)
                    for k in range(d.KT):
                        for j in range(TPC):
                            ins = nc.tensor.transpose(ps_t[:, k, j * P:(j + 1) * P],
                                                      XN[:, TPC * c + j, k * P:(k + 1) * P], ident[:])
                        ins.then_inc(t_ps, 1)

                def expand(t):
                    c, j = t // TPC, t % TPC
                    pe.wait_ge(lo_ok, d.KT * (c + 1))
                    if t == 0:
                        pe.wait_ge(ws_ok, 1)
                        pe.wait_ge(bs_ok, 1)
                        pe.wait_ge(on, 1)
                    dst = slot("z", t)
                    for n in range(NH):
                        cols = slice(n * d.CH, (n + 1) * d.CH)
                        for k in range(d.KT):
                            x, w = slice(j * P, (j + 1) * P), slice(k * d.N + n * d.CH, k * d.N + (n + 1) * d.CH)
                            mm_split(nc, dst[:, cols], xt_hi[:, k, x], xt_lo[:, k, x], ws_t[:, w], None, k == 0,
                                     False)
                        nc.tensor.matmul(dst[:, cols], share[:], bs_hi[:, cols], start=False, stop=False)
                        ins = nc.tensor.matmul(dst[:, cols], share[:], bs_lo[:, cols], start=False, stop=True)
                    ins.then_inc(ring_ps, 1)

                def turn_hidden(t):
                    dst = slot("h", t)
                    pe.wait_ge(hid_ok, t + 1)
                    for n in range(NN):
                        ins = nc.tensor.transpose(dst[:, n * P:(n + 1) * P], hid[:, t % 2, n * P:(n + 1) * P],
                                                  ident[:])
                    ins.then_inc(ring_ps, 1)

                def reduce(t):
                    pe.wait_ge(ring_rd, nth("h", t))
                    if t == 0:
                        pe.wait_ge(wo_ok, 1)
                    c, j = t // TPC, t % TPC
                    if j < 2 and c:
                        pe.wait_ge(o_rd, TPC * c)
                    elif j >= 2 and c + DEPTH - 1 < d.NC:
                        pe.wait_ge(o_rd, t - 1)
                    for n in range(NN):
                        ins = nc.tensor.matmul(out_bank(t), ht[:, t % TPC, n * P:(n + 1) * P],
                                               wo_t[:, n * d.E:(n + 1) * d.E], start=n == 0, stop=n == NN - 1)
                    ins.then_inc(o_ps, 1)

                def any_row(c, outputs):
                    pe.wait_ge(on, 1)
                    pe.wait_ge(flag_ok, c + 1)
                    if outputs:
                        pe.wait_ge(o_rd, outputs)
                    nc.tensor.matmul(ps_p[:, 0, d.E:d.E + 1], ones[:], flag[:, 0:1], start=True, stop=True)\
                        .then_inc(any_ps, 1)

                attended(0)
                project(0)
                for s in range(d.NC + DEPTH - 1):
                    enter, _, settles, leave = steps(s)
                    if enter is not None:
                        turn(enter)
                    if leave is not None:
                        turn_hidden(TPC * leave)
                        turn_hidden(TPC * leave + 1)
                    if enter is not None:
                        expand(TPC * enter)
                        expand(TPC * enter + 1)
                    if leave is not None:
                        turn_hidden(TPC * leave + 2)
                        turn_hidden(TPC * leave + 3)
                    for j in (0, 1):
                        if leave is not None:
                            reduce(TPC * leave + j)
                        if enter is not None:
                            expand(TPC * enter + j + 2)
                    if enter is not None and enter + 1 < d.NC:
                        attended(enter + 1)
                    if leave is not None:
                        reduce(TPC * leave + 2)
                    if enter is not None and enter + 1 < d.NC:
                        project(enter + 1)
                    if leave is not None:
                        reduce(TPC * leave + 3)
                    if settles is not None:
                        any_row(settles, 0 if leave is None else TPC * leave + (2 if enter is None else TPC))


def general_threshold(nc, dve, first, end, Z, work, top, thr, keep):
    with dve.Fori(first, end) as t:
        dve.drain()
        nc.vector.tensor_copy(work[:, 0, :], Z[:, bass.ds(t, 1), :].rearrange("p a n -> p (a n)"))
        for r in range((keep - 1) // 8):
            dve.drain()
            nc.vector.max(top[:, 0, :], work[:, r % 2, :])
            dve.drain()
            nc.vector.match_replace(out=work[:, (r + 1) % 2, :], in_to_replace=top[:, 0, :],
                                    in_values=work[:, r % 2, :], imm_value=-3.0e38)
        r = (keep - 1) // 8
        dve.drain()
        nc.vector.max(top[:, 0, :], work[:, r % 2, :])
        dve.drain()
        nc.vector.tensor_copy(thr[:, bass.ds(t, 1)], top[:, 0, (keep - 1) % 8:(keep - 1) % 8 + 1])


def stage_keys(nc, d, io, keep):
    with ExitStack() as ctx:
        st = Store(nc, ctx, "key")
        X, ident = keep["X"], keep["ident"]
        xt_hi, xt_lo, M, ksum, wq_raw = (keep[n] for n in ("xt_hi", "xt_lo", "M", "ksum", "wq_raw"))
        NI = d.INNER // d.CH
        CPB = d.CH // P
        TPB = d.S // P
        HW = P // 2
        UN = NI * d.B
        NP = 2
        xn = st.sb("xn", [P, d.TPC, d.E])
        xk_hi = st.sb("xk_hi", [P, d.NT, d.E], F32R)
        xk_lo = st.sb("xk_lo", [P, d.NT, d.E], F32R)
        raw = wq_raw[:, 2:4]
        w_hi = st.sb("w_hi", [P, 4, 2 * d.CH], F32R)
        w_lo = st.sb("w_lo", [P, 4, 2 * d.CH], F32R)
        k_hi = st.sb("k_hi", [P, 2, d.CH], F32R)
        k_lo = st.sb("k_lo", [P, 2, d.CH], F32R)
        g_hi = st.sb("g_hi", [P, d.KT, d.CH], F32R)
        g_lo = st.sb("g_lo", [P, d.KT, d.CH], F32R)
        bd = xn[:].rearrange("p j e -> p (j e)")[:, 0:d.CH]
        bd_hi = st.sb("bd_hi", [P, d.CH], F32R)
        bd_lo = st.sb("bd_lo", [P, d.CH], F32R)
        mask = st.sb("mask", [P, P])
        ones = st.sb("ones", [P, P])
        k_sum = st.sb("k_sum", [P, 2, d.CH])
        bo = st.sb("bo", [P, d.E])
        w = [NormWork(st, d.TPC, str(c)) for c in range(d.NC)]
        ps_k = st.ps("ps_k", [P, 2, d.CH])
        ps_g = st.ps("ps_g", [P, 2, d.KT, d.CH])
        ps_s = st.ps("ps_s", [P, d.CH])
        ps_v = st.ps("ps_v", [P, d.CH])

        w_in = [st.sem(f"w_in{i}") for i in range(2)]
        wq_in, bo_in = st.sem("wq_in"), st.sem("bo_in")
        dv, gp, const_ok, xb_ok = st.sem("dv"), st.sem("gp"), st.sem("const_ok"), st.sem("xb_ok")
        w_h, w_l = st.sem("w_h"), st.sem("w_l")
        xn_ok, t_ps, hi_ok, lo_ok, xk_h, xk_ok = (
            st.sem(n) for n in ("xn_ok", "t_ps", "hi_ok", "lo_ok", "xk_h", "xk_ok"))
        k_ps, k_h, k_ok, g_ps, g_h, g_ok = (st.sem(n) for n in ("k_ps", "k_h", "k_ok", "g_ps", "g_h", "g_ok"))
        acc_ok, s_ps = st.sem("acc_ok"), st.sem("s_ps")
        s_ok, v_ps, bd_ok, bd_h, bd_l, m_ps, m_ok = (
            st.sem(n) for n in ("s_ok", "v_ps", "bd_ok", "bd_h", "bd_l", "m_ps", "m_ok"))

        WV_SPLIT, WO_SPLIT, WK_SPLIT = 4, 1, 6
        PREP = {1: 2, 3: 3}
        V_STEP, M_STEPS = 1, (4, 6)

        def turned(c):
            return ps_k if c < NP else ps_g[:, 1]

        with nc.Block() as block:
            @block.sync
            def _(sp):
                sp.dma_start(bo[:], io["L1_attn_bo"].rearrange("(a n) -> a n", a=1).to_broadcast([P, d.E]))\
                    .then_inc(bo_in, 16)
                for i in range(3 * NI):
                    n, name = i // 3, ("Wk", "Wv", "Wo")[i % 3]
                    src, dst = io["L1_attn_" + name], raw[:, i % 2, :]
                    if i >= 2:
                        sp.wait_ge(w_l, i - 1)
                    if name == "Wo":
                        sp.dma_start(dst.rearrange("p (c n) -> p c n", c=CPB),
                                     src[n * d.CH:(n + 1) * d.CH, :].rearrange("(c p) n -> p c n", p=P))\
                            .then_inc(w_in[i % 2], 16)
                    else:
                        sp.dma_start(dst.rearrange("p (k n) -> p k n", k=d.KT),
                                     src[:, n * d.CH:(n + 1) * d.CH].rearrange("(k p) n -> p k n", p=P))\
                            .then_inc(w_in[i % 2], 16)
                    if i == 1:
                        for q in range(2):
                            sp.dma_start(wq_raw[:, q, :].rearrange("p (k n) -> p k n", k=d.KT),
                                         io["L1_attn_Wq"][:, q * d.CH:(q + 1) * d.CH]
                                         .rearrange("(k p) n -> p k n", p=P)).then_inc(wq_in, 16)
                sp.wait_ge(wq_in, 32)

            @block.gpsimd
            def _(pool):
                link = chain(pool, gp)
                link(nc.gpsimd.memset(mask[:], 0.0))
                link(nc.gpsimd.memset(mask[0:HW, 0:HW], 1.0))
                link(nc.gpsimd.memset(mask[HW:P, HW:P], 1.0))
                nc.gpsimd.memset(ones[:], 1.0).then_inc(const_ok, 1)
                pool.wait_ge(bo_in, 16)
                pool.wait_ge(xn_ok, d.NC)
                for t in range(d.NT):
                    ins = nc.gpsimd.tensor_tensor(X[:, t, :], X[:, t, :], bo[:], ALU.add)
                ins.then_inc(xb_ok, 1)

            @block.vector
            def _(dve):
                def split(i, slot):
                    dve.wait_ge(w_h, i + 1)
                    nc.vector.tensor_tensor(w_lo[:, slot, :], raw[:, i % 2, :], as_f32(w_hi[:, slot, :]),
                                            ALU.subtract).then_inc(w_l, 1)

                def normal(c):
                    norm_rstd(nc, dve, link, w[c], 1)
                    if c >= 1:
                        dve.wait_ge(t_ps, d.KT * c)
                        dve.wait_ge(xk_h, c)
                        dve.wait_ge(xk_ok, c)
                    for j in range(d.TPC):
                        t = d.TPC * c + j
                        ins = norm_apply(nc, w[c], j, xn[:, j, :], X[:, t, :])
                    ins.then_inc(xn_ok, 1)
                    dve.wait_ge(xn_ok, c + 1)

                def prepare(c):
                    sl = slice(d.TPC * c, d.TPC * (c + 1))
                    dve.wait_ge(xk_h, c + 1)
                    nc.vector.tensor_tensor(xk_lo[:, sl, :], xn[:], as_f32(xk_hi[:, sl, :]),
                                            ALU.subtract).then_inc(xk_ok, 1)
                    for k in range(d.KT):
                        dve.wait_ge(hi_ok, d.KT * c + k + 1)
                        nc.vector.tensor_tensor(xt_lo[:, k, c * d.CH:(c + 1) * d.CH], turned(c)[:, k, :],
                                                as_f32(xt_hi[:, k, c * d.CH:(c + 1) * d.CH]),
                                                ALU.subtract).then_inc(lo_ok, 1)

                def finish(u, step):
                    if step == 0:
                        for k in range(d.KT):
                            dve.wait_ge(g_h, d.KT * u + k + 1)
                            nc.vector.tensor_tensor(g_lo[:, k, :], ps_g[:, u % 2, k, :], as_f32(g_hi[:, k, :]),
                                                    ALU.subtract).then_inc(g_ok, 1)
                    if step == V_STEP + 1:
                        dve.wait_ge(v_ps, u + 1)
                        dve.wait_ge(const_ok, 1)
                        if u:
                            dve.wait_ge(bd_h, u)
                            dve.wait_ge(bd_l, u)
                        nc.vector.tensor_tensor(bd.rearrange("p (c m) -> p c m", m=P),
                                                ps_v[:].rearrange("p (c m) -> p c m", m=P),
                                                mask[:].unsqueeze(1).to_broadcast([P, CPB, P]),
                                                ALU.mult).then_inc(bd_ok, 1)
                        dve.wait_ge(bd_h, u + 1)
                        nc.vector.tensor_tensor(bd_lo[:], bd, as_f32(bd_hi[:]), ALU.subtract).then_inc(bd_l, 1)

                link = chain(dve, dv)
                def var(c):
                    norm_var(nc, link, w[c], [X[:, d.TPC * c + j, :] for j in range(d.TPC)])

                var(0)
                var(1)
                normal(0)
                split(0, 0)
                for c in range(NP):
                    prepare(c)
                    if c + 1 < NP:
                        normal(c + 1)
                for u in range(UN):
                    n, b = u // d.B, u % d.B
                    for t in range(TPB):
                        i = TPB * u + t
                        dve.wait_ge(k_h, i + 1)
                        nc.vector.scalar_tensor_tensor(out=k_lo[:, i % 2, :], in0=ps_k[:, i % 2, :], scalar=0.0,
                                                       in1=as_f32(k_hi[:, i % 2, :]), op0=ALU.max,
                                                       op1=ALU.subtract).then_inc(k_ok, 1)
                        if t == 0:
                            if u >= 2:
                                dve.wait_ge(s_ps, u - 1)
                            nc.vector.tensor_scalar(k_sum[:, u % 2, :], ps_k[:, i % 2, :], 0.0, None, ALU.max)\
                                .then_inc(acc_ok, 1)
                        else:
                            dve.wait_ge(acc_ok, i)
                            nc.vector.scalar_tensor_tensor(out=k_sum[:, u % 2, :], in0=ps_k[:, i % 2, :], scalar=0.0,
                                                           in1=k_sum[:, u % 2, :], op0=ALU.max, op1=ALU.add)\
                                .then_inc(acc_ok, 1)
                        if u == 0 and t + 1 in PREP:
                            var(PREP[t + 1])
                        if u == 0 and t in PREP:
                            normal(PREP[t])
                            prepare(PREP[t])
                        if u:
                            finish(u - 1, t)
                        if b == 0 and t == WV_SPLIT:
                            split(3 * n + 1, 2)
                        if b == 1 and t == WO_SPLIT:
                            split(3 * n + 2, 3)
                        if b == 1 and t == WK_SPLIT and n + 1 < NI:
                            split(3 * n + 3, (n + 1) % 2)
                for t in range(TPB):
                    finish(UN - 1, t)

            @block.scalar
            def _(act):
                def split(i, slot):
                    act.wait_ge(w_in[i % 2], 16 * (i // 2 + 1))
                    nc.scalar.activation(w_hi[:, slot, :], raw[:, i % 2, :], ACT.Copy).then_inc(w_h, 1)

                def rows(c):
                    act.wait_ge(xn_ok, c + 1)
                    nc.scalar.activation(xk_hi[:, d.TPC * c:d.TPC * (c + 1), :], xn[:], ACT.Copy).then_inc(xk_h, 1)

                def prepare(c):
                    for k in range(d.KT):
                        act.wait_ge(t_ps, d.KT * c + k + 1)
                        nc.scalar.activation(xt_hi[:, k, c * d.CH:(c + 1) * d.CH], turned(c)[:, k, :], ACT.Copy)\
                            .then_inc(hi_ok, 1)

                def finish(u, step):
                    n, b = u // d.B, u % d.B
                    if step == 0:
                        act.wait_ge(g_ps, TPB * (u + 1))
                        if u >= 1:
                            act.wait_ge(v_ps, u)
                        for k in range(d.KT):
                            nc.scalar.activation(g_hi[:, k, :], ps_g[:, u % 2, k, :], ACT.Copy).then_inc(g_h, 1)
                    if step == 1:
                        act.wait_ge(s_ps, u + 1)
                        nc.scalar.activation(ksum[:, b, d.CH * n:d.CH * (n + 1)], ps_s[:], ACT.Copy).then_inc(s_ok, 1)
                    if step == V_STEP + 1:
                        act.wait_ge(bd_ok, u + 1)
                        if u:
                            act.wait_ge(m_ps, 2 * u)
                        nc.scalar.activation(bd_hi[:], bd, ACT.Copy).then_inc(bd_h, 1)
                    if step - 1 in M_STEPS:
                        j = M_STEPS.index(step - 1)
                        act.wait_ge(m_ps, 2 * u + j + 1)
                        nc.scalar.activation(M[:, b, CPB * n + 2 * j:CPB * n + 2 * j + 2, :],
                                             ps_v[:].rearrange("p (c e) -> p c e", e=d.E), ACT.Copy).then_inc(m_ok, 1)

                for c in range(NP):
                    norm_root(nc, act, w[c], 1)
                split(0, 0)
                for c in range(NP):
                    rows(c)
                    prepare(c)
                for u in range(UN):
                    n, b = u // d.B, u % d.B
                    for t in range(TPB):
                        i = TPB * u + t
                        act.wait_ge(k_ps, i + 1)
                        if i >= 2:
                            act.wait_ge(g_ps, i - 1)
                        nc.scalar.activation(k_hi[:, i % 2, :], ps_k[:, i % 2, :], ACT.Relu).then_inc(k_h, 1)
                        if u == 0 and t + 1 in PREP:
                            norm_root(nc, act, w[PREP[t + 1]], 1)
                        if u == 0 and t in PREP:
                            rows(PREP[t])
                            prepare(PREP[t])
                        if u:
                            finish(u - 1, t)
                        if b == 0 and t == WV_SPLIT:
                            if n:
                                act.wait_ge(v_ps, d.B * n)
                            split(3 * n + 1, 2)
                        if b == 1 and t == WO_SPLIT:
                            if n:
                                act.wait_ge(m_ps, 2 * d.B * n)
                            split(3 * n + 2, 3)
                        if b == 1 and t == WK_SPLIT and n + 1 < NI:
                            if n:
                                act.wait_ge(k_ps, TPB * d.B * n)
                            split(3 * n + 3, (n + 1) % 2)
                for t in range(TPB):
                    finish(UN - 1, t)

            @block.tensor
            def _(pe):
                def prepare(c):
                    pe.wait_ge(xn_ok, c + 1)
                    if 0 < c < NP or c > NP:
                        pe.wait_ge(lo_ok, d.KT * c)
                    for k in range(d.KT):
                        for j in range(d.TPC):
                            ins = nc.tensor.transpose(turned(c)[:, k, j * P:(j + 1) * P],
                                                      xn[:, j, k * P:(k + 1) * P], ident[:])
                        ins.then_inc(t_ps, 1)

                def keys(i):
                    u, t = i // TPB, i % TPB
                    n, b = u // d.B, u % d.B
                    if i % (TPB * d.B) == 0:
                        pe.wait_ge(w_l, 3 * n + 1)
                    if n == 0 and t % d.TPC == 0:
                        pe.wait_ge(lo_ok, d.KT * ((b * TPB + t) // d.TPC + 1))
                    if i < 2:
                        pe.wait_ge(lo_ok, d.KT * NP)
                    if i >= 2:
                        pe.wait_ge(acc_ok, i - 1)
                    tok = slice((b * TPB + t) * P, (b * TPB + t + 1) * P)
                    for k in range(d.KT):
                        wk = slice(k * d.CH, (k + 1) * d.CH)
                        ins = mm_split(nc, ps_k[:, i % 2, :], xt_hi[:, k, tok], xt_lo[:, k, tok],
                                       w_hi[:, n % 2, wk], w_lo[:, n % 2, wk], k == 0, k == d.KT - 1)
                    ins.then_inc(k_ps, 1)

                def sums(i):
                    u, t = i // TPB, i % TPB
                    n, b = u // d.B, u % d.B
                    pe.wait_ge(k_ok, i + 1)
                    if n == 0 and t % d.TPC == 0:
                        pe.wait_ge(xk_ok, (b * TPB + t) // d.TPC + 1)
                    if u == 1 and t == 0:
                        pe.wait_ge(lo_ok, d.KT * d.NC)
                    if t == 0 and u >= 2:
                        pe.wait_ge(g_ok, d.KT * (u - 1))
                    kh, kl = k_hi[:, i % 2, :], k_lo[:, i % 2, :]
                    for m in range(d.KT):
                        x = slice(m * P, (m + 1) * P)
                        ins = mm_split(nc, ps_g[:, u % 2, m, :], xk_hi[:, b * TPB + t, x], xk_lo[:, b * TPB + t, x],
                                       kh, kl, t == 0, t == TPB - 1)
                    ins.then_inc(g_ps, 1)

                def finish(u, step):
                    n = u // d.B
                    if step == 0:
                        pe.wait_ge(acc_ok, TPB * (u + 1))
                        if u:
                            pe.wait_ge(s_ok, u)
                        nc.tensor.matmul(ps_s[:], ones[:], k_sum[:, u % 2, :], start=True, stop=True)\
                            .then_inc(s_ps, 1)
                    if step == V_STEP:
                        pe.wait_ge(g_ok, d.KT * (u + 1))
                        pe.wait_ge(w_l, 3 * n + 2)
                        if u:
                            pe.wait_ge(m_ok, 2 * u)
                        for c in range(CPB):
                            cols = slice(c * P, (c + 1) * P)
                            for k in range(d.KT):
                                wv = slice(k * d.CH + c * P, k * d.CH + (c + 1) * P)
                                ins = mm_split(nc, ps_v[:, cols], w_hi[:, 2, wv], w_lo[:, 2, wv], g_hi[:, k, cols],
                                               g_lo[:, k, cols], k == 0, k == d.KT - 1)
                        ins.then_inc(v_ps, 1)
                    if step in M_STEPS:
                        j = M_STEPS.index(step)
                        pe.wait_ge(bd_l, u + 1)
                        pe.wait_ge(w_l, 3 * n + 3)
                        if j:
                            pe.wait_ge(m_ok, 2 * u + j)
                        for c in (2 * j, 2 * j + 1):
                            cols, wo = slice(c * P, (c + 1) * P), slice(c * d.E, (c + 1) * d.E)
                            ins = mm_split(nc, ps_v[:, (c % 2) * d.E:(c % 2 + 1) * d.E], bd_hi[:, cols],
                                           bd_lo[:, cols], w_hi[:, 3, wo], w_lo[:, 3, wo], True, True)
                        ins.then_inc(m_ps, 1)

                for c in range(NP):
                    prepare(c)
                pe.wait_ge(const_ok, 1)
                keys(0)
                for u in range(UN):
                    for t in range(TPB):
                        i = TPB * u + t
                        if i + 1 < TPB * UN:
                            keys(i + 1)
                        if u == 0 and t in PREP:
                            prepare(PREP[t])
                        sums(i)
                        if u:
                            finish(u - 1, t)
                for t in range(TPB):
                    finish(UN - 1, t)


def stage_queries(nc, d, io, keep):
    with ExitStack() as ctx:
        st = Store(nc, ctx, "qry")
        X, ident = keep["X"], keep["ident"]
        xt_hi, xt_lo, M, ksum, wq_raw = (keep[n] for n in ("xt_hi", "xt_lo", "M", "ksum", "wq_raw"))
        NI = d.INNER // d.CH
        CPB = d.CH // P
        TPB = d.S // P
        HW = P // 2
        HPB = d.CH // HW
        UN = d.NT * NI
        w_hi = st.sb("w_hi", [P, NI, d.KT * d.CH], F32R)
        w_lo = st.sb("w_lo", [P, NI, d.KT * d.CH], F32R)
        m_hi = st.sb("m_hi", [P, d.NCH, d.E], F32R)
        m_lo = st.sb("m_lo", [P, d.NCH, d.E], F32R)
        qr = st.sb("qr", [P, 2, d.CH])
        prod = st.sb("prod", [P, 2, d.CH])
        nrm = st.sb("nrm", [P, HPB])
        rec = st.sb("rec", [P, HPB])
        qn = st.sb("qn", [P, 2, d.CH])
        n_hi = st.sb("n_hi", [P, 2, d.CH], F32R)
        n_lo = st.sb("n_lo", [P, 2, d.CH], F32R)
        ps_q = st.ps("ps_q", [P, 2, d.CH])
        ps_t = st.ps("ps_t", [P, 2, d.CH])
        ps_o = st.ps("ps_o", [P, 2, d.CH])
        w_in = [st.sem(f"w_in{i}") for i in range(2)]
        w_h, w_ok, m_h, m_ok = (st.sem(n) for n in ("w_h", "w_ok", "m_h", "m_ok"))
        q_ps, q_ok, pr_ok, dv, qn_ok, t_ps, n_h, n_ok, o_ps, x_ok = (
            st.sem(n) for n in ("q_ps", "q_ok", "pr_ok", "dv", "qn_ok", "t_ps", "n_h", "n_ok", "o_ps", "x_ok"))

        def cols(n):
            return slice(n * d.CH, (n + 1) * d.CH)

        def split_at(u):
            b, n = u // (NI * TPB), u % (NI * TPB)
            return (b, n) if n < NI and b < d.B else None

        with nc.Block() as block:
            @block.sync
            def _(sp):
                for q in range(2, NI):
                    sp.dma_start(wq_raw[:, q, :].rearrange("p (k n) -> p k n", k=d.KT),
                                 io["L1_attn_Wq"][:, q * d.CH:(q + 1) * d.CH].rearrange("(k p) n -> p k n", p=P))\
                        .then_inc(w_in[q - 2], 16)

            @block.gpsimd
            def _(pool):
                for u in range(UN):
                    b, n = u // (TPB * NI), u % NI
                    pool.wait_ge(q_ok, u + 1)
                    if u >= 2:
                        pool.wait_ge(qn_ok, u - 1)
                    nc.gpsimd.tensor_tensor(prod[:, u % 2, :], qr[:, u % 2, :], ksum[:, b, cols(n)],
                                            ALU.mult).then_inc(pr_ok, 1)
                    if split_at(u):
                        blk = slice(CPB * n, CPB * (n + 1))
                        pool.wait_ge(m_h, NI * b + n + 1)
                        nc.gpsimd.tensor_tensor(m_lo[:, blk, :], M[:, b, blk, :], as_f32(m_hi[:, blk, :]),
                                                ALU.subtract).then_inc(m_ok, 1)

            @block.vector
            def _(dve):
                link = chain(dve, dv)

                def divide(u):
                    dve.wait_ge(pr_ok, u + 1)
                    link(nc.vector.tensor_reduce(nrm[:], prod[:, u % 2, :].rearrange("p (h e) -> p h e", e=HW),
                                                 AX.X, ALU.add))
                    link(nc.vector.reciprocal(rec[:], nrm[:]))
                    if u >= 2:
                        dve.wait_ge(t_ps, u - 1)
                    nc.vector.scalar_tensor_tensor(out=qn[:, u % 2, :].rearrange("p (h e) -> p h e", e=HW),
                                                   in0=rec[:].unsqueeze(2).to_broadcast([P, HPB, HW]), scalar=1e6,
                                                   in1=qr[:, u % 2, :].rearrange("p (h e) -> p h e", e=HW),
                                                   op0=ALU.min, op1=ALU.mult).then_inc(qn_ok, 1)
                    dve.wait_ge(qn_ok, u + 1)

                def low(u):
                    dve.wait_ge(n_h, u + 1)
                    if u >= 2:
                        dve.wait_ge(o_ps, u - 1)
                    nc.vector.tensor_tensor(n_lo[:, u % 2, :], ps_t[:, u % 2, :], as_f32(n_hi[:, u % 2, :]),
                                            ALU.subtract).then_inc(n_ok, 1)

                def add(t):
                    dve.wait_ge(o_ps, NI * (t + 1))
                    nc.vector.tensor_tensor(X[:, t, :], X[:, t, :], ps_o[:, t % 2, 0:d.E], ALU.add).then_inc(x_ok, 1)

                for n in range(NI):
                    dve.wait_ge(w_h, n + 1)
                    nc.vector.tensor_tensor(w_lo[:, n, :], wq_raw[:, n, :], as_f32(w_hi[:, n, :]),
                                            ALU.subtract).then_inc(w_ok, 1)
                for u in range(UN + 4):
                    if 1 <= u <= UN:
                        divide(u - 1)
                    if 2 <= u < UN + 2:
                        low(u - 2)
                    if u >= NI + 3 and (u - 3) % NI == 0:
                        add((u - 3) // NI - 1)

            @block.scalar
            def _(act):
                def high(u):
                    act.wait_ge(t_ps, u + 1)
                    if u >= 2:
                        act.wait_ge(o_ps, u - 1)
                    nc.scalar.activation(n_hi[:, u % 2, :], ps_t[:, u % 2, :], ACT.Copy).then_inc(n_h, 1)

                for n in range(NI):
                    if n >= 2:
                        act.wait_ge(w_in[n - 2], 16)
                    nc.scalar.activation(w_hi[:, n, :], wq_raw[:, n, :], ACT.Copy).then_inc(w_h, 1)
                for u in range(UN + 2):
                    if u < UN:
                        act.wait_ge(q_ps, u + 1)
                        if u >= 2:
                            act.wait_ge(qn_ok, u - 1)
                        nc.scalar.activation(qr[:, u % 2, :], ps_q[:, u % 2, :], ACT.Relu).then_inc(q_ok, 1)
                    if split_at(u):
                        b, n = split_at(u)
                        blk = slice(CPB * n, CPB * (n + 1))
                        if b:
                            act.wait_ge(o_ps, u - NI + 1)
                        nc.scalar.activation(m_hi[:, blk, :], M[:, b, blk, :], ACT.Copy).then_inc(m_h, 1)
                    if u >= 2:
                        high(u - 2)

            @block.tensor
            def _(pe):
                def query(u):
                    t, n = u // NI, u % NI
                    if u < NI:
                        pe.wait_ge(w_ok, n + 1)
                    if u >= 2:
                        pe.wait_ge(q_ok, u - 1)
                    tok = slice(t * P, (t + 1) * P)
                    for k in range(d.KT):
                        ins = mm_split(nc, ps_q[:, u % 2, :], xt_hi[:, k, tok], xt_lo[:, k, tok],
                                       w_hi[:, n, cols(k)], w_lo[:, n, cols(k)], k == 0, k == d.KT - 1)
                    ins.then_inc(q_ps, 1)

                def turn(u):
                    pe.wait_ge(qn_ok, u + 1)
                    if u >= 2:
                        pe.wait_ge(n_ok, u - 1)
                    for c in range(CPB):
                        ins = nc.tensor.transpose(ps_t[:, u % 2, c * P:(c + 1) * P], qn[:, u % 2, c * P:(c + 1) * P],
                                                  ident[:])
                    ins.then_inc(t_ps, 1)

                def result(u):
                    t, n = u // NI, u % NI
                    b = t // TPB
                    if t % TPB == 0:
                        pe.wait_ge(m_ok, NI * b + n + 1)
                    if n == 0 and t >= 2:
                        pe.wait_ge(x_ok, t - 1)
                    pe.wait_ge(n_ok, u + 1)
                    for c in range(CPB):
                        q = slice(c * P, (c + 1) * P)
                        ins = mm_split(nc, ps_o[:, t % 2, 0:d.E], n_hi[:, u % 2, q], n_lo[:, u % 2, q],
                                       m_hi[:, CPB * n + c, :], m_lo[:, CPB * n + c, :],
                                       n == 0 and c == 0, n == NI - 1 and c == CPB - 1)
                    ins.then_inc(o_ps, 1)

                for u in range(UN + 3):
                    if u < UN:
                        query(u)
                    if 2 <= u < UN + 2:
                        turn(u - 2)
                    if u >= 3:
                        result(u - 3)


def stage_routed(nc, d, io, keep, out):
    with ExitStack() as ctx:
        st = Store(nc, ctx, "rt")
        X, ident = keep["X"], keep["ident"]
        NE = io["L1_ffn_wr"].shape[0]
        TPC = d.TPC
        names = ("w1", "w3", "w2")
        raw = st.sb("raw", [P, 3, d.KT, d.E])
        wr_raw = st.sb("wr_raw", [NE, d.E])
        wt_hi = st.sb("wt_hi", [P, 2, d.KT * d.E], F32R)
        wt_lo = st.sb("wt_lo", [P, 2, d.KT * d.E], F32R)
        w2t = st.sb("w2t", [P, d.KT * d.E])
        wr_hi = st.sb("wr_hi", [P, d.KT * NE], F32R)
        wr_lo = st.sb("wr_lo", [P, d.KT * NE], F32R)
        xn = st.sb("xn", [P, 2, TPC, d.E])
        xt_hi = st.sb("xt_hi", [P, d.KT, d.TOK], F32R)
        xt_lo = st.sb("xt_lo", [P, d.KT, d.TOK], F32R)
        h1 = st.sb("h1", [P, 2, d.KT, d.CH])
        h_hi = st.sb("h_hi", [P, 2, d.KT, d.CH], F32R)
        h_lo = st.sb("h_lo", [P, 2, d.KT, d.CH], F32R)
        h2 = st.sb("h2", [P, d.NT, d.E])
        lg, ex, pr, gate = (st.sb(n, [P, d.NT, NE]) for n in ("lg", "ex", "pr", "gate"))
        lmax, esum, rsum, gs, rgs = (st.sb(n, [P, d.NT]) for n in ("lmax", "esum", "rsum", "gs", "rgs"))
        best = st.sb("best", [P, d.NT, 8])
        idx = st.sb("idx", [P, d.NT, 8], U32)
        idx_f = st.sb("idx_f", [P, d.NT, 2])
        oh = st.sb("oh", [P, 2, d.NT, NE])
        iota_i = st.sb("iota_i", [P, NE], mybir.dt.int32)
        iota_f = st.sb("iota_f", [P, NE])
        acc = st.sb("acc", [NE, d.E])
        acc_t = st.sb("acc_t", [P, d.KT, NE])
        w = [NormWork(st, TPC, str(c)) for c in range(d.NC)]
        ps_th = [st.ps(f"ps_th{i}", [P, d.KT, d.CH]) for i in range(2)]
        ps_2 = st.ps("ps_2", [P, 2, d.CH])
        ps_l = st.ps("ps_l", [P, d.NT, NE])
        ps_a = st.ps("ps_a", [P, d.CH])
        w_in = [st.sem(f"w_in{i}") for i in range(4)]
        dv, iota_ok, out_s = st.sem("dv"), st.sem("iota_ok"), st.sem("out")
        wt_ps, wt_h, wt_l, w2_ok = (st.sem(n) for n in ("wt_ps", "wt_h", "wt_l", "w2_ok"))
        xn_ok, t_ps, hi_ok, lo_ok = (st.sem(n) for n in ("xn_ok", "t_ps", "hi_ok", "lo_ok"))
        h_ps, h1_ok, hh_ok, hl_ok, l_ps, l_rd, lmax_ok, ex_ok = (
            st.sem(n) for n in ("h_ps", "h1_ok", "hh_ok", "hl_ok", "l_ps", "l_rd", "lmax_ok", "ex_ok"))
        h2_ps, h2_ok, g_ok, a_ps = st.sem("h2_ps"), st.sem("h2_ok"), st.sem("g_ok"), st.sem("a_ps")
        acc_ok, fin_ok = st.sem("acc_ok"), st.sem("fin_ok")
        out_tiles = out.rearrange("b (t p) e -> p (b t) e", p=P)
        HALVES = TPC // 2

        with nc.Block() as block:
            @block.sync
            def _(sp):
                for i, name in enumerate(names):
                    sp.dma_start(raw[:, i], io["L1_ffn_" + name].rearrange("(a p) n -> p a n", p=P))\
                        .then_inc(w_in[i], 16)
                sp.dma_start(wr_raw[:], io["L1_ffn_wr"]).then_inc(w_in[3], 16)
                sp.dma_start(out_tiles[:, 1:, :], X[:, 1:, :]).then_inc(out_s, 16)
                sp.wait_ge(fin_ok, 1)
                sp.dma_start(out_tiles[:, 0, :], X[:, 0, :]).then_inc(out_s, 16)
                sp.wait_ge(out_s, 32)

            @block.gpsimd
            def _(pool):
                nc.gpsimd.iota(iota_i[:], pattern=[[1, NE]], base=0, channel_multiplier=0).then_inc(iota_ok, 1)

            @block.vector
            def _(dve):
                link = chain(dve, dv)

                def normal(c):
                    norm_rstd(nc, dve, link, w[c], 1)
                    if c >= 2:
                        dve.wait_ge(t_ps, d.KT * (c - 1))
                    for j in range(TPC):
                        t = TPC * c + j
                        ins = norm_apply(nc, w[c], j, xn[:, c % 2, j, :], X[:, t, :])
                    ins.then_inc(xn_ok, 1)

                def low(c):
                    for k in range(d.KT):
                        dve.wait_ge(hi_ok, d.KT * c + k + 1)
                        cols = slice(c * d.CH, (c + 1) * d.CH)
                        nc.vector.tensor_tensor(xt_lo[:, k, cols], ps_th[c % 2][:, k, :], as_f32(xt_hi[:, k, cols]),
                                                ALU.subtract).then_inc(lo_ok, 1)

                def low_h(c):
                    if c >= 2:
                        dve.wait_ge(h2_ps, HALVES * (c - 1))
                    for m in range(d.KT):
                        dve.wait_ge(hh_ok, d.KT * c + m + 1)
                        nc.vector.tensor_tensor(h_lo[:, c % 2, m, :], h1[:, c % 2, m, :],
                                                as_f32(h_hi[:, c % 2, m, :]), ALU.subtract).then_inc(hl_ok, 1)

                def spread(ap, n):
                    return ap.unsqueeze(2).to_broadcast([P, d.NT, n])

                def gates():
                    dve.wait_ge(ex_ok, 1)
                    link(nc.vector.tensor_reduce(esum[:], ex[:], AX.X, ALU.add))
                    link(nc.vector.reciprocal(rsum[:], esum[:]))
                    link(nc.vector.tensor_tensor(pr[:], ex[:], spread(rsum[:], NE), ALU.mult))
                    for t in range(d.NT):
                        ins = nc.vector.max(best[:, t, :], pr[:, t, :])
                    link(ins)
                    for t in range(d.NT):
                        ins = nc.vector.max_index(idx[:, t, :], best[:, t, :], pr[:, t, :])
                    link(ins)
                    link(nc.vector.tensor_tensor(gs[:], best[:, :, 0], best[:, :, 1], ALU.add))
                    nc.vector.reciprocal(rgs[:], gs[:])
                    link(nc.vector.tensor_copy(idx_f[:], idx[:, :, 0:2]))
                    for i in range(2):
                        ins = nc.vector.tensor_tensor(oh[:, i], spread(idx_f[:, :, i], NE),
                                                      iota_f[:].unsqueeze(1).to_broadcast([P, d.NT, NE]),
                                                      ALU.is_equal)
                    link(ins)
                    for i in range(2):
                        ins = nc.vector.tensor_tensor(oh[:, i], oh[:, i], spread(best[:, :, i], NE), ALU.mult)
                    link(ins)
                    link(nc.vector.tensor_tensor(oh[:, 0], oh[:, 0], oh[:, 1], ALU.add))
                    nc.vector.tensor_tensor(gate[:], oh[:, 0], spread(rgs[:], NE), ALU.mult).then_inc(g_ok, 1)

                def var(c):
                    norm_var(nc, link, w[c], [X[:, TPC * c + j, :] for j in range(TPC)])

                var(0)
                var(1)
                normal(0)
                var(2)
                normal(1)
                var(3)
                for i in range(2):
                    dve.wait_ge(wt_h, i + 1)
                    nc.vector.tensor_tensor(wt_lo[:, i], ps_2[:, i, :], as_f32(wt_hi[:, i]),
                                            ALU.subtract).then_inc(wt_l, 1)
                dve.wait_ge(wt_h, 3)
                nc.vector.tensor_tensor(wr_lo[:], ps_l[:].rearrange("p t e -> p (t e)")[:, 0:d.KT * NE],
                                        as_f32(wr_hi[:]), ALU.subtract).then_inc(wt_l, 1)
                for c in range(d.NC):
                    low(c)
                    if c + 2 < d.NC:
                        normal(c + 2)
                dve.wait_ge(l_ps, d.NC)
                link(nc.vector.tensor_reduce(lmax[:], ps_l[:], AX.X, ALU.max))
                nc.vector.tensor_tensor(lg[:], ps_l[:], spread(lmax[:], NE), ALU.subtract).then_inc(lmax_ok, 1)
                dve.wait_ge(iota_ok, 1)
                nc.vector.tensor_copy(iota_f[:], iota_i[:]).then_inc(l_rd, 1)
                dve.wait_ge(l_rd, 1)
                low_h(0)
                gates()
                for c in range(1, d.NC):
                    low_h(c)
                dve.wait_ge(a_ps, 1)
                nc.vector.tensor_copy(acc[:], ps_a[0:NE, 0:d.E]).then_inc(acc_ok, 1)
                dve.wait_ge(a_ps, 2)
                nc.vector.tensor_copy(acc_t[:].rearrange("p k e -> p (k e)"),
                                      ps_l[:].rearrange("p t e -> p (t e)")[:, 0:d.KT * NE]).then_inc(acc_ok, 1)
                dve.wait_ge(a_ps, 3)
                nc.vector.tensor_tensor(X[0:NE, 0, :], X[0:NE, 0, :], ps_a[0:NE, 0:d.E], ALU.add).then_inc(fin_ok, 1)

            @block.scalar
            def _(act):
                for c in range(d.NC):
                    norm_root(nc, act, w[c], 1)
                for i in range(2):
                    act.wait_ge(wt_ps, i + 1)
                    nc.scalar.activation(wt_hi[:, i], ps_2[:, i, :], ACT.Copy).then_inc(wt_h, 1)
                act.wait_ge(wt_ps, 4)
                nc.scalar.activation(wr_hi[:], ps_l[:].rearrange("p t e -> p (t e)")[:, 0:d.KT * NE], ACT.Copy)\
                    .then_inc(wt_h, 1)
                for c in range(d.NC):
                    for k in range(d.KT):
                        act.wait_ge(t_ps, d.KT * c + k + 1)
                        nc.scalar.activation(xt_hi[:, k, c * d.CH:(c + 1) * d.CH], ps_th[c % 2][:, k, :], ACT.Copy)\
                            .then_inc(hi_ok, 1)
                nc.scalar.activation(w2t[:], ps_a[:], ACT.Copy).then_inc(w2_ok, 1)
                act.wait_ge(lmax_ok, 1)
                nc.scalar.activation(ex[:], lg[:], ACT.Exp).then_inc(ex_ok, 1)

                def layer1(c):
                    for m in range(d.KT):
                        act.wait_ge(h_ps, d.KT * c + m + 1)
                        if c >= 2:
                            act.wait_ge(hl_ok, d.KT * (c - 1))
                            act.wait_ge(h2_ps, HALVES * (c - 1))
                        nc.scalar.activation(h1[:, c % 2, m, :], ps_th[c % 2][:, m, :], ACT.Silu).then_inc(h1_ok, 1)
                        act.wait_ge(h1_ok, d.KT * c + m + 1)
                        nc.scalar.activation(h_hi[:, c % 2, m, :], h1[:, c % 2, m, :], ACT.Copy).then_inc(hh_ok, 1)

                def layer2(c):
                    for j in range(HALVES):
                        act.wait_ge(h2_ps, HALVES * c + j + 1)
                        t = TPC * c + 2 * j
                        nc.scalar.activation(h2[:, t:t + 2, :].rearrange("p t e -> p (t e)"), ps_2[:, j, :], ACT.Silu)\
                            .then_inc(h2_ok, 1)

                layer1(0)
                for c in range(d.NC):
                    if c + 1 < d.NC:
                        layer1(c + 1)
                    layer2(c)

            @block.tensor
            def _(pe):
                for i in range(3):
                    pe.wait_ge(w_in[i], 16)
                    dst = ps_a[:] if i == 2 else ps_2[:, i, :]
                    for k in range(d.KT):
                        for a in range(d.KT):
                            ins = nc.tensor.transpose(dst[:, k * d.E + a * P:k * d.E + (a + 1) * P],
                                                      raw[:, i, a, k * P:(k + 1) * P], ident[:])
                    ins.then_inc(wt_ps, 1)
                pe.wait_ge(w_in[3], 16)
                flat_l = ps_l[:].rearrange("p t e -> p (t e)")
                for k in range(d.KT):
                    ins = nc.tensor.transpose(flat_l[:, k * NE:(k + 1) * NE], wr_raw[:, k * P:(k + 1) * P],
                                              ident[0:NE, 0:NE])
                ins.then_inc(wt_ps, 1)

                def turn(c):
                    pe.wait_ge(xn_ok, c + 1)
                    if c >= 2:
                        pe.wait_ge(lo_ok, d.KT * (c - 1))
                    for k in range(d.KT):
                        for j in range(TPC):
                            ins = nc.tensor.transpose(ps_th[c % 2][:, k, j * P:(j + 1) * P],
                                                      xn[:, c % 2, j, k * P:(k + 1) * P], ident[:])
                        ins.then_inc(t_ps, 1)

                def route(c):
                    pe.wait_ge(wt_l, 3)
                    pe.wait_ge(lo_ok, d.KT * (c + 1))
                    for j in range(TPC):
                        t = TPC * c + j
                        x = slice(t * P, (t + 1) * P)
                        for k in range(d.KT):
                            e = slice(k * NE, (k + 1) * NE)
                            ins = mm_split(nc, ps_l[:, t, :], xt_hi[:, k, x], xt_lo[:, k, x], wr_hi[:, e],
                                           wr_lo[:, e], k == 0, k == d.KT - 1)
                    ins.then_inc(l_ps, 1)

                def layer1(c):
                    x = slice(c * d.CH, (c + 1) * d.CH)
                    if c < 2:
                        pe.wait_ge(lo_ok, d.KT * (d.NC - 1 + c))
                    else:
                        pe.wait_ge(h1_ok, d.KT * (c - 1))
                    for m in range(d.KT):
                        for k in range(d.KT):
                            cols = slice(k * d.E + m * P, k * d.E + (m + 1) * P)
                            ins = mm_split(nc, ps_th[c % 2][:, m, :], wt_hi[:, 0, cols], wt_lo[:, 0, cols],
                                           xt_hi[:, k, x], xt_lo[:, k, x], k == 0, k == d.KT - 1)
                        ins.then_inc(h_ps, 1)

                def layer2(c):
                    pe.wait_ge(hl_ok, d.KT * (c + 1))
                    for j in range(HALVES):
                        if c:
                            pe.wait_ge(h2_ok, HALVES * (c - 1) + j + 1)
                        for i in range(2):
                            x = slice((2 * j + i) * P, (2 * j + i + 1) * P)
                            for k in range(d.KT):
                                wk = slice(k * d.E, (k + 1) * d.E)
                                ins = mm_split(nc, ps_2[:, j, i * d.E:(i + 1) * d.E], h_hi[:, c % 2, k, x],
                                               h_lo[:, c % 2, k, x], wt_hi[:, 1, wk], wt_lo[:, 1, wk], k == 0,
                                               k == d.KT - 1)
                        ins.then_inc(h2_ps, 1)

                def add_up(c):
                    pe.wait_ge(g_ok, 1)
                    pe.wait_ge(w2_ok, 1)
                    pe.wait_ge(h2_ok, HALVES * (c + 1))
                    for j in range(TPC):
                        t = TPC * c + j
                        ins = nc.tensor.matmul(ps_a[0:NE, 0:d.E], gate[:, t, :], h2[:, t, :], start=t == 0,
                                               stop=t == d.NT - 1)
                    if c == d.NC - 1:
                        ins.then_inc(a_ps, 1)

                for c in range(d.NC):
                    turn(c)
                    if c:
                        route(c - 1)
                route(d.NC - 1)
                layer1(0)
                for c in range(d.NC):
                    if c + 1 < d.NC:
                        layer1(c + 1)
                    layer2(c)
                    if c:
                        add_up(c - 1)
                add_up(d.NC - 1)
                pe.wait_ge(acc_ok, 1)
                pe.wait_ge(l_rd, 1)
                for k in range(d.KT):
                    ins = nc.tensor.transpose(flat_l[:, k * NE:(k + 1) * NE], acc[:, k * P:(k + 1) * P],
                                              ident[0:NE, 0:NE])
                ins.then_inc(a_ps, 1)
                pe.wait_ge(acc_ok, 2)
                for k in range(d.KT):
                    ins = nc.tensor.matmul(ps_a[0:NE, 0:d.E], acc_t[:, k, :], w2t[:, k * d.E:(k + 1) * d.E],
                                           start=k == 0, stop=k == d.KT - 1)
                ins.then_inc(a_ps, 1)


INS = ["L0_attn_x", "L0_attn_W_attn", "L0_attn_W_proj", "L0_attn_lambda_q1", "L0_attn_lambda_k1",
       "L0_attn_lambda_q2", "L0_attn_lambda_k2", "L0_ffn_W_syn", "L0_ffn_b_syn", "L0_ffn_W_out", "L0_ffn_b_out",
       "L0_ffn_gamma", "L0_ffn_beta", "L1_attn_Wq", "L1_attn_Wk", "L1_attn_Wv", "L1_attn_Wo", "L1_attn_bo",
       "L1_ffn_w1", "L1_ffn_w3", "L1_ffn_w2", "L1_ffn_wr"]


def two_layers(nc, io, out):
    d = Dims(io["L0_attn_x"], io["L0_ffn_W_syn"], io["L1_attn_Wq"])
    with ExitStack() as ctx:
        keep = {
            "X": ctx.enter_context(nc.sbuf_tensor("residual", [P, d.NT, d.E], F32)),
            "ident": ctx.enter_context(nc.sbuf_tensor("ident", [P, P], F32)),
        }
        with ExitStack() as att:
            scratch = {
                "qk": nc.dram_tensor("qk_parts", [2, d.B, 2 * d.E, d.S], F32).ap(),
                "v": nc.dram_tensor("v_rows", [d.B, d.H // d.G, P, d.S // P, d.G * 32], F32).ap(),
                "zero": nc.dram_tensor("zero_rows", [2, d.G * d.S], F32).ap(),
                "qk_out": [att.enter_context(nc.semaphore(f"qk_out{i}")) for i in range(2)],
                "v_out": [att.enter_context(nc.semaphore(f"v_out{i}")) for i in range(2)],
            }
            keep["AO"] = att.enter_context(nc.sbuf_tensor("att_out", [P, d.NT, d.E], F32))
            keep["tern"] = att.enter_context(nc.sbuf_tensor("ternary", [P, 2, d.KT * d.N], mybir.dt.bfloat16))
            keep["sc"] = att.enter_context(nc.sbuf_tensor("weight_scales", [P, 2], F32))
            with ExitStack() as stacks:
                for name in ("qst", "kst"):
                    keep[name] = [stacks.enter_context(nc.sbuf_tensor(f"{name}{i}", [P, d.G, d.S], F32R))
                                  for i in range(3)]
                stage_qkv(nc, d, io, keep, scratch)
                stage_attention(nc, d, io, keep, scratch)
            stage_mlp(nc, d, io, keep)
        with ExitStack() as lin:
            def sb(name, shape, dt=F32):
                return lin.enter_context(nc.sbuf_tensor("lin_" + name, shape, dt))
            keep["xt_hi"] = sb("xt_hi", [P, d.KT, d.TOK], F32R)
            keep["xt_lo"] = sb("xt_lo", [P, d.KT, d.TOK], F32R)
            keep["M"] = sb("m", [P, d.B, d.NCH, d.E])
            keep["ksum"] = sb("ksum", [P, d.B, d.INNER])
            keep["wq_raw"] = sb("wq_raw", [P, d.INNER // d.CH, d.KT * d.CH])
            stage_keys(nc, d, io, keep)
            stage_queries(nc, d, io, keep)
        stage_routed(nc, d, io, keep, out)


def kernel(**inputs):
    import numpy as np
    import concourse.bacc as bacc
    from concourse.bass_utils import run_bass_kernel_spmd

    nc = bacc.Bacc("TRN2", target_bir_lowering=False, num_devices=1)
    arrays, io = {}, {}
    for name in INS:
        a = np.ascontiguousarray(inputs[name])
        arrays[name] = a
        io[name] = nc.dram_tensor(name, a.shape, mybir.dt.from_np(a.dtype), kind="ExternalInput").ap()
    shape = arrays["L0_attn_x"].shape
    out = nc.dram_tensor("out", shape, F32, kind="ExternalOutput").ap()
    two_layers(nc, io, out)
    r = run_bass_kernel_spmd(nc, [arrays], core_ids=[0])
    return r.results[0]["out"]
```
